# Optimizing a Trainium2 kernel written in Bass

```python
import numpy as np
import jax
import jax.numpy as jnp

def _softmax(x, axis=-1):
    return jax.nn.softmax(x, axis=axis)

def _gelu(x):
    return jax.nn.gelu(x, approximate=True)

def _silu(x):
    return jax.nn.silu(x)

def _sigmoid(x):
    return jax.nn.sigmoid(x)

def _layernorm(x, axis=-1, eps=1e-05):
    m = jnp.mean(x, axis=axis, keepdims=True)
    v = jnp.var(x, axis=axis, keepdims=True)
    return (x - m) / jnp.sqrt(v + eps)

def _scatter_add(tgt, idx, src, axis=0):
    return tgt.at[idx].add(src)

def _segment_sum(src, seg, n):
    return jax.ops.segment_sum(src, seg, n)
kernel_name = 'mk_macaron_d2_jaxref_r8_ccd573'

def setup_inputs(seed: int=0):
    np.random.seed(seed)
    _w = jnp.asarray

    def _L0_attn_setup():
        import jax, jax.numpy as jnp
        import numpy as np
        import math
        D_MODEL = 128
        N_HEADS = 16
        LATENT = 32
        key = jax.random.key(seed)
        ks = jax.random.split(key, 9)
        B, T, C, L = (2, 256, D_MODEL, LATENT)
        s = 0.02
        return {'x': jax.random.normal(ks[0], (B, T, C), dtype=jnp.float32), 'Wq': jax.random.normal(ks[1], (C, C), dtype=jnp.float32) * s, 'bq': jnp.zeros((C,), dtype=jnp.float32), 'Wkd': jax.random.normal(ks[2], (C, 2 * L), dtype=jnp.float32) * s, 'bkd': jnp.zeros((2 * L,), dtype=jnp.float32), 'Wku': jax.random.normal(ks[3], (L, 2 * C), dtype=jnp.float32) * s, 'bku': jnp.zeros((2 * C,), dtype=jnp.float32), 'Wo': jax.random.normal(ks[4], (C, C), dtype=jnp.float32) * s, 'bo': jnp.zeros((C,), dtype=jnp.float32)}
    _L0_attn_in = _L0_attn_setup()

    def _L0_ffn_setup():
        import jax, jax.numpy as jnp
        import numpy as np
        DIM = 128
        HIDDEN = 384
        SCALE = 1.0 / 127.0

        def _dequant(w_int, dtype):
            return w_int.astype(dtype) * jnp.asarray(SCALE, dtype)
        key = jax.random.key(seed)
        k_x, k_g, k_u, k_d = jax.random.split(key, 4)
        x = jax.random.normal(k_x, (4, 256, DIM), dtype=jnp.float32)
        w_gate = jax.random.randint(k_g, (HIDDEN, DIM), -127, 128, dtype=jnp.int32)
        w_up = jax.random.randint(k_u, (HIDDEN, DIM), -127, 128, dtype=jnp.int32)
        w_down = jax.random.randint(k_d, (DIM, HIDDEN), -127, 128, dtype=jnp.int32)
        return {'x': x, 'w_gate': w_gate, 'w_up': w_up, 'w_down': w_down}
    _L0_ffn_in = _L0_ffn_setup()

    def _L1_attn_setup():
        import jax, jax.numpy as jnp
        import numpy as np
        HEADS = 16
        KERNEL_SIZE = 4
        STRIDE = 2
        DIM = 128
        key = jax.random.key(seed)
        k1, k2, k3, k4 = jax.random.split(key, 4)
        B, L, C = (4, 512, DIM)
        x = jax.random.normal(k1, (B, L, C), dtype=jnp.float32)
        w_qkv = jax.random.normal(k2, (C, 3 * C), dtype=jnp.float32) * C ** (-0.5)
        w_out = jax.random.normal(k3, (C, C), dtype=jnp.float32) * C ** (-0.5)
        b_out = jax.random.normal(k4, (C,), dtype=jnp.float32) * 0.01
        return {'x': x, 'w_qkv': w_qkv, 'w_out': w_out, 'b_out': b_out}
    _L1_attn_in = _L1_attn_setup()

    def _L1_ffn_setup():
        import jax, jax.numpy as jnp
        import numpy as np
        D_MODEL = 128
        D1, D2 = (32, 32)
        F1, F2 = (64, 64)
        E = 64
        TOP_K = 2

        def kmoe(x_flat, W_router, A, B, scale, bias, d_in1, d_in2, d_out1, d_out2, top_k):
            logits = x_flat @ W_router.T
            vals, idx = jax.lax.top_k(logits, top_k)
            probs = jax.nn.softmax(vals, axis=-1)
            xs = x_flat.reshape(-1, d_in1, d_in2)
            Ag = A[idx]
            Bg = B[idx]
            Y = jnp.einsum('nkoi,nij,nkpj->nkop', Ag, xs, Bg)
            out = jnp.einsum('nkop,nk->nop', Y, probs).reshape(-1, d_out1 * d_out2)
            return out * scale + bias
        key = jax.random.key(seed)
        ks = jax.random.split(key, 12)
        s = 0.02
        return {'x': jax.random.normal(ks[0], (4, 256, D_MODEL), dtype=jnp.float32), 'W_up': jax.random.normal(ks[1], (E, D1 * D2), dtype=jnp.float32) * s, 'A_up': jax.random.normal(ks[2], (E, F1, D1), dtype=jnp.float32) * s, 'B_up': jax.random.normal(ks[3], (E, F2, D2), dtype=jnp.float32) * s, 'scale_up': jnp.ones((1,), dtype=jnp.float32), 'bias_up': jnp.zeros((F1 * F2,), dtype=jnp.float32), 'W_down': jax.random.normal(ks[4], (E, F1 * F2), dtype=jnp.float32) * s, 'A_down': jax.random.normal(ks[5], (E, D1, F1), dtype=jnp.float32) * s, 'B_down': jax.random.normal(ks[6], (E, D2, F2), dtype=jnp.float32) * s, 'scale_down': jnp.ones((1,), dtype=jnp.float32), 'bias_down': jnp.zeros((D1 * D2,), dtype=jnp.float32)}
    _L1_ffn_in = _L1_ffn_setup()
    _d = {'L0_attn_x': _L0_attn_in['x'], 'L0_attn_Wq': _L0_attn_in['Wq'], 'L0_attn_bq': _L0_attn_in['bq'], 'L0_attn_Wkd': _L0_attn_in['Wkd'], 'L0_attn_bkd': _L0_attn_in['bkd'], 'L0_attn_Wku': _L0_attn_in['Wku'], 'L0_attn_bku': _L0_attn_in['bku'], 'L0_attn_Wo': _L0_attn_in['Wo'], 'L0_attn_bo': _L0_attn_in['bo'], 'L0_ffn_w_gate': _L0_ffn_in['w_gate'], 'L0_ffn_w_up': _L0_ffn_in['w_up'], 'L0_ffn_w_down': _L0_ffn_in['w_down'], 'L1_attn_w_qkv': _L1_attn_in['w_qkv'], 'L1_attn_w_out': _L1_attn_in['w_out'], 'L1_attn_b_out': _L1_attn_in['b_out'], 'L1_ffn_W_up': _L1_ffn_in['W_up'], 'L1_ffn_A_up': _L1_ffn_in['A_up'], 'L1_ffn_B_up': _L1_ffn_in['B_up'], 'L1_ffn_scale_up': _L1_ffn_in['scale_up'], 'L1_ffn_bias_up': _L1_ffn_in['bias_up'], 'L1_ffn_W_down': _L1_ffn_in['W_down'], 'L1_ffn_A_down': _L1_ffn_in['A_down'], 'L1_ffn_B_down': _L1_ffn_in['B_down'], 'L1_ffn_scale_down': _L1_ffn_in['scale_down'], 'L1_ffn_bias_down': _L1_ffn_in['bias_down']}
    _x0 = _d['L0_attn_x']
    _d['L0_attn_x'] = jax.random.normal(jax.random.fold_in(jax.random.key(seed), 1), (16, 512, 128), dtype=_x0.dtype)
    del _x0
    return _d

def reference(L0_attn_x, L0_attn_Wq, L0_attn_bq, L0_attn_Wkd, L0_attn_bkd, L0_attn_Wku, L0_attn_bku, L0_attn_Wo, L0_attn_bo, L0_ffn_w_gate, L0_ffn_w_up, L0_ffn_w_down, L1_attn_w_qkv, L1_attn_w_out, L1_attn_b_out, L1_ffn_W_up, L1_ffn_A_up, L1_ffn_B_up, L1_ffn_scale_up, L1_ffn_bias_up, L1_ffn_W_down, L1_ffn_A_down, L1_ffn_B_down, L1_ffn_scale_down, L1_ffn_bias_down):

    def _L0_attn_ref(x, Wq, bq, Wkd, bkd, Wku, bku, Wo, bo):
        import jax, jax.numpy as jnp
        import numpy as np
        import math
        D_MODEL = 128
        N_HEADS = 16
        LATENT = 32
        B, T, C = x.shape
        H = N_HEADS
        D = C // H
        L = LATENT
        q = (x @ Wq + bq).reshape(B, T, H, D)
        kv_latent = jax.nn.gelu(x @ Wkd + bkd, approximate=False)
        lat = kv_latent[..., :L] + kv_latent[..., L:]
        kv = lat @ Wku + bku
        k = kv[..., :C].reshape(B, T, H, D)
        v = kv[..., C:].reshape(B, T, H, D)
        scale = 1.0 / math.sqrt(D)
        attn = jnp.einsum('bqhd,bkhd->bhqk', q, k) * scale
        causal = jnp.tril(jnp.ones((T, T), dtype=bool))
        attn = jnp.where(causal, attn, -jnp.inf)
        attn = jax.nn.softmax(attn, axis=-1)
        out = jnp.einsum('bhqk,bkhd->bqhd', attn, v).reshape(B, T, C)
        return out @ Wo + bo

    def _L0_ffn_ref(x, w_gate, w_up, w_down):
        import jax, jax.numpy as jnp
        import numpy as np
        DIM = 128
        HIDDEN = 384
        SCALE = 1.0 / 127.0

        def _dequant(w_int, dtype):
            return w_int.astype(dtype) * jnp.asarray(SCALE, dtype)
        wg = _dequant(w_gate, x.dtype)
        wu = _dequant(w_up, x.dtype)
        wd = _dequant(w_down, x.dtype)
        gate = jnp.einsum('bsd,hd->bsh', x, wg)
        up = jnp.einsum('bsd,hd->bsh', x, wu)
        h = jax.nn.silu(gate) * up
        return jnp.einsum('bsh,dh->bsd', h, wd)

    def _L1_attn_ref(x, w_qkv, w_out, b_out):
        import jax, jax.numpy as jnp
        import numpy as np
        HEADS = 16
        KERNEL_SIZE = 4
        STRIDE = 2
        DIM = 128
        B, L, C = x.shape
        ks, stride, heads = (KERNEL_SIZE, STRIDE, HEADS)
        hd = C // heads
        scale = C ** (-0.5)
        W = (L - ks) // stride + 1
        idx = jnp.arange(W)[:, None] * stride + jnp.arange(ks)[None, :]
        xw = x[:, idx]
        qkv = xw @ w_qkv
        q, k, v = jnp.split(qkv, 3, axis=-1)
        q = q.reshape(B, W, ks, heads, hd)
        k = k.reshape(B, W, ks, heads, hd)
        v = v.reshape(B, W, ks, heads, hd)
        dots = jnp.einsum('bwqhd,bwkhd->bwhqk', q, k) * scale
        attn = jax.nn.softmax(dots, axis=-1)
        o = jnp.einsum('bwhqk,bwkhd->bwqhd', attn, v).reshape(B, W, ks, C)
        o = o @ w_out + b_out
        out = jnp.zeros_like(x).at[:, idx.reshape(-1)].add(o.reshape(B, W * ks, C))
        return out

    def _L1_ffn_ref(x, W_up, A_up, B_up, scale_up, bias_up, W_down, A_down, B_down, scale_down, bias_down):
        import jax, jax.numpy as jnp
        import numpy as np
        D_MODEL = 128
        D1, D2 = (32, 32)
        F1, F2 = (64, 64)
        E = 64
        TOP_K = 2

        def kmoe(x_flat, W_router, A, B, scale, bias, d_in1, d_in2, d_out1, d_out2, top_k):
            logits = x_flat @ W_router.T
            vals, idx = jax.lax.top_k(logits, top_k)
            probs = jax.nn.softmax(vals, axis=-1)
            xs = x_flat.reshape(-1, d_in1, d_in2)
            Ag = A[idx]
            Bg = B[idx]
            Y = jnp.einsum('nkoi,nij,nkpj->nkop', Ag, xs, Bg)
            out = jnp.einsum('nkop,nk->nop', Y, probs).reshape(-1, d_out1 * d_out2)
            return out * scale + bias
        orig_shape = x.shape
        x_flat = x.reshape(-1, D1 * D2)
        h = kmoe(x_flat, W_up, A_up, B_up, scale_up, bias_up, D1, D2, F1, F2, TOP_K)
        h = jax.nn.gelu(h, approximate=False)
        y = kmoe(h, W_down, A_down, B_down, scale_down, bias_down, F1, F2, D1, D2, TOP_K)
        return y.reshape(*orig_shape[:-1], D_MODEL)
    x = L0_attn_x
    x = x + 0.5 * _L0_ffn_ref(_layernorm(x, axis=-1), L0_ffn_w_gate, L0_ffn_w_up, L0_ffn_w_down)
    x = x + _L0_attn_ref(_layernorm(x, axis=-1), L0_attn_Wq, L0_attn_bq, L0_attn_Wkd, L0_attn_bkd, L0_attn_Wku, L0_attn_bku, L0_attn_Wo, L0_attn_bo)
    x = x + 0.5 * _L0_ffn_ref(_layernorm(x, axis=-1), L0_ffn_w_gate, L0_ffn_w_up, L0_ffn_w_down)
    x = x + 0.5 * _L1_ffn_ref(_layernorm(x, axis=-1), L1_ffn_W_up, L1_ffn_A_up, L1_ffn_B_up, L1_ffn_scale_up, L1_ffn_bias_up, L1_ffn_W_down, L1_ffn_A_down, L1_ffn_B_down, L1_ffn_scale_down, L1_ffn_bias_down)
    x = x + _L1_attn_ref(_layernorm(x, axis=-1), L1_attn_w_qkv, L1_attn_w_out, L1_attn_b_out)
    x = x + 0.5 * _L1_ffn_ref(_layernorm(x, axis=-1), L1_ffn_W_up, L1_ffn_A_up, L1_ffn_B_up, L1_ffn_scale_up, L1_ffn_bias_up, L1_ffn_W_down, L1_ffn_A_down, L1_ffn_B_down, L1_ffn_scale_down, L1_ffn_bias_down)
    return x

_drawn_inputs = setup_inputs


def setup_inputs(seed=0):
    import zlib

    import numpy as np

    out = dict(_drawn_inputs(seed))
    spreads = {'L0_attn_bq': (0.0, 2.0),
     'L0_attn_bkd': (0.0, 2.0),
     'L0_attn_bku': (0.0, 2.0),
     'L0_attn_bo': (0.0, 2.0),
     'L1_ffn_bias_up': (0.0, 2.0),
     'L1_ffn_bias_down': (0.0, 2.0)}
    factors = {'L0_attn_Wq': 26.382,
     'L0_attn_Wkd': 32.341,
     'L0_attn_Wku': 8.0,
     'L0_attn_Wo': 8.0,
     'L1_attn_w_qkv': 8.0,
     'L1_attn_w_out': 8.0,
     'L1_attn_b_out': 64.0,
     'L1_ffn_W_up': 64.0,
     'L1_ffn_A_up': 64.0,
     'L1_ffn_B_up': 64.0,
     'L1_ffn_W_down': 64.0,
     'L1_ffn_A_down': 64.0,
     'L1_ffn_B_down': 64.0}
    for name, (base, spread) in spreads.items():
        noise = np.random.default_rng([zlib.crc32(name.encode()), seed]).standard_normal(out[name].shape)
        drawn = base * np.exp(spread * noise) if base else spread * noise
        out[name] = jnp.asarray(drawn.astype(out[name].dtype))
    for name, factor in factors.items():
        out[name] = (out[name] * factor).astype(out[name].dtype)
    return out
```

```python
from contextlib import ExitStack

import numpy as np
import concourse.bass as bass
from concourse import mybir

F32 = mybir.dt.float32
BF16 = mybir.dt.bfloat16
I32 = mybir.dt.int32
U32 = mybir.dt.uint32
ALU = mybir.AluOpType
ACT = mybir.ActivationFunctionType
AX = mybir.AxisListType

P = 128
D = 128
RUN = 64
TOK = P * RUN
CH = 4
NCH = RUN // CH
HID = 384
HB = HID // P
EPS = 1e-5
BATCH, SEQ, HEADS, HD = 16, 512, 16, 8
LAT = 32


class Stage:
    used = []

    def __init__(self, nc, name):
        self.nc, self.name, self.stack, self.sems = nc, name, ExitStack(), []

    def __enter__(self):
        return self

    def __exit__(self, *e):
        Stage.used = self.sems
        return self.stack.__exit__(*e)

    def sb(self, name, shape, dt=F32):
        return self.stack.enter_context(self.nc.sbuf_tensor(f"{self.name}_{name}", shape, dt))

    def ps(self, name, shape, dt=F32):
        return self.stack.enter_context(self.nc.psum_tensor(f"{self.name}_{name}", shape, dt))

    def sem(self, name):
        self.sems.append(self.nc.alloc_semaphore(f"{self.name}_{name}"))
        return self.sems[-1]

    def block(self):
        if Stage.used:
            self.nc.clear_and_free_semaphores(Stage.used)
        return self.stack.enter_context(self.nc.Block())


def chained(eng, sem):
    n = [0]

    def link(ins):
        n[0] += 1
        ins.then_inc(sem, 1)
        eng.wait_ge(sem, n[0])
    return link


def pass_waits(eng, sem):
    eng.sem_inc(sem, 1)


def setup(nc, keep, a):
    with Stage(nc, "setup") as st:
        raw = {n: st.sb(f"raw_{n}", [P, HB * D], I32) for n in ("gate", "up", "down")}
        deq = {n: st.sb(f"deq_{n}", [P, HB, D]) for n in ("gate", "up", "down")}
        turned_ps = [st.ps(f"turned{n}", [P, HB, P]) for n in range(3)]
        loaded_x, loaded_w, zeroed, made = (st.sem(n) for n in ("loaded_x", "loaded_w", "zeroed", "made"))
        dequantized, turned, kept = (st.sem(n) for n in ("dequantized", "turned", "kept"))
        block = st.block()

        @block.sync
        def _(sp):
            sp.dma_start(keep["x"][:, :, :], a["L0_attn_x"].rearrange("b (g r) d -> (b g) r d", r=RUN))\
              .then_inc(loaded_x, 16)
            sp.wait_ge(loaded_x, 16)

        @block.scalar
        def _(act):
            act.dma_start(raw["gate"][:, :].rearrange("p (h d) -> p h d", h=HB),
                          a["L0_ffn_w_gate"].rearrange("(h p) d -> p h d", p=P)).then_inc(loaded_w, 16)
            act.dma_start(raw["up"][:, :].rearrange("p (h d) -> p h d", h=HB),
                          a["L0_ffn_w_up"].rearrange("(h p) d -> p h d", p=P)).then_inc(loaded_w, 16)
            act.dma_start(raw["down"][:, :], a["L0_ffn_w_down"]).then_inc(loaded_w, 16)
            for n, w in enumerate(("gateT", "upT", "downT")):
                act.wait_ge(turned, n + 1)
                nc.scalar.copy(keep[w][:, :, :], turned_ps[n][:, :, :]).then_inc(kept, 1)
            act.wait_ge(kept, 3)

        @block.gpsimd
        def _(pool):
            nc.gpsimd.memset(keep["ident"][:, :], 0.0).then_inc(zeroed, 1)
            nc.gpsimd.memset(keep["half_neg"][:, :], -0.5).then_inc(zeroed, 1)
            pool.wait_ge(zeroed, 2)
            nc.gpsimd.affine_select(out=keep["ident"][:, :], in_=keep["ident"][:, :],
                                    compare_op=ALU.not_equal, fill=1.0, base=0, pattern=[[-1, P]],
                                    channel_multiplier=1).then_inc(made, 1)

        @block.vector
        def _(dve):
            dve.wait_ge(loaded_w, 48)
            for n in ("gate", "up", "down"):
                nc.vector.tensor_scalar(deq[n][:, :, :].rearrange("p h d -> p (h d)"), raw[n][:, :],
                                        1.0 / 127.0, None, ALU.mult).then_inc(dequantized, 1)
            dve.wait_ge(made, 1)
            nc.vector.tensor_copy(keep["identb"][:, :], keep["ident"][:, :]).then_inc(made, 1)
            dve.wait_ge(made, 2)

        @block.tensor
        def _(pe):
            pe.wait_ge(made, 1)
            for n, w in enumerate(("gate", "up", "down")):
                pe.wait_ge(dequantized, n + 1)
                for h in range(HB):
                    mm = nc.tensor.transpose(turned_ps[n][:, h, :], deq[w][:, h, :], keep["ident"][:, :])
                mm.then_inc(turned, 1)


def layer_norm_stats(nc, keep, name):
    x, mean, rstd = keep["x"], keep["mean"], keep["rstd"]
    with Stage(nc, name) as st:
        stats = st.sb("stats", [P, RUN, 6])
        diff, var = st.sb("diff", [P, RUN]), st.sb("var", [P, RUN])
        summed, link_sem, var_ready, rstd_ready = (st.sem(n) for n in ("summed", "link", "var_ready", "rstd_ready"))
        block = st.block()

        @block.vector
        def _(dve):
            with dve.Fori(0, NCH) as c:
                for t in range(CH):
                    ins = nc.vector.bn_stats(stats[:, bass.ds(c * CH + t, 1), :].rearrange("p a b -> p (a b)"),
                                             x[:, bass.ds(c * CH + t, 1), :].rearrange("p a b -> p (a b)"))
                ins.then_inc(summed, 1)
            dve.wait_ge(summed, NCH)
            link = chained(dve, link_sem)
            even, odd = stats[:, :, 1], stats[:, :, 4]
            link(nc.vector.tensor_tensor(mean[:, :], even, odd, ALU.add))
            link(nc.vector.tensor_tensor(diff[:, :], even, odd, ALU.subtract))
            link(nc.vector.tensor_tensor(var[:, :], stats[:, :, 2], stats[:, :, 5], ALU.add))
            link(nc.vector.tensor_scalar(mean[:, :], mean[:, :], 0.5, None, ALU.mult))
            link(nc.vector.tensor_scalar(diff[:, :], diff[:, :], 0.5, None, ALU.mult))
            link(nc.vector.tensor_tensor(diff[:, :], diff[:, :], diff[:, :], ALU.mult))
            link(nc.vector.tensor_scalar(var[:, :], var[:, :], 1.0 / D, EPS, ALU.mult, ALU.add))
            nc.vector.tensor_tensor(var[:, :], var[:, :], diff[:, :], ALU.add).then_inc(var_ready, 1)

        @block.gpsimd
        def _(pool):
            pool.wait_ge(var_ready, 1)
            nc.gpsimd.tensor_tensor(rstd[:, :], var[:, :], keep["half_neg"][:, :], ALU.pow).then_inc(rstd_ready, 1)
            pool.wait_ge(rstd_ready, 1)


def normalize(nc, keep, out, r):
    return nc.vector.tensor_scalar(out, keep["x"][:, bass.ds(r, 1), :].rearrange("p a b -> p (a b)"),
                                   keep["mean"][:, bass.ds(r, 1)], keep["rstd"][:, bass.ds(r, 1)],
                                   ALU.subtract, ALU.mult)


def ffn(nc, keep, name):
    x, ident = keep["x"], keep["ident"]
    with Stage(nc, name) as st:
        xn = [st.sb(f"xn{k}", [P, CH, D]) for k in range(2)]
        xnT = [st.sb(f"xnT{k}", [P, CH * P]) for k in range(2)]
        silu = [st.sb(f"silu{k}", [P, CH * P]) for k in range(HB)]
        hT = [st.sb(f"hT{k}", [P, HB, CH * P]) for k in range(2)]
        turn_ps, down_ps = st.ps("turn", [P, CH, P]), st.ps("downp", [P, CH, D])
        gate_ps = [st.ps(f"gate{k}", [P, CH * P]) for k in range(HB)]
        up_ps = [st.ps(f"up{k}", [P, CH * P]) for k in range(HB)]
        xn_ready, turned, xnT_ready, gated = (st.sem(n) for n in ("xn_ready", "turned", "xnT_ready", "gated"))
        silu_ready, h_ready, down_ready, added = (st.sem(n) for n in ("silu_ready", "h_ready", "down_ready", "added"))
        block = st.block()

        @block.vector
        def _(dve):
            def norm(c, k, ring=True):
                if ring:
                    dve.wait_ge(turned, c - 1)
                for t in range(CH):
                    ins = normalize(nc, keep, xn[k][:, t, :], c * CH + t)
                ins.then_inc(xn_ready, 1)

            def hidden(c, k, ring=True):
                if ring:
                    dve.wait_ge(down_ready, c - 1)
                for h in range(HB):
                    dve.wait_ge(silu_ready, c * HB + h + 1)
                    nc.vector.tensor_tensor(hT[k][:, h, :], silu[h][:, :], up_ps[h][:, :], ALU.mult)\
                      .then_inc(h_ready, 1)

            def add(c):
                dve.wait_ge(down_ready, c + 1)
                xs = x[:, bass.ds(c * CH, CH), :]
                nc.vector.scalar_tensor_tensor(out=xs, in0=down_ps[:, :, :], scalar=0.5, in1=xs,
                                               op0=ALU.mult, op1=ALU.add).then_inc(added, 1)

            norm(0, 0, False)
            norm(1, 1, False)
            hidden(0, 0, False)
            norm(2, 0)
            hidden(1, 1, False)
            add(0)
            with dve.Fori(1, NCH // 2 - 1) as j:
                norm(2 * j + 1, 1)
                hidden(2 * j, 0)
                add(2 * j - 1)
                norm(2 * j + 2, 0)
                hidden(2 * j + 1, 1)
                add(2 * j)
            norm(NCH - 1, 1)
            hidden(NCH - 2, 0)
            add(NCH - 3)
            hidden(NCH - 1, 1)
            add(NCH - 2)
            add(NCH - 1)
            dve.wait_ge(added, NCH)

        @block.tensor
        def _(pe):
            def turn(c, k, ring=True):
                pe.wait_ge(xn_ready, c + 1)
                if ring:
                    pe.wait_ge(xnT_ready, c)
                for t in range(CH):
                    mm = nc.tensor.transpose(turn_ps[:, t, :], xn[k][:, t, :], ident[:, :])
                mm.then_inc(turned, 1)

            def gate_up(c, k, ring=True):
                pe.wait_ge(xnT_ready, c + 1)
                for h in range(HB):
                    if ring:
                        pe.wait_ge(h_ready, (c - 1) * HB + h + 1)
                    nc.tensor.matmul(gate_ps[h][:, :], keep["gateT"][:, h, :], xnT[k][:, :], start=True, stop=True)
                    nc.tensor.matmul(up_ps[h][:, :], keep["upT"][:, h, :], xnT[k][:, :], start=True, stop=True)\
                      .then_inc(gated, 1)

            def down(c, k, ring=True):
                pe.wait_ge(h_ready, (c + 1) * HB)
                if ring:
                    pe.wait_ge(added, c)
                for t in range(CH):
                    for h in range(HB):
                        mm = nc.tensor.matmul(down_ps[:, t, :], hT[k][:, h, t * P:(t + 1) * P],
                                              keep["downT"][:, h, :], start=(h == 0), stop=(h == HB - 1))
                mm.then_inc(down_ready, 1)

            turn(0, 0, False)
            turn(1, 1)
            gate_up(0, 0, False)
            turn(2, 0)
            gate_up(1, 1)
            down(0, 0, False)
            with pe.Fori(1, NCH // 2 - 1) as j:
                turn(2 * j + 1, 1)
                gate_up(2 * j, 0)
                down(2 * j - 1, 1)
                turn(2 * j + 2, 0)
                gate_up(2 * j + 1, 1)
                down(2 * j, 0)
            turn(NCH - 1, 1)
            gate_up(NCH - 2, 0)
            down(NCH - 3, 1)
            gate_up(NCH - 1, 1)
            down(NCH - 2, 0)
            down(NCH - 1, 1)

        @block.scalar
        def _(act):
            def copy_turned(c, k, ring=True):
                act.wait_ge(turned, c + 1)
                if ring:
                    act.wait_ge(gated, (c - 1) * HB)
                nc.scalar.copy(xnT[k][:, :], turn_ps[:, :, :].rearrange("p a b -> p (a b)")).then_inc(xnT_ready, 1)

            def gates(c, ring=True):
                for h in range(HB):
                    act.wait_ge(gated, c * HB + h + 1)
                    if ring:
                        act.wait_ge(h_ready, (c - 1) * HB + h + 1)
                    nc.scalar.activation(silu[h][:, :], gate_ps[h][:, :], ACT.Silu).then_inc(silu_ready, 1)

            copy_turned(0, 0, False)
            copy_turned(1, 1, False)
            gates(0, False)
            copy_turned(2, 0)
            gates(1)
            with act.Fori(1, NCH // 2 - 1) as j:
                copy_turned(2 * j + 1, 1)
                gates(2 * j)
                copy_turned(2 * j + 2, 0)
                gates(2 * j + 1)
            copy_turned(NCH - 1, 1)
            gates(NCH - 2)
            gates(NCH - 1)


NEG = -1e30
NPAIR = HEADS // 2
SLOTS = 6
Q_PART = (0, 0, 1, 1, 0, 2)
K_PART = (0, 1, 0, 1, 2, 0)
ROWS = 16 * SLOTS
NG = 4
NSTEP = BATCH * NG
NKB = SEQ // P


def mla_project(nc, keep, a, st0, name):
    x, ident = keep["x"], keep["ident"]
    xnT, q_dram, k_dram, v_dram = st0
    with Stage(nc, name + "t") as st:
        xn = [st.sb(f"xn{k}", [P, CH, D]) for k in range(2)]
        turn_ps = [st.ps(f"turn{k}", [P, CH, P]) for k in range(2)]
        xn_ready, turned, copied = (st.sem(n) for n in ("xn_ready", "turned", "copied"))
        xnT_runs = xnT[:, :].rearrange("d (p r) -> d p r", r=RUN)
        block = st.block()

        @block.vector
        def _(dve):
            def norm(c, k, ring=True):
                if ring:
                    dve.wait_ge(turned, c - 1)
                for t in range(CH):
                    ins = normalize(nc, keep, xn[k][:, t, :], c * CH + t)
                ins.then_inc(xn_ready, 1)
            norm(0, 0, False)
            norm(1, 1, False)
            with dve.Fori(1, NCH // 2) as j:
                norm(2 * j, 0)
                norm(2 * j + 1, 1)

        @block.tensor
        def _(pe):
            def turn(c, k, ring=True):
                pe.wait_ge(xn_ready, c + 1)
                if ring:
                    pe.wait_ge(copied, c - 1)
                for t in range(CH):
                    mm = nc.tensor.transpose(turn_ps[k][:, t, :], xn[k][:, t, :], ident[:, :])
                mm.then_inc(turned, 1)
            turn(0, 0, False)
            turn(1, 1, False)
            with pe.Fori(1, NCH // 2) as j:
                turn(2 * j, 0)
                turn(2 * j + 1, 1)

        @block.scalar
        def _(act):
            with act.Fori(0, NCH // 2) as j:
                for k in range(2):
                    c = 2 * j + k
                    act.wait_ge(turned, c + 1)
                    nc.scalar.copy(xnT_runs[:, :, bass.ds(c * CH, CH)].rearrange("d p t -> d t p"),
                                   turn_ps[k][:, :, :]).then_inc(copied, 1)
            act.wait_ge(copied, NCH)

    with Stage(nc, name + "p") as st:
        wq, wkd, wku = st.sb("wq", [P, D]), st.sb("wkd", [P, 2 * LAT]), st.sb("wku", [P, 2 * D])
        bq, bkd = st.sb("bq", [P, 1]), st.sb("bkd", [LAT, 2])
        act_half = [st.sb(f"act_half{h}", [LAT, SEQ]) for h in range(2)]
        lat = [st.sb(f"lat{k}", [P, SEQ]) for k in range(2)]
        whole = [[st.sb(f"{n}whole{k}", [P, SEQ]) for k in range(2)] for n in "qk"]
        rest1 = [[st.sb(f"{n}rest1{k}", [P, SEQ]) for k in range(2)] for n in "qk"]
        rest2 = [[st.sb(f"{n}rest2{k}", [P, SEQ]) for k in range(2)] for n in "qk"]
        part = [[st.sb(f"{n}part{k}", [P, 3, SEQ], BF16) for k in range(2)] for n in "qk"]
        v_sb = [st.sb(f"v{k}", [P, NKB, D]) for k in range(2)]
        lat_ps = [st.ps(f"latp{h}", [P, SEQ]) for h in range(2)]
        q_ps, k_ps, v_ps = (st.ps(n, [P, SEQ]) for n in ("qp", "kp", "vp"))
        wloaded, cleared, scaled = (st.sem(n) for n in ("wloaded", "cleared", "scaled"))
        lat_mm, gelu, lat_ready, q_mm, k_mm, v_mm = (st.sem(n) for n in ("lat_mm", "gelu", "lat_ready", "q_mm", "k_mm", "v_mm"))
        whole_ready, part1, left1, part2, left2, part3 = (st.sem(n) for n in ("whole_ready", "part1", "left1", "part2", "left2", "part3"))
        v_ready = st.sem("v_ready")
        parts_stored, v_stored = [st.sem(f"parts_stored{k}") for k in range(2)], [st.sem(f"v_stored{k}") for k in range(2)]
        block = st.block()
        NST = 2 * SLOTS * 16

        def batches(eng, one, n=BATCH // 2):
            one(0, 0, True)
            one(1, 1, True)
            with eng.Fori(1, n) as j:
                one(2 * j, 0, False)
                one(2 * j + 1, 1, False)

        @block.sync
        def _(sp):
            sp.wait_ge(cleared, 3)
            sp.dma_start(wq[:, :], a["L0_attn_Wq"]).then_inc(wloaded, 16)
            sp.dma_start(wkd[:, :], a["L0_attn_Wkd"]).then_inc(wloaded, 16)
            sp.dma_start(wku[0:LAT, :], a["L0_attn_Wku"]).then_inc(wloaded, 16)
            sp.dma_start(wku[LAT:LAT + 1, :], a["L0_attn_bku"].rearrange("(a n) -> a n", a=1)).then_inc(wloaded, 16)
            sp.dma_start(bq[:, :], a["L0_attn_bq"].rearrange("(p a) -> p a", a=1)).then_inc(wloaded, 16)
            sp.dma_start(bkd[:, :], a["L0_attn_bkd"].rearrange("(h p) -> p h", p=LAT),
                         allow_slow_non_contiguous=True).then_inc(wloaded, 16)

            def store(b, k, first):
                for n, (dram, order) in enumerate(((q_dram, Q_PART), (k_dram, K_PART))):
                    sp.wait_ge(part3, 2 * b + n + 1)
                    for s in range(SLOTS):
                        sp.dma_start(dram[:, 16 * s:16 * s + 16, bass.ds(b * SEQ, SEQ)],
                                     part[n][k][:, order[s], :]).then_inc(parts_stored[k], 16)
                sp.wait_ge(v_ready, b + 1)
                sp.dma_start(v_dram[:, bass.ds(b * NKB, NKB), :], v_sb[k][:, :, :]).then_inc(v_stored[k], 16)
            batches(sp, store)
            for k in range(2):
                sp.wait_ge(parts_stored[k], BATCH // 2 * NST)
                sp.wait_ge(v_stored[k], BATCH // 2 * 16)

        @block.gpsimd
        def _(pool):
            nc.gpsimd.memset(wku[:, :], 0.0).then_inc(cleared, 1)
            for k in range(2):
                nc.gpsimd.memset(lat[k][:, :], 0.0).then_inc(scaled, 1)
            pool.wait_ge(scaled, 2)
            for k in range(2):
                nc.gpsimd.memset(lat[k][LAT:LAT + 1, :], 1.0).then_inc(cleared, 1)

            def split(b, k, first):
                for n in range(2):
                    pool.wait_ge(part1, 2 * b + n + 1)
                    if not first:
                        pool.wait_ge(part3, 2 * (b - 2) + n + 1)
                    nc.gpsimd.tensor_tensor(rest1[n][k][:, :], whole[n][k][:, :], part[n][k][:, 0, :],
                                            ALU.subtract).then_inc(left1, 1)
                for n in range(2):
                    pool.wait_ge(part2, 2 * b + n + 1)
                    nc.gpsimd.tensor_tensor(rest2[n][k][:, :], rest1[n][k][:, :], part[n][k][:, 1, :],
                                            ALU.subtract).then_inc(left2, 1)
            batches(pool, split)

        @block.scalar
        def _(act):
            def evacuate(b, k, first):
                act.wait_ge(lat_mm, b + 1)
                if not first or k:
                    act.wait_ge(lat_ready, b)
                for h in range(2):
                    nc.scalar.activation(act_half[h][:, :], lat_ps[h][0:LAT, :], ACT.Gelu, bias=bkd[:, h:h + 1])\
                      .then_inc(gelu, 1)
                for n, (ps, mm) in enumerate(((q_ps, q_mm), (k_ps, k_mm))):
                    act.wait_ge(mm, b + 1)
                    if not first:
                        act.wait_ge(left1, 2 * (b - 2) + n + 1)
                    if n == 0:
                        nc.scalar.activation(whole[n][k][:, :], ps[:, :], ACT.Identity, bias=bq[:, 0:1],
                                             scale=HD ** -0.5).then_inc(whole_ready, 1)
                    else:
                        nc.scalar.copy(whole[n][k][:, :], ps[:, :]).then_inc(whole_ready, 1)
            act.wait_ge(wloaded, 96)
            act.wait_ge(scaled, 3)
            batches(act, evacuate)

        @block.vector
        def _(dve):
            dve.wait_ge(wloaded, 96)
            nc.vector.tensor_scalar(bq[:, :], bq[:, :], HD ** -0.5, None, ALU.mult).then_inc(scaled, 1)

            def work(b, k, first):
                dve.wait_ge(gelu, 2 * b + 2)
                if not first:
                    dve.wait_ge(v_mm, b - 1)
                nc.vector.tensor_tensor(lat[k][0:LAT, :], act_half[0][:, :], act_half[1][:, :], ALU.add)\
                  .then_inc(lat_ready, 1)
                for n in range(2):
                    dve.wait_ge(whole_ready, 2 * b + n + 1)
                    if not first:
                        dve.wait_ge(parts_stored[k], (b - k) * (NST // 2))
                    nc.vector.tensor_copy(part[n][k][:, 0, :], whole[n][k][:, :]).then_inc(part1, 1)
                dve.wait_ge(v_mm, b + 1)
                if not first:
                    dve.wait_ge(v_stored[k], (b - k) * 8)
                nc.vector.tensor_copy(v_sb[k][:, :, :].rearrange("p a b -> p (a b)"), v_ps[:, :]).then_inc(v_ready, 1)
                for n in range(2):
                    dve.wait_ge(left1, 2 * b + n + 1)
                    nc.vector.tensor_copy(part[n][k][:, 1, :], rest1[n][k][:, :]).then_inc(part2, 1)
                for n in range(2):
                    dve.wait_ge(left2, 2 * b + n + 1)
                    nc.vector.tensor_copy(part[n][k][:, 2, :], rest2[n][k][:, :]).then_inc(part3, 1)
            batches(dve, work)

        @block.tensor
        def _(pe):
            pe.wait_ge(wloaded, 96)
            pe.wait_ge(cleared, 3)

            def product(b, k, first):
                xb = xnT[:, bass.ds(b * SEQ, SEQ)]
                if not first or k:
                    pe.wait_ge(gelu, 2 * b)
                for h in range(2):
                    mm = nc.tensor.matmul(lat_ps[h][0:LAT, :], wkd[:, h * LAT:(h + 1) * LAT], xb, start=True, stop=True)
                mm.then_inc(lat_mm, 1)
                if not first or k:
                    pe.wait_ge(whole_ready, 2 * b)
                nc.tensor.matmul(q_ps[:, :], wq[:, :], xb, start=True, stop=True).then_inc(q_mm, 1)
                pe.wait_ge(lat_ready, b + 1)
                nc.tensor.matmul(k_ps[:, :], wku[:, 0:D], lat[k][:, :], start=True, stop=True).then_inc(k_mm, 1)
                if not first or k:
                    pe.wait_ge(v_ready, b)
                for kb in range(NKB):
                    mm = nc.tensor.matmul(v_ps[:, kb * D:(kb + 1) * D], lat[k][:, kb * P:(kb + 1) * P],
                                          wku[:, D:2 * D], start=True, stop=True)
                mm.then_inc(v_mm, 1)
            batches(pe, product)


EXP_UNITS = [(2 * SEQ, [(0, 0, 0), (SEQ, 1, 0)]),
             (2 * SEQ, [(0, 0, 1), (384, 0, 3), (SEQ, 1, 1), (SEQ + 384, 1, 3)]),
             (SEQ, [(0, 0, 2), (256, 1, 2)])]
EXP_AT = [0, 2 * SEQ, 4 * SEQ]
PROBS = 5 * SEQ
PROB_AT = {(hp, kb): EXP_AT[u] + c for u, (_, ps) in enumerate(EXP_UNITS) for c, hp, kb in ps}
MAX_UNITS = [(h, 1, 3) for h in range(4)] + [(h, 1, 2) for h in range(4)] + [(0, 2, 1), (2, 2, 1), (0, 4, 0)]
NEX, NMX = 2 * len(EXP_UNITS), len(MAX_UNITS)


def mla_attend(nc, keep, a, st0, name):
    ident, identb = keep["ident"], keep["identb"]
    xnT, q_dram, k_dram, v_dram = st0
    with Stage(nc, name) as st:
        QS = [st.sb(f"QS{k}", [P, NPAIR, SEQ], BF16) for k in range(2)]
        KS = [st.sb(f"KS{k}", [P, HEADS, SEQ], BF16) for k in range(2)]
        KP = [st.sb(f"KP{k}", [P, 2, SEQ], BF16) for k in range(2)]
        probs = [st.sb(f"probs{k}", [P, 2, PROBS]) for k in range(2)]
        v_in = [st.sb(f"v_in{k}", [P, NKB, D]) for k in range(2)]
        v_aug = [st.sb(f"v_aug{k}", [P, NKB, HEADS, 32]) for k in range(2)]
        out_raw = st.sb("out_raw", [P, SEQ])
        recip = st.sb("recip", [P, NKB, 4])
        out_tok = st.sb("out_tok", [P, NKB, D])
        mx = [st.sb(f"mx{k}", [P, NKB, 4]) for k in range(2)]
        mrest = [st.sb(f"mrest{k}", [P, NKB, 4]) for k in range(2)]
        mstack = [st.sb(f"mstack{k}", [P, NKB, 4, 8], BF16) for k in range(2)]
        mask_q, mask_k = st.sb("mask_q", [P, P], BF16), st.sb("mask_k", [P, P], BF16)
        head_rows = st.sb("head_rows", [P, 2])
        bo = st.sb("bo", [P, D])
        max_ps = [st.ps(f"maxp{k}", [P, SEQ]) for k in range(2)]
        exp_ps = [st.ps(f"expp{k}", [P, 2 * SEQ]) for k in range(2)]
        sum_ps = st.ps("sump", [P, SEQ])
        misc_ps = st.ps("misc", [P, SEQ])
        misc_b = misc_ps[:, :].bitcast(BF16).rearrange("p (j q) -> p j q", j=2)
        cleared, consts = st.sem("cleared"), st.sem("consts")
        loaded = [st.sem(f"loaded{k}") for k in range(2 * NG)]
        v_loaded = [st.sem(f"v_loaded{k}") for k in range(2)]
        bo_loaded = st.sem("bo_loaded")
        keys_ready, v_ready, x_biased = st.sem("keys_ready"), st.sem("v_ready"), st.sem("x_biased")
        score_mm, exp_done, max_mm, max_done = (st.sem(n) for n in ("score_mm", "exp_done", "max_mm", "max_done"))
        values_mm, raw_ready, raw_turned, tok_ready = (st.sem(n) for n in ("values_mm", "raw_ready", "raw_turned", "tok_ready"))
        link_sem, mstack_ready, m_turned, m_ready = (st.sem(n) for n in ("link", "mstack_ready", "m_turned", "m_ready"))
        all_turned, batch_done = st.sem("all_turned"), st.sem("batch_done")
        block = st.block()

        row_no = st.sb("row_no", [P, 1], I32)
        recip_ready, heads_ready = st.sem("recip_ready"), st.sem("heads_ready")
        sp_passed, pool_passed = st.sem("sp_passed"), st.sem("pool_passed")

        def steps(eng, one):
            for k in range(-4, 8):
                one(0, k)
            with eng.Fori(1, BATCH // 2 - 1) as i:
                for k in range(8):
                    one(i, k)
            for k in range(10):
                one(BATCH // 2 - 1, k)

        def there(i, k):
            return not isinstance(i, int) or 0 <= 8 * i + k < NSTEP

        @block.sync
        def _(sp):
            sp.wait_ge(cleared, 4)

            def load(i, k):
                if not 0 <= k < 8:
                    return
                s, par, g = 8 * i + k, k // 4, k % 4
                if there(i, k - 8):
                    sp.wait_ge(score_mm, (s - 7) * NEX)
                cols = bass.ds((8 * i + 4 * par) * P, SEQ)
                sp.dma_start(QS[par][0:ROWS, 2 * g:2 * g + 2, :],
                             q_dram[2 * g:2 * g + 2, :, cols].rearrange("j r t -> r j t")).then_inc(loaded[k], 16)
                if there(i, k - 2):
                    sp.wait_ge(keys_ready, s - 1)
                sp.dma_start(KP[k % 2][0:ROWS, :, :],
                             k_dram[2 * g:2 * g + 2, :, cols].rearrange("j r t -> r j t")).then_inc(loaded[k], 16)
                if g == 2:
                    if there(i, k - 8):
                        sp.wait_ge(v_ready, 2 * i + par - 1)
                        pass_waits(sp, sp_passed)
                    sp.dma_start(v_in[par][:, :, :], v_dram[:, bass.ds(8 * i + 4 * par, NKB), :])\
                      .then_inc(v_loaded[par], 16)
            steps(sp, load)

        @block.scalar
        def _(act):
            act.dma_start(bo[:, :], a["L0_attn_bo"].partition_broadcast(P)).then_inc(bo_loaded, 16)

            def expo(i, k, u):
                if not there(i, k):
                    return
                s = 8 * i + k
                act.wait_ge(score_mm, s * NEX + u + 1)
                if u == 0 and there(i, k - 2):
                    act.wait_ge(values_mm, s - 1)
                w, at = EXP_UNITS[u % 3][0], EXP_AT[u % 3]
                nc.scalar.activation(probs[k % 2][:, u // 3, at:at + w], exp_ps[u % 2][:, 0:w], ACT.Exp)\
                  .then_inc(exp_done, 1)

            def copy_batch(i, k):
                if k % 4 == 1 and there(i, k - 2):
                    b = 2 * i + (k - 2) // 4
                    act.wait_ge(all_turned, b + 1)
                    nc.scalar.copy(xnT[:, bass.ds(b * SEQ, SEQ)], misc_ps[:, :]).then_inc(batch_done, 1)

            def copy_raw(i, k):
                if there(i, k - 1):
                    s = 8 * i + k - 1
                    act.wait_ge(values_mm, s + 1)
                    if there(i, k - 2):
                        act.wait_ge(raw_turned, s)
                    nc.scalar.copy(out_raw[:, :], sum_ps[:, :]).then_inc(raw_ready, 1)

            def copy_max(i, k):
                if there(i, k + 3):
                    m, par, g = 8 * i + k + 3, (k + 3) % 8 // 4, (k + 3) % 4
                    act.wait_ge(m_turned, m + 1)
                    nc.scalar.copy(QS[par][ROWS:P - 16, 2 * g:2 * g + 2, :], misc_b[ROWS:P - 16, :, :])\
                      .then_inc(m_ready, 1)

            def step(i, k):
                expo(i, k, 0)
                expo(i, k, 1)
                copy_batch(i, k)
                expo(i, k, 2)
                expo(i, k, 3)
                copy_raw(i, k)
                expo(i, k, 4)
                copy_max(i, k)
                expo(i, k, 5)
            steps(act, step)
            act.wait_ge(batch_done, BATCH)

        @block.vector
        def _(dve):
            link = chained(dve, link_sem)
            dve.wait_ge(cleared, 5)
            link(nc.vector.tensor_scalar(row_no[:, :], row_no[:, :], 8, None, ALU.bitwise_and))
            link(nc.vector.tensor_scalar(head_rows[:, 1:2], row_no[:, :], 0.125, None, ALU.mult))
            nc.vector.tensor_scalar(head_rows[:, 0:1], head_rows[:, 1:2], -1.0, 1.0, ALU.mult, ALU.add)\
              .then_inc(heads_ready, 1)
            LINKED = 2

            def maxima(i, k):
                if not there(i, k):
                    return
                m = 8 * i + k
                for u, (h, n, qb) in enumerate(MAX_UNITS):
                    dve.wait_ge(max_mm, m * NMX + u + 1)
                    N = (qb + 1) * P
                    nc.vector.tensor_reduce(mx[k % 2][:, qb, h:h + n],
                                            max_ps[(k + u) % 2][:, 0:n * N].rearrange("p (n k) -> p n k", n=n),
                                            AX.X, ALU.max).then_inc(max_done, 1)

            def split_max(i, k):
                if not there(i, k):
                    return
                m = 8 * i + k
                top, rest, parts = mx[k % 2], mrest[k % 2], mstack[k % 2]

                def linked(n, ins):
                    ins.then_inc(link_sem, 1)
                    dve.wait_ge(link_sem, LINKED + 4 * m + n)
                dve.wait_ge(max_done, (m + 1) * NMX)
                if there(i, k - 2):
                    dve.wait_ge(m_turned, m - 1)
                linked(1, nc.vector.tensor_scalar(parts[:, :, :, 0], top[:, :, :], -1.0, None, ALU.mult))
                linked(2, nc.vector.scalar_tensor_tensor(out=rest[:, :, :], in0=top[:, :, :], scalar=-1.0,
                                                         in1=parts[:, :, :, 0], op0=ALU.mult, op1=ALU.subtract))
                linked(3, nc.vector.tensor_copy(parts[:, :, :, 1], rest[:, :, :]))
                linked(4, nc.vector.tensor_tensor(rest[:, :, :], rest[:, :, :], parts[:, :, :, 1], ALU.subtract))
                nc.vector.tensor_copy(parts[:, :, :, 2], rest[:, :, :]).then_inc(mstack_ready, 1)

            def divide(i, k):
                if not there(i, k):
                    return
                s, g = 8 * i + k, k % 4
                dve.wait_ge(raw_turned, s + 1)
                raw = misc_ps[:, :].rearrange("p (b h c) -> p b h c", b=NKB, h=4)
                nc.vector.reciprocal(recip[:, :, :], raw[:, :, :, HD]).then_inc(recip_ready, 1)
                dve.wait_ge(recip_ready, s + 1)
                if g == 0 and there(i, k - 4):
                    dve.wait_ge(all_turned, 2 * i + k // 4)
                nc.vector.tensor_tensor(
                    out_tok[:, :, g * 32:g * 32 + 32].rearrange("p b (h c) -> p b h c", h=4), raw[:, :, :, 0:HD],
                    recip[:, :, :].unsqueeze(3).broadcast_to([P, NKB, 4, HD]), ALU.mult).then_inc(tok_ready, 1)

            dve.wait_ge(consts, 7)
            def step(i, k):
                maxima(i, k + 4)
                split_max(i, k + 4)
                divide(i, k - 1)
            steps(dve, step)

        @block.gpsimd
        def _(pool):
            for k in range(2):
                nc.gpsimd.memset(QS[k][ROWS:P, :, :], 0.0).then_inc(cleared, 1)
                nc.gpsimd.memset(KP[k][ROWS:P, :, :], 1.0).then_inc(cleared, 1)
            pool.wait_ge(cleared, 4)
            nc.gpsimd.iota(row_no[:, :], pattern=[[0, 1]], base=0, channel_multiplier=1).then_inc(cleared, 1)
            for k in range(2):
                nc.gpsimd.memset(v_aug[k][:, :, :, :], 0.0).then_inc(consts, 1)
                nc.gpsimd.memset(mstack[k][:, :, :, :], 0.0).then_inc(consts, 1)
            nc.gpsimd.memset(mask_q[:, :], 0.0).then_inc(consts, 1)
            nc.gpsimd.memset(mask_k[:, :], 0.0).then_inc(consts, 1)
            pool.wait_ge(consts, 6)
            nc.gpsimd.affine_select(out=mask_q[:, :], in_=mask_q[:, :], compare_op=ALU.is_ge, fill=NEG, base=0,
                                    pattern=[[-1, P]], channel_multiplier=1).then_inc(consts, 1)
            nc.gpsimd.affine_select(out=mask_k[:, :], in_=mask_k[:, :], compare_op=ALU.is_ge, fill=NEG, base=0,
                                    pattern=[[1, P]], channel_multiplier=-1).then_inc(consts, 1)
            for k in range(2):
                nc.gpsimd.memset(v_aug[k][:, :, :, HD:HD + 1], 1.0).then_inc(consts, 1)
            pool.wait_ge(heads_ready, 1)

            def keys(i, k):
                if not 0 <= k < 8:
                    return
                s, par, g = 8 * i + k, k // 4, k % 4
                pool.wait_ge(loaded[k], 32 * (i + 1))
                if there(i, k - 8):
                    pool.wait_ge(score_mm, (s - 7) * NEX)
                    pass_waits(pool, pool_passed)
                heads = KS[par][:, :, :].rearrange("p (j e) t -> p j e t", e=2)
                for e in range(2):
                    ins = nc.gpsimd.tensor_scalar(heads[:, 2 * g:2 * g + 2, e, :], KP[k % 2][:, :, :],
                                                  head_rows[:, e:e + 1], None, ALU.mult)
                ins.then_inc(keys_ready, 1)
                if g == 2:
                    pool.wait_ge(v_loaded[par], 16 * (i + 1))
                    if there(i, k - 8):
                        pool.wait_ge(values_mm, 8 * i + 4 * par - 4)
                        pass_waits(pool, pool_passed)
                    nc.gpsimd.tensor_copy(v_aug[par][:, :, :, 0:HD],
                                          v_in[par][:, :, :].rearrange("p b (h c) -> p b h c", h=HEADS))\
                      .then_inc(v_ready, 1)
            pool.wait_ge(consts, 10)
            steps(pool, keys)
            pool.wait_ge(bo_loaded, 16)
            nc.gpsimd.tensor_tensor(keep["x"][:, :, :], keep["x"][:, :, :],
                                    bo[:, :].unsqueeze(1).broadcast_to([P, RUN, D]), ALU.add).then_inc(x_biased, 1)
            pool.wait_ge(x_biased, 1)

        @block.tensor
        def _(pe):
            pe.wait_ge(consts, 10)

            def score(i, k, u):
                if not there(i, k):
                    return
                s, par, g = 8 * i + k, k % 8 // 4, k % 4
                if u == 0:
                    pe.wait_ge(m_ready, s + 1)
                if u >= 2 or there(i, k - 1):
                    pe.wait_ge(exp_done, s * NEX + u - 1)
                out, j = exp_ps[u % 2], 2 * g + u // 3
                for c, e, kb in EXP_UNITS[u % 3][1]:
                    n = SEQ - kb * P
                    nc.tensor.matmul(out[:, c:c + n], KS[par][:, 2 * j + e, kb * P:(kb + 1) * P],
                                     QS[par][:, j, kb * P:SEQ], start=True, stop=False)
                    mm = nc.tensor.matmul(out[:, c:c + P], identb[:, :], mask_k[:, :], start=False, stop=True)
                mm.then_inc(score_mm, 1)

            def maximum(i, k, u):
                if not there(i, k):
                    return
                m, par, g = 8 * i + k, k % 8 // 4, k % 4
                if u == 0:
                    pe.wait_ge(keys_ready, m + 1)
                if u >= 2 or there(i, k - 1):
                    pe.wait_ge(max_done, m * NMX + u - 1)
                h0, heads, qb = MAX_UNITS[u]
                n = (qb + 1) * P
                for e in range(heads):
                    h, out = 4 * g + h0 + e, max_ps[(k + u) % 2]
                    nc.tensor.matmul(out[:, e * n:(e + 1) * n], QS[par][0:ROWS, h // 2, qb * P:(qb + 1) * P],
                                     KS[par][0:ROWS, h, 0:n], start=True, stop=False)
                    mm = nc.tensor.matmul(out[:, (e + 1) * n - P:(e + 1) * n], identb[:, :], mask_q[:, :],
                                          start=False, stop=True)
                mm.then_inc(max_mm, 1)

            def values(i, k, kb):
                if not there(i, k):
                    return
                s, par, g = 8 * i + k, k % 8 // 4, k % 4
                if kb == 0:
                    pe.wait_ge(exp_done, (s + 1) * NEX)
                    pe.wait_ge(v_ready, 2 * i + k // 4 + 1)
                    if there(i, k - 1):
                        pe.wait_ge(raw_ready, s)
                n = SEQ - kb * P
                for h in range(4):
                    at = PROB_AT[h % 2, kb]
                    mm = nc.tensor.matmul(sum_ps[32 * h:32 * h + 32, kb * P:SEQ], v_aug[par][:, kb, 4 * g + h, :],
                                          probs[k % 2][:, h // 2, at:at + n], start=(kb == 0), stop=(kb == NKB - 1))
                if kb == NKB - 1:
                    mm.then_inc(values_mm, 1)

            def turn_batch(i, k):
                if k % 4 == 1 and there(i, k - 2):
                    pe.wait_ge(tok_ready, 8 * i + k - 1)
                    for b in range(NKB):
                        mm = nc.tensor.transpose(misc_ps[:, b * P:(b + 1) * P], out_tok[:, b, :], ident[:, :])
                    mm.then_inc(all_turned, 1)

            def turn_max(i, k):
                if there(i, k + 3):
                    pe.wait_ge(mstack_ready, 8 * i + k + 4)
                    if there(i, k - 2):
                        pe.wait_ge(tok_ready, 8 * i + k - 1)
                    if k % 4 == 1 and there(i, k - 2):
                        pe.wait_ge(batch_done, 2 * i + (k - 2) // 4 + 1)
                    if there(i, k + 2):
                        pe.wait_ge(m_ready, 8 * i + k + 3)
                    for j in range(2):
                        for b in range(NKB):
                            mm = nc.tensor.transpose(misc_b[ROWS:P - 16, j, b * P:(b + 1) * P],
                                                     mstack[(k + 3) % 2][:, b, 2 * j:2 * j + 2, :]
                                                     .rearrange("p h c -> p (h c)"), identb[:, :])
                    mm.then_inc(m_turned, 1)

            def turn_raw(i, k):
                if there(i, k - 1):
                    s = 8 * i + k - 1
                    pe.wait_ge(raw_ready, s + 1)
                    if there(i, k + 3):
                        pe.wait_ge(m_ready, s + 5)
                    elif k % 4 == 1 and there(i, k - 2):
                        pe.wait_ge(batch_done, 2 * i + (k - 2) // 4 + 1)
                    elif there(i, k - 2):
                        pe.wait_ge(tok_ready, s)
                    for b in range(NKB):
                        mm = nc.tensor.transpose(misc_ps[:, b * P:(b + 1) * P], out_raw[:, b * P:(b + 1) * P],
                                                 ident[:, :])
                    mm.then_inc(raw_turned, 1)

            def step(i, k):
                score(i, k, 0)
                maximum(i, k + 4, 0)
                maximum(i, k + 4, 1)
                score(i, k, 1)
                turn_batch(i, k)
                maximum(i, k + 4, 2)
                maximum(i, k + 4, 3)
                values(i, k - 1, 0)
                score(i, k, 2)
                maximum(i, k + 4, 4)
                maximum(i, k + 4, 5)
                values(i, k - 1, 1)
                score(i, k, 3)
                maximum(i, k + 4, 6)
                maximum(i, k + 4, 7)
                values(i, k - 1, 2)
                values(i, k - 1, 3)
                score(i, k, 4)
                maximum(i, k + 4, 8)
                maximum(i, k + 4, 9)
                turn_max(i, k)
                score(i, k, 5)
                maximum(i, k + 4, 10)
                turn_raw(i, k)
            steps(pe, step)


def mla_output(nc, keep, a, st0, name):
    x, outT = keep["x"], st0[0]
    with Stage(nc, name) as st:
        wo = st.sb("wo", [P, D])
        out_ps = [st.ps(f"out{k}", [P, CH, D]) for k in range(4)]
        loaded, projected, added = st.sem("loaded"), st.sem("projected"), st.sem("added")
        runs = outT[:, :].rearrange("d (p r) -> d p r", r=RUN)
        block = st.block()

        @block.sync
        def _(sp):
            sp.dma_start(wo[:, :], a["L0_attn_Wo"]).then_inc(loaded, 16)

        @block.tensor
        def _(pe):
            pe.wait_ge(loaded, 16)
            for c in range(NCH):
                if c >= 4:
                    pe.wait_ge(added, c - 3)
                for t in range(CH):
                    mm = nc.tensor.matmul(out_ps[c % 4][:, t, :], runs[:, :, c * CH + t], wo[:, :], start=True, stop=True)
                mm.then_inc(projected, 1)

        @block.vector
        def _(dve):
            for c in range(NCH):
                dve.wait_ge(projected, c + 1)
                xs = x[:, c * CH:(c + 1) * CH, :]
                nc.vector.tensor_tensor(xs, xs, out_ps[c % 4][:, :, :], ALU.add).then_inc(added, 1)
            dve.wait_ge(added, NCH)


def mla(nc, keep, a, name):
    with ExitStack() as ctx:
        xnT = ctx.enter_context(nc.sbuf_tensor(f"{name}_xnT", [P, TOK], F32))
        q_dram = nc.dram_tensor(f"{name}_q", [NPAIR, ROWS, TOK], BF16, kind="Internal").ap()
        k_dram = nc.dram_tensor(f"{name}_k", [NPAIR, ROWS, TOK], BF16, kind="Internal").ap()
        v_dram = nc.dram_tensor(f"{name}_v", [P, BATCH * NKB, D], F32, kind="Internal").ap()
        st0 = (xnT, q_dram, k_dram, v_dram)
        mla_project(nc, keep, a, st0, name)
        mla_attend(nc, keep, a, st0, name + "a")
        mla_output(nc, keep, a, st0, name + "o")


E = 64
TOKS = 8
NS = RUN // TOKS
UI, UO = 32, 64
TAB = UI * UO
HALF = P // 2
MOE_TABLES = ("A_up", "B_up", "A_down", "B_down")


def moe_tables(nc, keep, a, tab, name):
    ident = keep["ident"]
    with Stage(nc, name) as st:
        raw = [st.sb(f"raw{k}", [P, TAB]) for k in range(2)]
        rest = [st.sb(f"rest{k}", [P, TAB]) for k in range(2)]
        second = [st.sb(f"second{k}", [P, TAB], BF16) for k in range(2)]
        router_up, router_down = st.sb("router_up", [E, TOKS, P]), st.sb("router_down", [E, UI, 2, UO])
        bias_rows = st.sb("bias_rows", [UO, 2, UO])
        turn_ps = [st.ps(f"turn{k}", [P, TOKS, E]) for k in range(2)]
        loaded, loaded_r = [st.sem(f"loaded{k}") for k in range(2)], st.sem("loaded_r")
        link_sem, split_done, turned, copied = st.sem("link"), st.sem("split_done"), st.sem("turned"), st.sem("copied")
        zeroed, scaled, consts = st.sem("zeroed"), st.sem("scaled"), st.sem("consts")
        block = st.block()

        @block.sync
        def _(sp):
            sp.dma_start(router_up[:, :, :], a["L1_ffn_W_up"].rearrange("e (t d) -> e t d", t=TOKS)).then_inc(loaded_r, 16)
            for h in range(2):
                sp.dma_start(router_down[:, :, h, :], a["L1_ffn_W_down"].rearrange("e (h o p) -> e h o p", h=2, p=UO)[:, h])\
                  .then_inc(loaded_r, 16)
                sp.dma_start(bias_rows[:, h, :], a["L1_ffn_bias_up"].rearrange("(o p) -> o p", p=UO)).then_inc(loaded_r, 16)
            sp.dma_start(tab["bias_down"][:, :], a["L1_ffn_bias_down"].partition_broadcast(P)).then_inc(loaded_r, 16)
            sp.dma_start(tab["scale_up"][:, :], a["L1_ffn_scale_up"].partition_broadcast(P)).then_inc(loaded_r, 16)
            sp.dma_start(tab["scale_down"][:, :], a["L1_ffn_scale_down"].partition_broadcast(P)).then_inc(loaded_r, 16)

        @block.scalar
        def _(act):
            for n, w in enumerate(MOE_TABLES):
                if n >= 2:
                    act.wait_ge(split_done, n - 1)
                for h in range(2):
                    act.dma_start(raw[n % 2][h * HALF:(h + 1) * HALF, :],
                                  a["L1_ffn_" + w].rearrange("e o i -> e (o i)")).then_inc(loaded[n % 2], 16)
            for n in range(6):
                act.wait_ge(turned, n + 1)
                if n == 0:
                    out, src = tab["router_upT"][:, :, :], turn_ps[0][:, :, :]
                elif n == 1:
                    out, src = tab["bias_upT"][:, :], turn_ps[1][:, 0, :]
                else:
                    out, src = tab["router_downT"][:, (n - 2) * TOKS:(n - 1) * TOKS, :], turn_ps[n % 2][:, :, :]
                nc.scalar.copy(out, src).then_inc(copied, 1)
            act.wait_ge(copied, 6)

        @block.tensor
        def _(pe):
            pe.wait_ge(loaded_r, 8 * 16)
            for t in range(TOKS):
                mm = nc.tensor.transpose(turn_ps[0][:, t, :], router_up[:, t, :], ident[0:E, 0:E])
            mm.then_inc(turned, 1)
            nc.tensor.transpose(turn_ps[1][:, 0, :], bias_rows[:, :, :].rearrange("o h p -> o (h p)"),
                                ident[0:UO, 0:UO]).then_inc(turned, 1)
            for n in range(4):
                pe.wait_ge(copied, n + 1)
                for t in range(TOKS):
                    mm = nc.tensor.transpose(turn_ps[n % 2][:, t, :], router_down[:, n * TOKS + t, :, :].rearrange("e h p -> e (h p)"),
                                             ident[0:E, 0:E])
                mm.then_inc(turned, 1)

        @block.gpsimd
        def _(pool):
            nc.gpsimd.iota(tab["expert_no"][:, :, :], pattern=[[0, 2], [1, E]], base=0, channel_multiplier=0,
                           allow_small_or_imprecise_dtypes=True).then_inc(consts, 1)
            for n in ("spread", "pick_half", "pick0", "pick1"):
                nc.gpsimd.memset(tab[n][:, :], 0.0).then_inc(zeroed, 1)
            nc.gpsimd.memset(tab["euler"][:, :], float(np.e)).then_inc(zeroed, 1)
            pool.wait_ge(zeroed, 5)
            for b in range(2):
                nc.gpsimd.affine_select(out=tab["spread"][:, :], in_=tab["spread"][:, :], compare_op=ALU.not_equal,
                                        fill=1.0, base=-HALF * b, pattern=[[-1, HALF]], channel_multiplier=1)\
                  .then_inc(consts, 1)
                pool.wait_ge(consts, 2 + b)

        @block.vector
        def _(dve):
            link = chained(dve, link_sem)
            dve.wait_ge(zeroed, 5)
            for h in range(2):
                rows = slice(h * HALF, (h + 1) * HALF)
                link(nc.vector.memset(tab["pick_half"][rows, rows], 1.0))
                link(nc.vector.memset(tab["pick0"][rows, h * HALF:h * HALF + 32], 1.0))
                link(nc.vector.memset(tab["pick1"][rows, h * HALF + 32:(h + 1) * HALF], 1.0))
            dve.wait_ge(loaded_r, 8 * 16)
            link(nc.vector.tensor_scalar(tab["bias_down"][:, :], tab["bias_down"][:, :], 0.5, None, ALU.mult))
            link(nc.vector.tensor_scalar(tab["scale_down"][:, :], tab["scale_down"][:, :], 0.5, None, ALU.mult))
            for n, w in enumerate(MOE_TABLES):
                dve.wait_ge(loaded[n % 2], 32 * (n // 2 + 1))
                r, left, mid = raw[n % 2], rest[n % 2], second[n % 2]
                two, third = tab[w], tab[w + "3"]
                link(nc.vector.tensor_copy(two[:, :], r[:, :]))
                link(nc.vector.tensor_tensor(left[:, :], r[:, :], two[:, :], ALU.subtract))
                link(nc.vector.tensor_copy(mid[:, :], left[:, :]))
                link(nc.vector.tensor_copy(two[HALF:P, :], mid[HALF:P, :]))
                link(nc.vector.tensor_tensor(left[0:HALF, :], left[0:HALF, :], mid[0:HALF, :], ALU.subtract))
                link(nc.vector.memset(third[HALF:P, :], 0.0))
                link(nc.vector.tensor_copy(third[0:HALF, :], left[0:HALF, :]))
                dve.sem_inc(split_done, 1)


def moe(nc, keep, tab, name):
    x, ident, identb = keep["x"], keep["ident"], keep["identb"]
    with Stage(nc, name) as st:
        xn = st.sb("xn", [P, TOKS, D])
        xnT = st.sb("xnT", [P, TOKS, P])
        xsT = st.sb("xsT", [P, 2, 32, UI])
        Bu, Au = st.sb("Bu", [P, 32, UO]), st.sb("Au", [P, 32, UO])
        Zu = st.sb("Zu", [P, 32, UO])
        hT = [st.sb(f"hT{k}", [P, 2, 32, UO]) for k in range(2)]
        hR = st.sb("hR", [P, UI, P])
        Bd = st.sb("Bd", [P, 2, 32, 2, 32])
        Ad = st.sb("Ad", [P, 2, 32, 2, 32])
        ytok = Zu[:, :, :].rearrange("p n o -> p (n o)")[:, 0:TOKS * D]
        lgT = st.sb("lgT", [P, P])
        lg, top, topi = st.sb("lg", [P, E]), st.sb("top", [P, 8]), st.sb("topi", [P, 8], U32)
        chosen, gap, ratio, den = st.sb("chosen", [P, 2]), st.sb("gap", [P, 1]), st.sb("ratio", [P, 1]), st.sb("den", [P, 1])
        prob = st.sb("prob", [P, 2])
        onehot = [st.sb(f"onehot{k}", [P, 2 * E], BF16) for k in range(2)]
        spreadp = st.sb("spreadp", [P, 2, HALF])
        ohTu = st.sb("ohTu", [P, 2, 2, 2, 32], BF16)
        ohTd = st.sb("ohTd", [P, 2, P], BF16)
        probu, probd = st.sb("probu", [P, HALF]), st.sb("probd", [P, 2, HALF])
        gat_ps = [st.ps(f"gat{k}", [P, 512]) for k in range(2)]
        z_ps = [st.ps(f"z{k}", [P, 8, UO]) for k in range(2)]
        y_ps = st.ps("y", [P, 32, 32])
        misc = [st.ps(f"misc{k}", [P, 512]) for k in range(2)]
        names = ("xn_ready", "turned_x", "log_mm", "logits", "one_ready", "pow_in", "pow_done",
                 "probs_ready", "oh_turned", "spread_mm", "free0", "free1", "gat_mm",
                 "gat_read", "z_mm", "z_read", "h_mm", "h_raw", "h_ready", "hR_ready", "pe_passed", "dve_passed",
                 "xsT_ready", "y_mm", "y_read", "x_done", "link")
        S = {n: st.sem(n) for n in names}
        block = st.block()
        y_flat = y_ps[:, :, :].rearrange("p a b -> p (a b)")
        h_ps = [y_flat[:, b * 512:(b + 1) * 512].rearrange("p (n o) -> p n o", n=8) for b in range(2)]

        def turns(eng, one):
            one(-1, 1)
            one(0, 0)
            with eng.Fori(0, NS // 2 - 1) as i:
                one(i * 2 + 1, 1)
                one(i * 2 + 2, 0)
            one(NS - 1, 1)
            one(NS, 0)

        def has(s, d):
            return not isinstance(s, int) or 0 <= s + d < NS

        def before(s, j, up):
            if not isinstance(s, int) or 0 < s < NS:
                return 2 * up * s - up + j
            return j if s == 0 else 2 * up * NS - 2 * up + j

        def uses(s, j):
            if isinstance(s, int) and s == -1:
                return j - 2
            return 5 * s + 1 + j - (3 if isinstance(s, int) and s == NS else 0)

        def routing(s, down):
            if isinstance(s, int) and s == -1:
                return 0
            if isinstance(s, int) and s == NS:
                return 2 * NS - 1
            return 2 * s + (0 if down else 1)

        @block.tensor
        def _(pe):
            def gather(s, j):
                if j < 16:
                    m, w, q = j // 8, "BA"[j // 4 % 2], j % 4
                    if j % 4 == 0 and m == 0:
                        pe.wait_ge(S["free0"], uses(s - 1, 4) + 1)
                else:
                    w, m, q = "BA"[(j - 16) // 8], (j - 16) // 4 % 2, j % 4
                    if j == 16:
                        pe.wait_ge(S["free0"], uses(s, 1) + 1)
                n = before(s, j, 16)
                if j >= 2 or not isinstance(s, int) or s > 0:
                    pe.wait_ge(S["gat_read"], n - 1)
                out = gat_ps[j % 2]
                if j < 16:
                    lhs = ohTu[:, m, :, :, :].rearrange("e h k n -> e (h k n)")
                    for c, t in enumerate((w + "_up", w + "_up3")):
                        mm = nc.tensor.matmul(out[:, :], lhs, tab[t][:, q * 512:(q + 1) * 512], start=(c == 0), stop=(c == 1))
                else:
                    k, half = q // 2, q % 2
                    for c, t in enumerate((w + "_down", w + "_down3")):
                        cols = tab[t][:, :].rearrange("e (p b j) -> e p b j", b=2, j=32)
                        for h in range(2):
                            for b in range(2):
                                n0 = 64 * h + 32 * m
                                mm = nc.tensor.matmul(out[64 * h + 32 * b:64 * h + 32 * b + 32, :],
                                                      ohTd[:, k, n0:n0 + 32], cols[:, half * 16:half * 16 + 16, b, :],
                                                      start=(c == 0), stop=(c == 1))
                mm.then_inc(S["gat_mm"], 1)

            def z_free(s, j):
                if j % 8 >= 2 or not isinstance(s, int) or s > 0:
                    pe.wait_ge(S["z_read"], before(s, j, 8) - 1)

            def up_right(s, m, u):
                if u == 0:
                    pe.wait_ge(S["gat_read"], before(s, 8 * m + 4, 16))
                    if m == 0:
                        pe.wait_ge(S["xsT_ready"], (s + 1) * 8)
                z_free(s, 4 * m + u)
                pass_waits(pe, S["pe_passed"])
                for n in range(8 * u, 8 * u + 8):
                    for q in range(4):
                        rows = slice(32 * q, 32 * q + 32)
                        mm = nc.tensor.matmul(z_ps[u % 2][rows, n % 8, :], xsT[rows, m, n, :], Bu[rows, n, :],
                                              start=True, stop=True)
                mm.then_inc(S["z_mm"], 1)

            def up_left(s, m, u):
                if u == 0:
                    pe.wait_ge(S["gat_read"], before(s, 8 * m + 8, 16))
                    pe.wait_ge(S["z_read"], before(s, 4 * m + 4, 8))
                if m == 0 and u < 2:
                    if not isinstance(s, int) or s > 1:
                        pe.wait_ge(S["y_read"], s - 1)
                if 4 * m + u >= 2 or not isinstance(s, int) or s > 0:
                    pe.wait_ge(S["h_raw"], 8 * s + 4 * m + u - 1)
                pass_waits(pe, S["pe_passed"])
                for n in range(8 * u, 8 * u + 8):
                    for h in range(2):
                        rows = slice(64 * h, 64 * h + 64)
                        mm = nc.tensor.matmul(h_ps[u % 2][rows, n % 8, :], Zu[rows, n, :], Au[rows, n, :],
                                              start=True, stop=True)
                mm.then_inc(S["h_mm"], 1)

            def down_right(s, m, u, k):
                if u == 0:
                    pe.wait_ge(S["gat_read"], before(s, 20 + 4 * m, 16))
                    pe.wait_ge(S["h_ready"], 8 * s)
                z_free(s, 8 + 4 * m + u)
                pass_waits(pe, S["pe_passed"])
                for n in range(8 * u, 8 * u + 8):
                    for h in range(2):
                        rows = slice(64 * h, 64 * h + 64)
                        mm = nc.tensor.matmul(z_ps[u % 2][rows, n % 8, :], hT[k][rows, m, n, :],
                                              Bd[rows, m, n, :, :].rearrange("p k c -> p (k c)"), start=True, stop=True)
                mm.then_inc(S["z_mm"], 1)

            def down_left(s):
                pe.wait_ge(S["gat_read"], before(s, 32, 16))
                pe.wait_ge(S["z_read"], before(s, 16, 8))
                if has(s, 0):
                    pe.wait_ge(S["h_raw"], 8 * s + 8)
                pass_waits(pe, S["pe_passed"])
                for n in range(32):
                    for h in range(2):
                        for m in range(2):
                            rows, g = slice(64 * h, 64 * h + 64), 2 * h + m
                            for k in range(2):
                                mm = nc.tensor.matmul(y_ps[32 * g:32 * g + 32, n, :], Ad[rows, m, n, k, :],
                                                      Bd[rows, m, n, k, :], start=(k == 0), stop=(k == 1))
                mm.then_inc(S["y_mm"], 1)

            def router(s, down):
                use = 0 if down else 3
                if down:
                    pe.wait_ge(S["hR_ready"], s)
                else:
                    for b in range(2):
                        pe.wait_ge(S[f"free{b}"], uses(s, 2) + 1)
                pe.wait_ge(S["free0"], uses(s, use))
                for t in range(UI if down else TOKS):
                    half = slice(64 * (t % 2), 64 * (t % 2) + 64)
                    if down:
                        lhs, rhs = tab["router_downT"][:, t, :], hR[:, t, :]
                    else:
                        lhs, rhs = tab["router_upT"][:, t, :], xnT[:, t, :]
                    mm = nc.tensor.matmul(misc[0][half, 0:P], lhs, rhs, start=(t < 2), stop=(t >= (UI if down else TOKS) - 2))
                mm.then_inc(S["log_mm"], 1)

            def logits(s, down):
                n = uses(s, 0 if down else 3)
                pe.wait_ge(S["free0"], n + 1)
                pe.wait_ge(S["free1"], n)
                nc.tensor.matmul(misc[1][:, 0:E], lgT[:, :], tab["spread"][:, :], start=True, stop=True).then_inc(S["logits"], 1)

            def choices(s, down):
                pe.wait_ge(S["one_ready"], routing(s, down) + 1)
                pe.wait_ge(S["free0"], uses(s, 1 if down else 4))
                for k in range(2):
                    mm = nc.tensor.transpose(misc[0][:, :].bitcast(BF16)[:, k * P:(k + 1) * P], onehot[k][:, :], identb[:, :])
                mm.then_inc(S["oh_turned"], 1)
                pe.wait_ge(S["probs_ready"], routing(s, down) + 1)
                pe.wait_ge(S["free1"], uses(s, 1 if down else 4))
                if down:
                    mm = nc.tensor.matmul(misc[1][:, 0:P], tab["pick_half"][:, :], spreadp[:, :, :].rearrange("p k c -> p (k c)"),
                                          start=True, stop=True)
                else:
                    for k in range(2):
                        mm = nc.tensor.matmul(misc[1][:, 0:HALF], tab[f"pick{k}"][:, :], spreadp[:, k, :],
                                              start=(k == 0), stop=(k == 1))
                mm.then_inc(S["spread_mm"], 1)

            def turn_x(s):
                pe.wait_ge(S["xn_ready"], s + 2)
                for b in range(2):
                    if not (isinstance(s, int) and s == -1):
                        pe.wait_ge(S[f"free{b}"], uses(s, 2))
                    for t in range(4):
                        mm = nc.tensor.transpose(misc[b][:, t * P:(t + 1) * P], xn[:, 4 * b + t, :], ident[:, :])
                    mm.then_inc(S["turned_x"], 1)

            def turn(s, k):
                up, down, nxt = has(s, 0), has(s, -1), has(s, 1)
                if down:
                    router(s, True)
                if up:
                    for u in range(4):
                        gather(s, u)
                if down:
                    logits(s, True)
                if up:
                    for u in range(4):
                        up_right(s, 0, u)
                        gather(s, 4 + u)
                if down:
                    choices(s, True)
                if up:
                    for u in range(4):
                        up_left(s, 0, u)
                        gather(s, 8 + u)
                    for u in range(4):
                        up_right(s, 1, u)
                        gather(s, 12 + u)
                if nxt:
                    turn_x(s)
                for u in range(4):
                    if up:
                        up_left(s, 1, u)
                    if down:
                        gather(s, 16 + u)
                if nxt:
                    router(s, False)
                if down:
                    for u in range(4):
                        down_right(s, 0, u, 1 - k)
                        gather(s, 20 + u)
                if nxt:
                    logits(s, False)
                if down:
                    for u in range(4):
                        down_right(s, 1, u, 1 - k)
                        gather(s, 24 + u)
                if nxt:
                    choices(s, False)
                if down:
                    for u in range(4):
                        gather(s, 28 + u)
                    down_left(s)
            turns(pe, turn)

        @block.vector
        def _(dve):
            def norm(s):
                if not (isinstance(s, int) and s == -1):
                    dve.wait_ge(S["turned_x"], 2 * s + 2)
                for t in range(TOKS):
                    ins = normalize(nc, keep, xn[:, t, :], s * TOKS + TOKS + t)
                ins.then_inc(S["xn_ready"], 1)

            def square(s, u):
                m, h, k = u // 4, u // 2 % 2, u % 2
                if u == 0:
                    dve.wait_ge(S["xn_ready"], s + 2)
                src, dst = 64 * h + 32 * m, 64 * h + 32 * k
                nc.vector.transpose(xsT[dst:dst + 32, m, :, :].rearrange("j n i -> j i n"),
                                    xn[src:src + 32, :, :].rearrange("n t (c j) -> n (t c) j", j=32))\
                  .then_inc(S["xsT_ready"], 1)

            def placed(s, j):
                dve.wait_ge(S["gat_mm"], before(s, j, 16) + 1)
                src = gat_ps[j % 2][:, :].rearrange("n (c j) -> n c j", j=32)
                if j < 16:
                    q, dst = j % 4, (Bu, Au)[j // 4 % 2]
                    out = dst[:, :, q * 16:q * 16 + 16].rearrange("j n c -> j c n")
                else:
                    t, m, q = (j - 16) // 8, (j - 16) // 4 % 2, j % 4
                    if j % 8 == 0 and not (isinstance(s, int) and s == 1):
                        dve.wait_ge(S["y_mm"], s - 1)
                    dst = (Bd, Ad)[t]
                    out = dst[:, m, :, q // 2, q % 2 * 16:q % 2 * 16 + 16].rearrange("j n c -> j c n")
                nc.vector.transpose(out, src).then_inc(S["gat_read"], 1)

            def weigh_up(s, m, u):
                dve.wait_ge(S["z_mm"], before(s, 4 * m + u, 8) + 1)
                if u == 0 and m == 0:
                    dve.wait_ge(S["free1"], uses(s - 1, 4) + 1)
                c = 32 * m + 8 * u
                nc.vector.tensor_tensor(Zu[:, 8 * u:8 * u + 8, :], z_ps[u % 2][:, :, :],
                                        probu[:, c:c + 8].unsqueeze(2).broadcast_to([P, 8, UO]), ALU.mult)\
                  .then_inc(S["z_read"], 1)

            def bias_up(s, m, u, k):
                dve.wait_ge(S["h_mm"], 8 * s + 4 * m + u + 1)
                if m == 0 and u == 0 and (not isinstance(s, int) or s > 1):
                    dve.wait_ge(S["hR_ready"], s - 1)
                nc.vector.scalar_tensor_tensor(out=hT[k][:, m, 8 * u:8 * u + 8, :], in0=h_ps[u % 2], scalar=tab["scale_up"][:, 0:1],
                                               in1=tab["bias_upT"][:, :].unsqueeze(1).broadcast_to([P, 8, UO]),
                                               op0=ALU.mult, op1=ALU.add).then_inc(S["h_raw"], 1)

            def weigh_down(s, m, u):
                dve.wait_ge(S["z_mm"], before(s, 8 + 4 * m + u, 8) + 1)
                if m == 0 and u == 0:
                    dve.wait_ge(S["free1"], uses(s, 1) + 1)
                c = 32 * m + 8 * u
                nc.vector.tensor_tensor(Bd[:, m, 8 * u:8 * u + 8, :, :],
                                        z_ps[u % 2][:, :, :].rearrange("p n (k c) -> p n k c", k=2),
                                        probd[:, :, c:c + 8].rearrange("p k n -> p n k").unsqueeze(3)
                                        .broadcast_to([P, 8, 2, 32]), ALU.mult).then_inc(S["z_read"], 1)

            def route(s, down):
                r = routing(s, down)
                LINKS = 7

                def link(n, ins):
                    ins.then_inc(S["link"], 1)
                    dve.wait_ge(S["link"], r * LINKS + n)
                dve.wait_ge(S["logits"], r + 1)
                nc.vector.tensor_copy(lg[:, :], misc[1][:, 0:E]).then_inc(S["free1"], 1)
                dve.wait_ge(S["free1"], uses(s, 0 if down else 3) + 1)
                pass_waits(dve, S["dve_passed"])
                link(1, nc.vector.max(out=top[:, :], in_=lg[:, :]))
                nc.vector.tensor_tensor(gap[:, :], top[:, 1:2], top[:, 0:1], ALU.subtract).then_inc(S["pow_in"], 1)
                link(2, nc.vector.max_index(out=topi[:, :], in_max=top[:, :], in_values=lg[:, :]))
                link(3, nc.vector.tensor_copy(chosen[:, :], topi[:, 0:2]))
                if not (isinstance(s, int) and s == -1):
                    dve.wait_ge(S["oh_turned"], r)
                    dve.wait_ge(S["spread_mm"], r)
                for k in range(2):
                    ins = nc.vector.tensor_scalar(onehot[k][:, :], tab["expert_no"][:, :, :].rearrange("p a e -> p (a e)"),
                                                  chosen[:, k:k + 1], None, ALU.is_equal)
                ins.then_inc(S["one_ready"], 1)
                dve.wait_ge(S["pow_done"], r + 1)
                link(4, nc.vector.tensor_scalar(den[:, :], ratio[:, :], 1.0, None, ALU.add))
                link(5, nc.vector.reciprocal(prob[:, 0:1], den[:, :]))
                link(6, nc.vector.tensor_tensor(prob[:, 1:2], ratio[:, :], prob[:, 0:1], ALU.mult))
                link(7, nc.vector.tensor_scalar(spreadp[:, 0, :], tab["spread"][:, :], prob[:, 0:1], None, ALU.mult))
                nc.vector.tensor_scalar(spreadp[:, 1, :], tab["spread"][:, :], prob[:, 1:2], None, ALU.mult)\
                  .then_inc(S["probs_ready"], 1)

            def add(s):
                dve.wait_ge(S["y_mm"], s)
                nc.vector.transpose(ytok.rearrange("n (o p) -> n p o", p=32),
                                    y_ps[:, :, :].rearrange("o n p -> o p n")).then_inc(S["y_read"], 1)
                dve.wait_ge(S["y_read"], s)
                xs = x[:, bass.ds(s * TOKS - TOKS, TOKS), :].rearrange("p t d -> p (t d)")
                nc.vector.scalar_tensor_tensor(out=xs, in0=ytok, scalar=tab["scale_down"][:, 0:1], in1=xs,
                                               op0=ALU.mult, op1=ALU.add).then_inc(S["x_done"], 1)
                dve.wait_ge(S["x_done"], 2 * s - 1)
                nc.vector.tensor_tensor(xs, xs, tab["bias_down"][:, :], ALU.add).then_inc(S["x_done"], 1)

            def turn(s, k):
                up, down, nxt = has(s, 0), has(s, -1), has(s, 1)
                if up:
                    for u in range(4):
                        placed(s, u)
                if down:
                    route(s, True)
                if up:
                    for u in range(4):
                        weigh_up(s, 0, u)
                        placed(s, 4 + u)
                    for u in range(4):
                        bias_up(s, 0, u, k)
                        placed(s, 8 + u)
                if nxt:
                    norm(s)
                if up:
                    for u in range(4):
                        weigh_up(s, 1, u)
                        placed(s, 12 + u)
                for u in range(4):
                    if up:
                        bias_up(s, 1, u, k)
                    if down:
                        placed(s, 16 + u)
                for u in range(4):
                    if down:
                        weigh_down(s, 0, u)
                        placed(s, 20 + u)
                    if nxt:
                        square(s, u)
                if nxt:
                    route(s, False)
                for u in range(4):
                    if down:
                        weigh_down(s, 1, u)
                        placed(s, 24 + u)
                    if nxt:
                        square(s, 4 + u)
                if down:
                    for u in range(4):
                        placed(s, 28 + u)
                    add(s)
            turns(dve, turn)
            dve.wait_ge(S["x_done"], 2 * NS)

        @block.gpsimd
        def _(pool):
            def turn(s, k):
                for down in (True, False):
                    if has(s, -1 if down else 1):
                        r = routing(s, down)
                        pool.wait_ge(S["pow_in"], r + 1)
                        nc.gpsimd.tensor_tensor(ratio[:, :], tab["euler"][:, :], gap[:, :], ALU.pow).then_inc(S["pow_done"], 1)
            turns(pool, turn)

        @block.scalar
        def _(act):
            def copy_logits(s, down):
                act.wait_ge(S["log_mm"], routing(s, down) + 1)
                if not (isinstance(s, int) and s == -1):
                    act.wait_ge(S["logits"], routing(s, down))
                nc.scalar.copy(lgT[:, :], misc[0][:, 0:P]).then_inc(S["free0"], 1)

            def copy_choices(s, down):
                r = routing(s, down)
                act.wait_ge(S["oh_turned"], r + 1)
                turned = misc[0][:, :].bitcast(BF16)[:, 0:2 * P]
                if down:
                    nc.scalar.copy(ohTd[:, :, :], turned.rearrange("e (k n) -> e k n", k=2)).then_inc(S["free0"], 1)
                else:
                    if has(s, 0):
                        act.wait_ge(S["gat_mm"], before(s, 16, 16))
                    for k in range(2):
                        ins = nc.scalar.copy(ohTu[:, :, :, k, :].rearrange("e m h n -> e h m n"),
                                             turned[:, k * P:(k + 1) * P].rearrange("e (h m n) -> e h m n", h=2, m=2))
                    ins.then_inc(S["free0"], 1)
                act.wait_ge(S["spread_mm"], r + 1)
                if down:
                    nc.scalar.copy(probd[:, :, :], misc[1][:, 0:P].rearrange("p (k c) -> p k c", k=2)).then_inc(S["free1"], 1)
                else:
                    if has(s, 0):
                        act.wait_ge(S["z_read"], before(s, 8, 8))
                    nc.scalar.copy(probu[:, :], misc[1][:, 0:HALF]).then_inc(S["free1"], 1)

            def gelu(s, m, u, k):
                act.wait_ge(S["h_raw"], 8 * s + 4 * m + u + 1)
                hs = hT[k][:, m, 8 * u:8 * u + 8, :]
                nc.scalar.activation(hs, hs, ACT.Gelu).then_inc(S["h_ready"], 1)

            def copy_turned(s):
                for b in range(2):
                    act.wait_ge(S["turned_x"], 2 * s + 3 + b)
                    nc.scalar.copy(xnT[:, 4 * b:4 * b + 4, :].rearrange("p t n -> p (t n)"), misc[b][:, :])\
                      .then_inc(S[f"free{b}"], 1)

            def for_router(s, k):
                act.wait_ge(S["h_ready"], 8 * s + 8)
                if has(s, -1):
                    act.wait_ge(S["log_mm"], routing(s, True) + 1)
                for h in range(2):
                    for o in range(2):
                        ins = nc.scalar.copy(
                            hR[64 * o:64 * o + 64, :, 64 * h:64 * h + 64],
                            hT[k][64 * h:64 * h + 64, :, :, 32 * o:32 * o + 32].rearrange("p m n o -> p o (m n)"))
                ins.then_inc(S["hR_ready"], 1)

            def turn(s, k):
                up, down, nxt = has(s, 0), has(s, -1), has(s, 1)
                if down:
                    copy_logits(s, True)
                    copy_choices(s, True)
                if up:
                    for u in range(4):
                        gelu(s, 0, u, k)
                if nxt:
                    copy_turned(s)
                if up:
                    for u in range(4):
                        gelu(s, 1, u, k)
                if nxt:
                    copy_logits(s, False)
                if up:
                    for_router(s, k)
                if nxt:
                    copy_choices(s, False)
            turns(act, turn)


WR = 8
WCH = RUN // WR
WKEYS = 6
WSCALE = D ** -0.5


def window(nc, keep, a, name):
    x, ident = keep["x"], keep["ident"]
    with Stage(nc, name) as st:
        wqkv, wo = st.sb("wqkv", [P, 3, D]), st.sb("wo", [P, D])
        bias = st.sb("bias", [P, D])
        inner = [st.sb(n, [P, 1]) for n in ("has_before", "has_after")]
        count = [st.sb(n, [P, 1]) for n in ("count_first", "count_last")]
        xn = st.sb("xn", [P, WR, D])
        xnT = st.sb("xnT", [P, WR, P])
        haloT = st.sb("haloT", [P, 4, P + 2])
        q = [st.sb(f"q{k}", [P, WR + 2, D]) for k in range(2)]
        kk = [st.sb(f"k{k}", [P, WR + 4, D]) for k in range(2)]
        vv = [st.sb(f"v{k}", [P, WR + 4, D]) for k in range(2)]
        k_end, v_end = st.sb("k_end", [P, 2, D]), st.sb("v_end", [P, 2, D])
        prod = [st.sb(f"prod{o}", [P, WR, D]) for o in range(WKEYS)]
        sc = st.sb("sc", [P, WKEYS, WR * HEADS])
        pair_max, win_max = st.sb("pair_max", [P, 3, WR * HEADS]), st.sb("win_max", [P, 2, WR * HEADS])
        pr = st.sb("pr", [P, 2, 4, WR * HEADS])
        half_sum = st.sb("half_sum", [P, 2, 2, WR * HEADS])
        den = st.sb("den", [P, 2, WR * HEADS])
        weighed = [st.sb(f"weighed{j}", [P, WR, D]) for j in range(3)]
        oT = st.sb("oT", [P, WR, P])
        bank = [st.ps(f"bank{j}", [P, 4, D]) for j in range(4)]
        oT_ps = [st.ps(f"oT{b}", [P, 4, P]) for b in range(2)]
        out_ps = st.ps("out", [P, WR, D])
        names = ("loaded", "zeroed", "masks", "xn_ready", "filled", "moved", "carried", "prod_ready", "reduced", "link",
                 "dif_ready", "exp_done", "masked", "weighed", "accumulated", "oT_moved", "projected", "biased",
                 "added")
        S = {n: st.sem(n) for n in names}
        block = st.block()

        def turns(eng, one):
            one(-1, 1)
            one(0, 0)
            one(1, 1)
            with eng.Fori(0, WCH // 2 - 2) as i:
                one(i * 2 + 2, 0)
                one(i * 2 + 3, 1)
            one(WCH - 2, 0)
            one(WCH - 1, 1)
            one(WCH, 0)

        def first(c):
            return isinstance(c, int) and c == 0

        def last(c):
            return isinstance(c, int) and c == WCH

        def rows(c):
            return (2, WR) if first(c) else (0, 2) if last(c) else (0, WR)

        def fill(c, j):
            return 3 + 8 * c + j

        def link_value(c, n):
            return 8 * c + n

        @block.sync
        def _(sp):
            sp.dma_start(wqkv[:, :, :].rearrange("p a d -> p (a d)"), a["L1_attn_w_qkv"]).then_inc(S["loaded"], 16)
            sp.dma_start(wo[:, :], a["L1_attn_w_out"]).then_inc(S["loaded"], 16)
            sp.dma_start(bias[:, :], a["L1_attn_b_out"].partition_broadcast(P)).then_inc(S["loaded"], 16)

        @block.tensor
        def _(pe):
            def take(c, j, n=None):
                n = fill(c, j) if n is None else n
                if not isinstance(n, int) or n >= 4:
                    pe.wait_ge(S["moved"], n - 3)
                return bank[(3 + j) % 4 if n is None or not isinstance(n, int) else n % 4]

            def halo():
                pe.wait_ge(S["xn_ready"], 1)
                for t in range(4):
                    mm = nc.tensor.transpose(bank[0][:, t, :], xn[:, t, :], ident[:, :])
                mm.then_inc(S["filled"], 1)
                pe.wait_ge(S["loaded"], 48)
                pe.wait_ge(S["zeroed"], 2)
                pe.wait_ge(S["moved"], 1)
                for w in (1, 2):
                    for t in range(4):
                        at = 0 if t < 2 else 2
                        mm = nc.tensor.matmul(bank[w][:, t, :], haloT[:, t, at:at + P], wqkv[:, w, :], start=True, stop=True)
                    mm.then_inc(S["filled"], 1)

            def turn_chunk(c):
                pe.wait_ge(S["xn_ready"], c + 2)
                for b in range(2):
                    into = take(c, b)
                    for t in range(4):
                        mm = nc.tensor.transpose(into[:, t, :], xn[:, 4 * b + t, :], ident[:, :])
                    mm.then_inc(S["filled"], 1)

            def project(c):
                pe.wait_ge(S["moved"], fill(c, 1) + 1)
                for w in range(3):
                    for b in range(2):
                        into = take(c, 2 + 2 * w + b)
                        for t in range(4):
                            mm = nc.tensor.matmul(into[:, t, :], xnT[:, 4 * b + t, :], wqkv[:, w, :], start=True, stop=True)
                        mm.then_inc(S["filled"], 1)

            def accumulate(c):
                t0, t1 = rows(c)
                for o in range(WKEYS):
                    pe.wait_ge(S["weighed"], WKEYS * c + o + 1)
                    if o == 0 and not first(c):
                        pe.wait_ge(S["oT_moved"], 2 * c)
                    for t in range(t0, t1):
                        mm = nc.tensor.matmul(oT_ps[t // 4][:, t % 4, :], weighed[o % 3][:, t, :], ident[:, :],
                                              start=(o == 0 and t in (t0, 4)),
                                              stop=(o == WKEYS - 1 and t in (3, t1 - 1)))
                    mm.then_inc(S["accumulated"], 1)

            def output(c):
                t0, t1 = rows(c)
                pe.wait_ge(S["oT_moved"], 2 * c + 2)
                if not first(c):
                    pe.wait_ge(S["added"], c)
                for t in range(t0, t1):
                    mm = nc.tensor.matmul(out_ps[:, t, :], oT[:, t, :], wo[:, :], start=True, stop=True)
                mm.then_inc(S["projected"], 1)

            def turn(c, k):
                if isinstance(c, int) and c == -1:
                    halo()
                if not isinstance(c, int) or c + 1 < WCH:
                    turn_chunk(c + 1)
                    project(c + 1)
                if not isinstance(c, int) or c >= 0:
                    accumulate(c)
                    output(c)
            turns(pe, turn)

        @block.scalar
        def _(act):
            def move(c, j, out, src=None, n=None):
                n = fill(c, j) if n is None else n
                act.wait_ge(S["filled"], n + 1)
                nc.scalar.copy(out, bank[(3 + j) % 4][:, :, :] if src is None else src).then_inc(S["moved"], 1)

            def halo():
                act.wait_ge(S["zeroed"], 1)
                move(0, 0, haloT[:, :, 1:P + 1], bank[0][:, :, :], 0)
                for n, (ring, end) in enumerate(((kk, k_end), (vv, v_end))):
                    act.wait_ge(S["filled"], n + 2)
                    nc.scalar.copy(ring[0][:, 2:4, :], bank[1 + n][:, 0:2, :])
                    nc.scalar.copy(end[:, :, :], bank[1 + n][:, 2:4, :]).then_inc(S["moved"], 1)

            def carry(c, k):
                if not (isinstance(c, int) and c == 0):
                    act.wait_ge(S["moved"], fill(c - 1, 7) + 1)
                    if not (isinstance(c, int) and c == 1):
                        act.wait_ge(S["prod_ready"], WKEYS * c - WKEYS)
                        act.wait_ge(S["weighed"], WKEYS * c - WKEYS)
                    nc.scalar.copy(q[k][:, 0:2, :], q[1 - k][:, WR:WR + 2, :])
                    nc.scalar.copy(kk[k][:, 0:4, :], kk[1 - k][:, WR:WR + 4, :])
                    nc.scalar.copy(vv[k][:, 0:4, :], vv[1 - k][:, WR:WR + 4, :]).then_inc(S["carried"], 1)

            def move_chunk(c, k):
                for b in range(2):
                    move(c, b, xnT[:, 4 * b:4 * b + 4, :])
                for w, (dst, at) in enumerate(((q, 2), (kk, 4), (vv, 4))):
                    for b in range(2):
                        move(c, 2 + 2 * w + b, dst[k][:, at + 4 * b:at + 4 * b + 4, :])

            def attend(c):
                t0, t1 = rows(c)
                lanes = slice(t0 * HEADS, t1 * HEADS)
                for w in range(2):
                    act.wait_ge(S["dif_ready"], 2 * c + w + 1)
                    nc.scalar.activation(pr[:, w, :, lanes], pr[:, w, :, lanes], ACT.Exp, scale=WSCALE).then_inc(S["exp_done"], 1)
                act.wait_ge(S["accumulated"], WKEYS * c + WKEYS)
                if not first(c):
                    act.wait_ge(S["projected"], c)
                for b in range(2):
                    s0, s1 = max(t0, 4 * b), min(t1, 4 * b + 4)
                    if s1 > s0:
                        nc.scalar.copy(oT[:, s0:s1, :], oT_ps[b][:, s0 - 4 * b:s1 - 4 * b, :]).then_inc(S["oT_moved"], 1)
                    else:
                        act.sem_inc(S["oT_moved"], 1)

            def turn(c, k):
                if isinstance(c, int) and c == -1:
                    halo()
                if not last(c):
                    carry(c + 1, 1 - k)
                if not isinstance(c, int) or c + 1 < WCH:
                    move_chunk(c + 1, 1 - k)
                elif c + 1 == WCH:
                    nc.scalar.copy(kk[1 - k][:, 4:6, :], k_end[:, :, :])
                    nc.scalar.copy(vv[1 - k][:, 4:6, :], v_end[:, :, :]).then_inc(S["moved"], 1)
                if not isinstance(c, int) or c >= 0:
                    attend(c)
            turns(act, turn)

        @block.gpsimd
        def _(pool):
            nc.gpsimd.memset(haloT[:, :, 0:1], 0.0).then_inc(S["zeroed"], 1)
            nc.gpsimd.memset(haloT[:, :, P + 1:P + 2], 0.0).then_inc(S["zeroed"], 1)

            def turn(c, k):
                if isinstance(c, int) and c == -1:
                    return
                t0, t1 = rows(c)
                pairs = (t1 - t0) // 2
                if last(c):
                    pool.wait_ge(S["moved"], fill(c, 0) + 1)
                else:
                    pool.wait_ge(S["moved"], fill(c, 5) + 1)
                if not first(c):
                    pool.wait_ge(S["carried"], c)
                for o in range(WKEYS):
                    if not first(c):
                        pool.wait_ge(S["reduced"], WKEYS * c - WKEYS + o + 1)
                    keys = kk[k][:, t0 + o:t0 + o + 2 * pairs - 1:2, :].unsqueeze(2).broadcast_to([P, pairs, 2, D])
                    nc.gpsimd.tensor_tensor(prod[o][:, t0:t1, :].rearrange("p (m i) d -> p m i d", i=2),
                                            q[k][:, t0:t1, :].rearrange("p (m i) d -> p m i d", i=2), keys, ALU.mult)\
                      .then_inc(S["prod_ready"], 1)
            turns(pool, turn)

        @block.vector
        def _(dve):
            def edges():
                for n, at in enumerate((0, 7)):
                    nc.vector.tensor_reduce(inner[n][:, :], ident[:, at:P:8], AX.X, ALU.add).then_inc(S["masks"], 1)
                    dve.wait_ge(S["masks"], 3 * n + 1)
                    nc.vector.tensor_scalar(count[n][:, :], inner[n][:, :], -1.0, 2.0, ALU.mult, ALU.add).then_inc(S["masks"], 1)
                    nc.vector.tensor_scalar(inner[n][:, :], inner[n][:, :], -1.0, 1.0, ALU.mult, ALU.add).then_inc(S["masks"], 1)
                    dve.wait_ge(S["masks"], 3 * n + 3)

            def norm(c):
                if not (isinstance(c, int) and c == 0):
                    dve.wait_ge(S["filled"], fill(c - 1, 1) + 1)
                else:
                    dve.wait_ge(S["filled"], 1)
                for t in range(WR):
                    ins = normalize(nc, keep, xn[:, t, :], c * WR + t)
                ins.then_inc(S["xn_ready"], 1)

            def scores(c):
                t0, t1 = rows(c)
                for o in range(WKEYS):
                    dve.wait_ge(S["prod_ready"], WKEYS * c + o + 1)
                    nc.vector.tensor_reduce(sc[:, o, t0 * HEADS:t1 * HEADS],
                                            prod[o][:, t0:t1, :].rearrange("p t (h e) -> p (t h) e", e=HD), AX.X, ALU.add)\
                      .then_inc(S["reduced"], 1)

            def probabilities(c, between):
                t0, t1 = rows(c)
                at, n = slice(t0 * HEADS, t1 * HEADS), (t1 - t0) * HEADS

                def link(v, ins):
                    ins.then_inc(S["link"], 1)
                    dve.wait_ge(S["link"], link_value(c, v))
                dve.wait_ge(S["reduced"], WKEYS * c + WKEYS)
                link(1, nc.vector.tensor_tensor(pair_max[:, :, at], sc[:, 0:WKEYS:2, at], sc[:, 1:WKEYS:2, at], ALU.max))
                link(2, nc.vector.tensor_tensor(win_max[:, :, at], pair_max[:, 0:2, at], pair_max[:, 1:3, at], ALU.max))
                for w in range(2):
                    nc.vector.tensor_tensor(pr[:, w, :, at], sc[:, 2 * w:2 * w + 4, at],
                                            win_max[:, w, at].unsqueeze(1).broadcast_to([P, 4, n]), ALU.subtract)\
                      .then_inc(S["dif_ready"], 1)
                between()
                dve.wait_ge(S["exp_done"], 2 * c + 2)
                link(3, nc.vector.tensor_tensor(half_sum[:, :, :, at], pr[:, :, 0:2, at], pr[:, :, 2:4, at], ALU.add))
                link(4, nc.vector.tensor_tensor(den[:, :, at], half_sum[:, :, 0, at], half_sum[:, :, 1, at], ALU.add))
                link(5, nc.vector.reciprocal(den[:, :, at], den[:, :, at]))
                if first(c) or last(c):
                    w, edge = (0, slice(2 * HEADS, 4 * HEADS)) if first(c) else (1, slice(0, 2 * HEADS))
                    nc.vector.tensor_scalar(den[:, w, edge], den[:, w, edge], inner[w][:, 0:1], None, ALU.mult)\
                      .then_inc(S["masked"], 1)
                    dve.wait_ge(S["masked"], w + 1)
                for w in range(2):
                    link(6 + w, nc.vector.tensor_tensor(pr[:, w, :, at], pr[:, w, :, at],
                                                        den[:, w, at].unsqueeze(1).broadcast_to([P, 4, n]), ALU.mult))
                link(8, nc.vector.tensor_tensor(pr[:, 0, 2:4, at], pr[:, 0, 2:4, at], pr[:, 1, 0:2, at], ALU.add))

            def weigh(c, k):
                t0, t1 = rows(c)
                pairs = (t1 - t0) // 2
                if not last(c):
                    dve.wait_ge(S["moved"], fill(c, 7) + 1)
                for o in range(WKEYS):
                    if o >= 3 or not first(c):
                        dve.wait_ge(S["accumulated"], WKEYS * c + o - 2)
                    w, m = (0, o) if o < 4 else (1, o - 2)
                    for i in range(2):
                        values = vv[k][:, t0 + o:t0 + o + 2 * pairs - 1:2, :].rearrange("p m (h e) -> p m h e", e=HD)
                        weights = pr[:, w, m, :].rearrange("p (t h) -> p t h", h=HEADS)[:, t0 + i:t1 + i - 1:2, :]\
                            .unsqueeze(3).broadcast_to([P, pairs, HEADS, HD])
                        ins = nc.vector.tensor_tensor(weighed[o % 3][:, t0 + i:t1 + i - 1:2, :]
                                                      .rearrange("p m (h e) -> p m h e", e=HD), values, weights, ALU.mult)
                    ins.then_inc(S["weighed"], 1)

            def add_bias(c):
                t0, t1 = rows(c)
                parts = [(t0, t1, 2.0)]
                if first(c):
                    parts = [(2, 4, count[0][:, 0:1]), (4, WR, 2.0)]
                if last(c):
                    parts = [(0, 2, count[1][:, 0:1])]
                for s0, s1, times in parts:
                    xs = x[:, bass.ds(c * WR - 2 + s0, s1 - s0), :]
                    ins = nc.vector.scalar_tensor_tensor(out=xs, in0=bias[:, :].unsqueeze(1).broadcast_to([P, s1 - s0, D]),
                                                         scalar=times, in1=xs, op0=ALU.mult, op1=ALU.add)
                ins.then_inc(S["biased"], 1)

            def add(c):
                t0, t1 = rows(c)
                dve.wait_ge(S["biased"], c + 1)
                dve.wait_ge(S["projected"], c + 1)
                xs = x[:, bass.ds(c * WR - 2 + t0, t1 - t0), :]
                nc.vector.tensor_tensor(xs, xs, out_ps[:, t0:t1, :], ALU.add).then_inc(S["added"], 1)

            edges()
            for t, r in enumerate((RUN - 2, RUN - 1, 0, 1)):
                ins = normalize(nc, keep, xn[:, t, :], r)
            ins.then_inc(S["xn_ready"], 1)
            dve.wait_ge(S["loaded"], 48)

            def turn(c, k):
                if not isinstance(c, int) or c + 1 < WCH:
                    norm(c + 1)
                if not isinstance(c, int) or c >= 0:
                    scores(c)

                    def between():
                        add_bias(c)
                        if not first(c):
                            add(c - 1)
                    probabilities(c, between)
                    weigh(c, k)
            turns(dve, turn)
            add(WCH)
            dve.wait_ge(S["added"], WCH + 1)


def store(nc, keep, out):
    with Stage(nc, "store") as st:
        stored = st.sem("stored")
        block = st.block()

        @block.sync
        def _(sp):
            sp.dma_start(out.rearrange("b (g r) d -> (b g) r d", r=RUN), keep["x"][:, :, :]).then_inc(stored, 16)
            sp.wait_ge(stored, 16)


def macaron(nc, a, out, stages=range(6)):
    def allocate(ctx, shapes):
        return {n: ctx.enter_context(nc.sbuf_tensor(n, shape, dt)) for n, (shape, dt) in shapes.items()}

    Stage.used = []
    with ExitStack() as ctx:
        keep = allocate(ctx, {
            "x": ([P, RUN, D], F32), "ident": ([P, P], F32), "identb": ([P, P], BF16),
            "half_neg": ([P, RUN], F32), "mean": ([P, RUN], F32), "rstd": ([P, RUN], F32)})
        with ExitStack() as first:
            keep.update(allocate(first, {"gateT": ([P, HB, P], F32), "upT": ([P, HB, P], F32),
                                         "downT": ([P, HB, D], F32)}))
            setup(nc, keep, a)
            if 0 in stages:
                layer_norm_stats(nc, keep, "ln0")
                ffn(nc, keep, "ffn0")
            if 1 in stages:
                layer_norm_stats(nc, keep, "ln1")
                mla(nc, keep, a, "mla")
            if 2 in stages:
                layer_norm_stats(nc, keep, "ln2")
                ffn(nc, keep, "ffn1")
        tab = allocate(ctx, {
            **{w: ([P, TAB], BF16) for w in MOE_TABLES}, **{w + "3": ([P, TAB], BF16) for w in MOE_TABLES},
            "router_upT": ([P, TOKS, E], F32), "router_downT": ([P, UI, E], F32), "bias_upT": ([P, UO], F32),
            "bias_down": ([P, TOKS * D], F32), "scale_up": ([P, 1], F32), "scale_down": ([P, 1], F32),
            "expert_no": ([P, 2, E], F32), "spread": ([P, HALF], F32), "pick_half": ([P, P], F32),
            "pick0": ([P, P], F32), "pick1": ([P, P], F32), "euler": ([P, 1], F32)})
        if 3 in stages or 5 in stages:
            moe_tables(nc, keep, a, tab, "tables")
        if 3 in stages:
            layer_norm_stats(nc, keep, "ln3")
            moe(nc, keep, tab, "moe0")
        if 4 in stages:
            layer_norm_stats(nc, keep, "ln4")
            window(nc, keep, a, "window")
        if 5 in stages:
            layer_norm_stats(nc, keep, "ln5")
            moe(nc, keep, tab, "moe1")
        store(nc, keep, out)


_INS = ['L0_attn_x', 'L0_attn_Wq', 'L0_attn_bq', 'L0_attn_Wkd', 'L0_attn_bkd', 'L0_attn_Wku', 'L0_attn_bku',
        'L0_attn_Wo', 'L0_attn_bo', 'L0_ffn_w_gate', 'L0_ffn_w_up', 'L0_ffn_w_down', 'L1_attn_w_qkv',
        'L1_attn_w_out', 'L1_attn_b_out', 'L1_ffn_W_up', 'L1_ffn_A_up', 'L1_ffn_B_up', 'L1_ffn_scale_up',
        'L1_ffn_bias_up', 'L1_ffn_W_down', 'L1_ffn_A_down', 'L1_ffn_B_down', 'L1_ffn_scale_down',
        'L1_ffn_bias_down']


def kernel(**inputs):
    import concourse.bacc as bacc
    from concourse.bass_utils import run_bass_kernel_spmd

    nc = bacc.Bacc("TRN2", target_bir_lowering=False, num_devices=1)
    arrays, args = {}, {}
    for name in _INS:
        v = np.ascontiguousarray(inputs[name])
        arrays[f"in_{name}"] = v
        args[name] = nc.dram_tensor(f"in_{name}", v.shape, mybir.dt.from_np(v.dtype), kind="ExternalInput").ap()
    out = nc.dram_tensor("out_x", (BATCH, SEQ, D), F32, kind="ExternalOutput").ap()
    macaron(nc, args, out)
    r = run_bass_kernel_spmd(nc, [arrays], core_ids=[0])
    return r.results[0]["out_x"]
```

```python
from contextlib import ExitStack

import numpy as np
import concourse.bass as bass
from concourse import mybir

F32 = mybir.dt.float32
BF16 = mybir.dt.bfloat16
I32 = mybir.dt.int32
U32 = mybir.dt.uint32
ALU = mybir.AluOpType
ACT = mybir.ActivationFunctionType
AX = mybir.AxisListType

P = 128
D = 128
RUN = 64
TOK = P * RUN
CH = 4
NCH = RUN // CH
HID = 384
HB = HID // P
EPS = 1e-5
BATCH, SEQ, HEADS, HD = 16, 512, 16, 8
LAT = 32


class Stage:
    used = []

    def __init__(self, nc, name):
        self.nc, self.name, self.stack, self.sems = nc, name, ExitStack(), []

    def __enter__(self):
        return self

    def __exit__(self, *e):
        Stage.used = self.sems
        return self.stack.__exit__(*e)

    def sb(self, name, shape, dt=F32):
        return self.stack.enter_context(self.nc.sbuf_tensor(f"{self.name}_{name}", shape, dt))

    def ps(self, name, shape, dt=F32):
        return self.stack.enter_context(self.nc.psum_tensor(f"{self.name}_{name}", shape, dt))

    def sem(self, name):
        self.sems.append(self.nc.alloc_semaphore(f"{self.name}_{name}"))
        return self.sems[-1]

    def block(self):
        if Stage.used:
            self.nc.clear_and_free_semaphores(Stage.used)
        return self.stack.enter_context(self.nc.Block())


def chained(eng, sem):
    n = [0]

    def link(ins):
        n[0] += 1
        ins.then_inc(sem, 1)
        eng.wait_ge(sem, n[0])
    return link


def pass_waits(eng, sem):
    eng.sem_inc(sem, 1)


def setup(nc, keep, a):
    with Stage(nc, "setup") as st:
        raw = {n: st.sb(f"raw_{n}", [P, HB * D], I32) for n in ("gate", "up", "down")}
        deq = {n: st.sb(f"deq_{n}", [P, HB, D]) for n in ("gate", "up", "down")}
        turned_ps = [st.ps(f"turned{n}", [P, HB, P]) for n in range(3)]
        loaded_x, loaded_w, zeroed, made = (st.sem(n) for n in ("loaded_x", "loaded_w", "zeroed", "made"))
        dequantized, turned, kept = (st.sem(n) for n in ("dequantized", "turned", "kept"))
        block = st.block()

        @block.sync
        def _(sp):
            sp.dma_start(keep["x"][:, :, :], a["L0_attn_x"].rearrange("b (g r) d -> (b g) r d", r=RUN))\
              .then_inc(loaded_x, 16)
            sp.wait_ge(loaded_x, 16)

        @block.scalar
        def _(act):
            act.dma_start(raw["gate"][:, :].rearrange("p (h d) -> p h d", h=HB),
                          a["L0_ffn_w_gate"].rearrange("(h p) d -> p h d", p=P)).then_inc(loaded_w, 16)
            act.dma_start(raw["up"][:, :].rearrange("p (h d) -> p h d", h=HB),
                          a["L0_ffn_w_up"].rearrange("(h p) d -> p h d", p=P)).then_inc(loaded_w, 16)
            act.dma_start(raw["down"][:, :], a["L0_ffn_w_down"]).then_inc(loaded_w, 16)
            for n, w in enumerate(("gateT", "upT", "downT")):
                act.wait_ge(turned, n + 1)
                nc.scalar.copy(keep[w][:, :, :], turned_ps[n][:, :, :]).then_inc(kept, 1)
            act.wait_ge(kept, 3)

        @block.gpsimd
        def _(pool):
            nc.gpsimd.memset(keep["ident"][:, :], 0.0).then_inc(zeroed, 1)
            nc.gpsimd.memset(keep["half_neg"][:, :], -0.5).then_inc(zeroed, 1)
            pool.wait_ge(zeroed, 2)
            nc.gpsimd.affine_select(out=keep["ident"][:, :], in_=keep["ident"][:, :],
                                    compare_op=ALU.not_equal, fill=1.0, base=0, pattern=[[-1, P]],
                                    channel_multiplier=1).then_inc(made, 1)

        @block.vector
        def _(dve):
            dve.wait_ge(loaded_w, 48)
            for n in ("gate", "up", "down"):
                nc.vector.tensor_scalar(deq[n][:, :, :].rearrange("p h d -> p (h d)"), raw[n][:, :],
                                        1.0 / 127.0, None, ALU.mult).then_inc(dequantized, 1)
            dve.wait_ge(made, 1)
            nc.vector.tensor_copy(keep["identb"][:, :], keep["ident"][:, :]).then_inc(made, 1)
            dve.wait_ge(made, 2)

        @block.tensor
        def _(pe):
            pe.wait_ge(made, 1)
            for n, w in enumerate(("gate", "up", "down")):
                pe.wait_ge(dequantized, n + 1)
                for h in range(HB):
                    mm = nc.tensor.transpose(turned_ps[n][:, h, :], deq[w][:, h, :], keep["ident"][:, :])
                mm.then_inc(turned, 1)


def token_stats(nc, keep, r):
    return nc.vector.bn_stats(keep["stats"][:, bass.ds(r, 1), :].rearrange("p a b -> p (a b)"),
                              keep["x"][:, bass.ds(r, 1), :].rearrange("p a b -> p (a b)"))


def layer_norm_stats(nc, keep, name, counted):
    stats, mean, rstd = keep["stats"], keep["mean"], keep["rstd"]
    with Stage(nc, name) as st:
        diff, var = st.sb("diff", [P, RUN]), st.sb("var", [P, RUN])
        summed, link_sem, var_ready, rstd_ready = (st.sem(n) for n in ("summed", "link", "var_ready", "rstd_ready"))
        block = st.block()

        @block.vector
        def _(dve):
            if not counted:
                with dve.Fori(0, NCH) as c:
                    for t in range(CH):
                        ins = token_stats(nc, keep, c * CH + t)
                    ins.then_inc(summed, 1)
                dve.wait_ge(summed, NCH)
            link = chained(dve, link_sem)
            even, odd = stats[:, :, 1], stats[:, :, 4]
            link(nc.vector.tensor_tensor(mean[:, :], even, odd, ALU.add))
            link(nc.vector.tensor_tensor(diff[:, :], even, odd, ALU.subtract))
            link(nc.vector.tensor_tensor(var[:, :], stats[:, :, 2], stats[:, :, 5], ALU.add))
            link(nc.vector.tensor_scalar(mean[:, :], mean[:, :], 0.5, None, ALU.mult))
            link(nc.vector.tensor_scalar(diff[:, :], diff[:, :], 0.5, None, ALU.mult))
            link(nc.vector.tensor_tensor(diff[:, :], diff[:, :], diff[:, :], ALU.mult))
            link(nc.vector.tensor_scalar(var[:, :], var[:, :], 1.0 / D, EPS, ALU.mult, ALU.add))
            nc.vector.tensor_tensor(var[:, :], var[:, :], diff[:, :], ALU.add).then_inc(var_ready, 1)

        @block.gpsimd
        def _(pool):
            pool.wait_ge(var_ready, 1)
            nc.gpsimd.tensor_tensor(rstd[:, :], var[:, :], keep["half_neg"][:, :], ALU.pow).then_inc(rstd_ready, 1)
            pool.wait_ge(rstd_ready, 1)


def normalize(nc, keep, out, r):
    return nc.vector.tensor_scalar(out, keep["x"][:, bass.ds(r, 1), :].rearrange("p a b -> p (a b)"),
                                   keep["mean"][:, bass.ds(r, 1)], keep["rstd"][:, bass.ds(r, 1)],
                                   ALU.subtract, ALU.mult)


def split_tables(nc, st, a, tab):
    raw = [st.sb(f"raw{k}", [P, TAB]) for k in range(2)]
    left, mid = st.sb("rest", [P, TAB]), st.sb("second", [P, TAB], BF16)
    loaded = [st.sem(f"loaded{k}") for k in range(2)]
    link_sem, split_done = st.sem("link"), st.sem("split_done")

    def load(sp):
        for n, w in enumerate(MOE_TABLES):
            if n >= 2:
                sp.wait_ge(split_done, n - 1)
            for h in range(2):
                sp.dma_start(raw[n % 2][h * HALF:(h + 1) * HALF, :],
                             a["L1_ffn_" + w].rearrange("e o i -> e (o i)")).then_inc(loaded[n % 2], 16)

    def split(pool):
        link = chained(pool, link_sem)
        for n, w in enumerate(MOE_TABLES):
            pool.wait_ge(loaded[n % 2], 32 * (n // 2 + 1))
            r = raw[n % 2]
            two, third = tab[w], tab[w + "3"]
            link(nc.gpsimd.tensor_copy(two[:, :], r[:, :]))
            link(nc.gpsimd.tensor_tensor(left[:, :], r[:, :], two[:, :], ALU.subtract))
            link(nc.gpsimd.tensor_copy(mid[:, :], left[:, :]))
            link(nc.gpsimd.tensor_copy(two[HALF:P, :], mid[HALF:P, :]))
            link(nc.gpsimd.tensor_tensor(left[0:HALF, :], left[0:HALF, :], mid[0:HALF, :], ALU.subtract))
            link(nc.gpsimd.memset(third[HALF:P, :], 0.0))
            link(nc.gpsimd.tensor_copy(third[0:HALF, :], left[0:HALF, :]))
            pool.sem_inc(split_done, 1)
    return load, split


def ffn(nc, keep, name, a=None, tab=None):
    x, ident = keep["x"], keep["ident"]
    with Stage(nc, name) as st:
        xn = [st.sb(f"xn{k}", [P, CH, D]) for k in range(2)]
        xnT = [st.sb(f"xnT{k}", [P, CH * P]) for k in range(2)]
        silu = [st.sb(f"silu{k}", [P, CH * P]) for k in range(HB)]
        hT = [st.sb(f"hT{k}", [P, HB, CH * P]) for k in range(2)]
        turn_ps, down_ps = st.ps("turn", [P, CH, P]), st.ps("downp", [P, CH, D])
        gate_ps = [st.ps(f"gate{k}", [P, CH * P]) for k in range(HB)]
        up_ps = [st.ps(f"up{k}", [P, CH * P]) for k in range(HB)]
        xn_ready, turned, xnT_ready, gated = (st.sem(n) for n in ("xn_ready", "turned", "xnT_ready", "gated"))
        silu_ready, h_ready, down_ready, added = (st.sem(n) for n in ("silu_ready", "h_ready", "down_ready", "added"))
        load, split = split_tables(nc, st, a, tab) if tab else (None, None)
        block = st.block()

        if tab:
            @block.sync
            def _(sp):
                load(sp)

            @block.gpsimd
            def _(pool):
                split(pool)

        @block.vector
        def _(dve):
            def norm(c, k, ring=True):
                if ring:
                    dve.wait_ge(turned, c - 1)
                for t in range(CH):
                    ins = normalize(nc, keep, xn[k][:, t, :], c * CH + t)
                ins.then_inc(xn_ready, 1)

            def hidden(c, k, ring=True):
                if ring:
                    dve.wait_ge(down_ready, c - 1)
                for h in range(HB):
                    dve.wait_ge(silu_ready, c * HB + h + 1)
                    nc.vector.tensor_tensor(hT[k][:, h, :], silu[h][:, :], up_ps[h][:, :], ALU.mult)\
                      .then_inc(h_ready, 1)

            def add(c):
                dve.wait_ge(down_ready, c + 1)
                xs = x[:, bass.ds(c * CH, CH), :]
                nc.vector.scalar_tensor_tensor(out=xs, in0=down_ps[:, :, :], scalar=0.5, in1=xs,
                                               op0=ALU.mult, op1=ALU.add).then_inc(added, 1)

            def stats(c):
                for t in range(CH):
                    token_stats(nc, keep, c * CH + t)

            norm(0, 0, False)
            norm(1, 1, False)
            norm(2, 0)
            hidden(0, 0, False)
            norm(3, 1)
            hidden(1, 1, False)
            add(0)
            with dve.Fori(1, NCH // 2 - 1) as j:
                for k in range(2):
                    dve.wait_ge(added, 2 * j + k - 1)
                    norm(2 * j + k + 2, k)
                    stats(2 * j + k - 2)
                    hidden(2 * j + k, k)
                    add(2 * j + k - 1)
            for c in (NCH - 2, NCH - 1):
                dve.wait_ge(added, c - 1)
                stats(c - 2)
                hidden(c, c % 2)
                add(c - 1)
            add(NCH - 1)
            for c in (NCH - 2, NCH - 1):
                dve.wait_ge(added, c + 1)
                stats(c)
            dve.wait_ge(added, NCH)

        @block.tensor
        def _(pe):
            def turn(c, k, ring=True):
                pe.wait_ge(xn_ready, c + 1)
                if ring:
                    pe.wait_ge(xnT_ready, c)
                for t in range(CH):
                    mm = nc.tensor.transpose(turn_ps[:, t, :], xn[k][:, t, :], ident[:, :])
                mm.then_inc(turned, 1)

            def gate_up(c, k, ring=True):
                pe.wait_ge(xnT_ready, c + 1)
                for h in range(HB):
                    if ring:
                        pe.wait_ge(h_ready, (c - 1) * HB + h + 1)
                    nc.tensor.matmul(gate_ps[h][:, :], keep["gateT"][:, h, :], xnT[k][:, :], start=True, stop=True)
                    nc.tensor.matmul(up_ps[h][:, :], keep["upT"][:, h, :], xnT[k][:, :], start=True, stop=True)\
                      .then_inc(gated, 1)

            def down(c, k, ring=True):
                pe.wait_ge(h_ready, (c + 1) * HB)
                if ring:
                    pe.wait_ge(added, c)
                for t in range(CH):
                    for h in range(HB):
                        mm = nc.tensor.matmul(down_ps[:, t, :], hT[k][:, h, t * P:(t + 1) * P],
                                              keep["downT"][:, h, :], start=(h == 0), stop=(h == HB - 1))
                mm.then_inc(down_ready, 1)

            turn(0, 0, False)
            turn(1, 1)
            gate_up(0, 0, False)
            turn(2, 0)
            gate_up(1, 1)
            down(0, 0, False)
            with pe.Fori(1, NCH // 2 - 1) as j:
                turn(2 * j + 1, 1)
                gate_up(2 * j, 0)
                down(2 * j - 1, 1)
                turn(2 * j + 2, 0)
                gate_up(2 * j + 1, 1)
                down(2 * j, 0)
            turn(NCH - 1, 1)
            gate_up(NCH - 2, 0)
            down(NCH - 3, 1)
            gate_up(NCH - 1, 1)
            down(NCH - 2, 0)
            down(NCH - 1, 1)

        @block.scalar
        def _(act):
            def copy_turned(c, k, ring=True):
                act.wait_ge(turned, c + 1)
                if ring:
                    act.wait_ge(gated, (c - 1) * HB)
                nc.scalar.copy(xnT[k][:, :], turn_ps[:, :, :].rearrange("p a b -> p (a b)")).then_inc(xnT_ready, 1)

            def gates(c, ring=True):
                for h in range(HB):
                    act.wait_ge(gated, c * HB + h + 1)
                    if ring:
                        act.wait_ge(h_ready, (c - 1) * HB + h + 1)
                    nc.scalar.activation(silu[h][:, :], gate_ps[h][:, :], ACT.Silu).then_inc(silu_ready, 1)

            copy_turned(0, 0, False)
            copy_turned(1, 1, False)
            gates(0, False)
            copy_turned(2, 0)
            gates(1)
            with act.Fori(1, NCH // 2 - 1) as j:
                copy_turned(2 * j + 1, 1)
                gates(2 * j)
                copy_turned(2 * j + 2, 0)
                gates(2 * j + 1)
            copy_turned(NCH - 1, 1)
            gates(NCH - 2)
            gates(NCH - 1)


NEG = -1e30
NPAIR = HEADS // 2
SLOTS = 6
Q_SLOTS = ((0, 3, 0, True), (3, 2, 1, True), (5, 1, 2, False))
K_SLOTS = ((0, 3, 0, False), (3, 2, 0, False), (5, 1, 0, False))
ROWS = 16 * SLOTS
NG = 4
NSTEP = BATCH * NG
NKB = SEQ // P


def mla_project(nc, keep, a, st0, name):
    x, ident = keep["x"], keep["ident"]
    xnT, q_dram, k_dram, v_dram = st0
    with Stage(nc, name + "t") as st:
        xn = [st.sb(f"xn{k}", [P, CH, D]) for k in range(2)]
        turn_ps = [st.ps(f"turn{k}", [P, CH, P]) for k in range(2)]
        xn_ready, turned, copied = (st.sem(n) for n in ("xn_ready", "turned", "copied"))
        xnT_runs = xnT[:, :].rearrange("d (p r) -> d p r", r=RUN)
        block = st.block()

        @block.vector
        def _(dve):
            def norm(c, k, ring=True):
                if ring:
                    dve.wait_ge(turned, c - 1)
                for t in range(CH):
                    ins = normalize(nc, keep, xn[k][:, t, :], c * CH + t)
                ins.then_inc(xn_ready, 1)
            norm(0, 0, False)
            norm(1, 1, False)
            with dve.Fori(1, NCH // 2) as j:
                norm(2 * j, 0)
                norm(2 * j + 1, 1)

        @block.tensor
        def _(pe):
            def turn(c, k, ring=True):
                pe.wait_ge(xn_ready, c + 1)
                if ring:
                    pe.wait_ge(copied, c - 1)
                for t in range(CH):
                    mm = nc.tensor.transpose(turn_ps[k][:, t, :], xn[k][:, t, :], ident[:, :])
                mm.then_inc(turned, 1)
            turn(0, 0, False)
            turn(1, 1, False)
            with pe.Fori(1, NCH // 2) as j:
                turn(2 * j, 0)
                turn(2 * j + 1, 1)

        @block.scalar
        def _(act):
            with act.Fori(0, NCH // 2) as j:
                for k in range(2):
                    c = 2 * j + k
                    act.wait_ge(turned, c + 1)
                    nc.scalar.copy(xnT_runs[:, :, bass.ds(c * CH, CH)].rearrange("d p t -> d t p"),
                                   turn_ps[k][:, :, :]).then_inc(copied, 1)
            act.wait_ge(copied, NCH)

    with Stage(nc, name + "p") as st:
        wq, wkd, wku = st.sb("wq", [P, D]), st.sb("wkd", [P, 2 * LAT]), st.sb("wku", [P, 2 * D])
        bq, bkd = st.sb("bq", [P, 1]), st.sb("bkd", [LAT, 2])
        act_half = [st.sb(f"act_half{h}", [LAT, SEQ]) for h in range(2)]
        lat = [st.sb(f"lat{k}", [P, SEQ]) for k in range(2)]
        whole = [[st.sb(f"{n}whole{k}", [P, SEQ]) for k in range(2)] for n in "qk"]
        rest1 = [[st.sb(f"{n}rest1{k}", [P, SEQ]) for k in range(2)] for n in "qk"]
        rest2 = [[st.sb(f"{n}rest2{k}", [P, SEQ]) for k in range(2)] for n in "qk"]
        part = [[st.sb(f"{n}part{k}", [P, 3, SEQ], BF16) for k in range(2)] for n in "qk"]
        v_sb = [st.sb(f"v{k}", [P, NKB, D]) for k in range(2)]
        lat_ps = [st.ps(f"latp{h}", [P, SEQ]) for h in range(2)]
        q_ps, k_ps, v_ps = (st.ps(n, [P, SEQ]) for n in ("qp", "kp", "vp"))
        wloaded, cleared, scaled = (st.sem(n) for n in ("wloaded", "cleared", "scaled"))
        lat_mm, gelu, lat_ready, q_mm, k_mm, v_mm = (st.sem(n) for n in ("lat_mm", "gelu", "lat_ready", "q_mm", "k_mm", "v_mm"))
        whole_ready, part1, left1, part2, left2, part3 = (st.sem(n) for n in ("whole_ready", "part1", "left1", "part2", "left2", "part3"))
        v_ready = st.sem("v_ready")
        parts_stored, v_stored = [st.sem(f"parts_stored{k}") for k in range(2)], [st.sem(f"v_stored{k}") for k in range(2)]
        block = st.block()
        NST = (len(Q_SLOTS) + len(K_SLOTS)) * 16

        def batches(eng, one, n=BATCH // 2):
            one(0, 0, True)
            one(1, 1, True)
            with eng.Fori(1, n) as j:
                one(2 * j, 0, False)
                one(2 * j + 1, 1, False)

        @block.sync
        def _(sp):
            sp.wait_ge(cleared, 3)
            sp.dma_start(wq[:, :], a["L0_attn_Wq"]).then_inc(wloaded, 16)
            sp.dma_start(wkd[:, :], a["L0_attn_Wkd"]).then_inc(wloaded, 16)
            sp.dma_start(wku[0:LAT, :], a["L0_attn_Wku"]).then_inc(wloaded, 16)
            sp.dma_start(wku[LAT:LAT + 1, :], a["L0_attn_bku"].rearrange("(a n) -> a n", a=1)).then_inc(wloaded, 16)
            sp.dma_start(bq[:, :], a["L0_attn_bq"].rearrange("(p a) -> p a", a=1)).then_inc(wloaded, 16)
            sp.dma_start(bkd[:, :], a["L0_attn_bkd"].rearrange("(h p) -> p h", p=LAT),
                         allow_slow_non_contiguous=True).then_inc(wloaded, 16)

            def store(b, k, first):
                for n, (dram, order) in enumerate(((q_dram, Q_SLOTS), (k_dram, K_SLOTS))):
                    sp.wait_ge(part3, 2 * b + n + 1)
                    for s0, slots, p0, repeated in order:
                        src = part[n][k][:, p0:p0 + 1, :].broadcast_to([P, slots, SEQ]) if repeated \
                            else part[n][k][:, p0:p0 + slots, :]
                        sp.dma_start(dram[s0:s0 + slots, :, bass.ds(b * SEQ, SEQ)].rearrange("s r t -> r s t"), src)\
                          .then_inc(parts_stored[k], 16)
                sp.wait_ge(v_ready, b + 1)
                sp.dma_start(v_dram[:, bass.ds(b * NKB, NKB), :], v_sb[k][:, :, :]).then_inc(v_stored[k], 16)
            batches(sp, store)
            for k in range(2):
                sp.wait_ge(parts_stored[k], BATCH // 2 * NST)
                sp.wait_ge(v_stored[k], BATCH // 2 * 16)

        @block.gpsimd
        def _(pool):
            nc.gpsimd.memset(wku[:, :], 0.0).then_inc(cleared, 1)
            for k in range(2):
                nc.gpsimd.memset(lat[k][:, :], 0.0).then_inc(scaled, 1)
            pool.wait_ge(scaled, 2)
            for k in range(2):
                nc.gpsimd.memset(lat[k][LAT:LAT + 1, :], 1.0).then_inc(cleared, 1)

            def split(b, k, first):
                for n in range(2):
                    pool.wait_ge(part1, 2 * b + n + 1)
                    if not first:
                        pool.wait_ge(part3, 2 * (b - 2) + n + 1)
                    nc.gpsimd.tensor_tensor(rest1[n][k][:, :], whole[n][k][:, :], part[n][k][:, 0, :],
                                            ALU.subtract).then_inc(left1, 1)
                for n in range(2):
                    pool.wait_ge(part2, 2 * b + n + 1)
                    nc.gpsimd.tensor_tensor(rest2[n][k][:, :], rest1[n][k][:, :], part[n][k][:, 1, :],
                                            ALU.subtract).then_inc(left2, 1)
            batches(pool, split)

        @block.scalar
        def _(act):
            def evacuate(b, k, first):
                act.wait_ge(lat_mm, b + 1)
                if not first or k:
                    act.wait_ge(lat_ready, b)
                for h in range(2):
                    nc.scalar.activation(act_half[h][:, :], lat_ps[h][0:LAT, :], ACT.Gelu, bias=bkd[:, h:h + 1])\
                      .then_inc(gelu, 1)
                for n, (ps, mm) in enumerate(((q_ps, q_mm), (k_ps, k_mm))):
                    act.wait_ge(mm, b + 1)
                    if not first:
                        act.wait_ge(left1, 2 * (b - 2) + n + 1)
                    if n == 0:
                        nc.scalar.activation(whole[n][k][:, :], ps[:, :], ACT.Identity, bias=bq[:, 0:1],
                                             scale=HD ** -0.5).then_inc(whole_ready, 1)
                    else:
                        nc.scalar.copy(whole[n][k][:, :], ps[:, :]).then_inc(whole_ready, 1)
            act.wait_ge(wloaded, 96)
            act.wait_ge(scaled, 3)
            batches(act, evacuate)

        @block.vector
        def _(dve):
            dve.wait_ge(wloaded, 96)
            nc.vector.tensor_scalar(bq[:, :], bq[:, :], HD ** -0.5, None, ALU.mult).then_inc(scaled, 1)

            def latent(b, k, first):
                dve.wait_ge(gelu, 2 * b + 2)
                if not first:
                    dve.wait_ge(v_mm, b - 1)
                nc.vector.tensor_tensor(lat[k][0:LAT, :], act_half[0][:, :], act_half[1][:, :], ALU.add)\
                  .then_inc(lat_ready, 1)

            def work(b, k, first):
                for n in range(2):
                    dve.wait_ge(whole_ready, 2 * b + n + 1)
                    if not first:
                        dve.wait_ge(parts_stored[k], (b - k) * (NST // 2))
                    nc.vector.tensor_copy(part[n][k][:, 0, :], whole[n][k][:, :]).then_inc(part1, 1)
                dve.wait_ge(v_mm, b + 1)
                if not first:
                    dve.wait_ge(v_stored[k], (b - k) * 8)
                nc.vector.tensor_copy(v_sb[k][:, :, :].rearrange("p a b -> p (a b)"), v_ps[:, :]).then_inc(v_ready, 1)
                if not isinstance(b, int) or b < BATCH - 1:
                    latent(b + 1, 1 - k, isinstance(b, int) and b == 0)
                for n in range(2):
                    dve.wait_ge(left1, 2 * b + n + 1)
                    nc.vector.tensor_copy(part[n][k][:, 1, :], rest1[n][k][:, :]).then_inc(part2, 1)
                for n in range(2):
                    dve.wait_ge(left2, 2 * b + n + 1)
                    nc.vector.tensor_copy(part[n][k][:, 2, :], rest2[n][k][:, :]).then_inc(part3, 1)
            latent(0, 0, True)
            batches(dve, work, BATCH // 2 - 1)
            work(BATCH - 2, 0, False)
            work(BATCH - 1, 1, False)

        @block.tensor
        def _(pe):
            pe.wait_ge(wloaded, 96)
            pe.wait_ge(cleared, 3)

            def product(b, k, first):
                xb = xnT[:, bass.ds(b * SEQ, SEQ)]
                if not first or k:
                    pe.wait_ge(gelu, 2 * b)
                for h in range(2):
                    mm = nc.tensor.matmul(lat_ps[h][0:LAT, :], wkd[:, h * LAT:(h + 1) * LAT], xb, start=True, stop=True)
                mm.then_inc(lat_mm, 1)
                if not first or k:
                    pe.wait_ge(whole_ready, 2 * b)
                nc.tensor.matmul(q_ps[:, :], wq[:, :], xb, start=True, stop=True).then_inc(q_mm, 1)
                pe.wait_ge(lat_ready, b + 1)
                nc.tensor.matmul(k_ps[:, :], wku[:, 0:D], lat[k][:, :], start=True, stop=True).then_inc(k_mm, 1)
                if not first or k:
                    pe.wait_ge(v_ready, b)
                for kb in range(NKB):
                    mm = nc.tensor.matmul(v_ps[:, kb * D:(kb + 1) * D], lat[k][:, kb * P:(kb + 1) * P],
                                          wku[:, D:2 * D], start=True, stop=True)
                mm.then_inc(v_mm, 1)
            batches(pe, product)


EXP_UNITS = [(2 * SEQ, [(0, 0, 0), (SEQ, 1, 0)]),
             (2 * SEQ, [(0, 0, 1), (384, 0, 3), (SEQ, 1, 1), (SEQ + 384, 1, 3)]),
             (SEQ, [(0, 0, 2), (256, 1, 2)])]
EXP_AT = [0, 2 * SEQ, 4 * SEQ]
PROBS = 5 * SEQ
PROB_AT = {(hp, kb): EXP_AT[u] + c for u, (_, ps) in enumerate(EXP_UNITS) for c, hp, kb in ps}
MAX_UNITS = [(h, 1, 3) for h in range(4)] + [(h, 1, 2) for h in range(4)] + [(0, 2, 1), (2, 2, 1), (0, 4, 0)]
NEX, NMX = 2 * len(EXP_UNITS), len(MAX_UNITS)


def mla_attend(nc, keep, a, st0, name):
    ident, identb = keep["ident"], keep["identb"]
    xnT, q_dram, k_dram, v_dram = st0
    with Stage(nc, name) as st:
        QS = [st.sb(f"QS{k}", [P, NPAIR, SEQ], BF16) for k in range(2)]
        KS = [st.sb(f"KS{k}", [P, HEADS, SEQ], BF16) for k in range(2)]
        KP = [st.sb(f"KP{k}", [P, 2, SEQ], BF16) for k in range(2)]
        probs = [st.sb(f"probs{k}", [P, 2, PROBS]) for k in range(2)]
        v_in = [st.sb(f"v_in{k}", [P, NKB, D]) for k in range(2)]
        v_aug = [st.sb(f"v_aug{k}", [P, NKB, HEADS, 32]) for k in range(2)]
        out_raw = st.sb("out_raw", [P, SEQ])
        recip = st.sb("recip", [P, NKB, 4])
        out_tok = st.sb("out_tok", [P, NKB, D])
        mx = [st.sb(f"mx{k}", [P, NKB, 4]) for k in range(2)]
        mrest = [st.sb(f"mrest{k}", [P, NKB, 4]) for k in range(2)]
        mstack = [st.sb(f"mstack{k}", [P, NKB, 4, 8], BF16) for k in range(2)]
        mask_q, mask_k = st.sb("mask_q", [P, P], BF16), st.sb("mask_k", [P, P], BF16)
        head_rows = st.sb("head_rows", [P, 2])
        bo = st.sb("bo", [P, D])
        max_ps = [st.ps(f"maxp{k}", [P, SEQ]) for k in range(2)]
        exp_ps = [st.ps(f"expp{k}", [P, 2 * SEQ]) for k in range(2)]
        sum_ps = st.ps("sump", [P, SEQ])
        misc_ps = st.ps("misc", [P, SEQ])
        misc_b = misc_ps[:, :].bitcast(BF16).rearrange("p (j q) -> p j q", j=2)
        cleared, consts = st.sem("cleared"), st.sem("consts")
        loaded = [st.sem(f"loaded{k}") for k in range(2 * NG)]
        v_loaded = [st.sem(f"v_loaded{k}") for k in range(2)]
        bo_loaded = st.sem("bo_loaded")
        keys_ready, v_ready, x_biased = st.sem("keys_ready"), st.sem("v_ready"), st.sem("x_biased")
        score_mm, exp_done, max_mm, max_done = (st.sem(n) for n in ("score_mm", "exp_done", "max_mm", "max_done"))
        values_mm, raw_ready, raw_turned, tok_ready = (st.sem(n) for n in ("values_mm", "raw_ready", "raw_turned", "tok_ready"))
        link_sem, mstack_ready, m_turned, m_ready = (st.sem(n) for n in ("link", "mstack_ready", "m_turned", "m_ready"))
        all_turned, batch_done = st.sem("all_turned"), st.sem("batch_done")
        block = st.block()

        row_no = st.sb("row_no", [P, 1], I32)
        recip_ready, heads_ready = st.sem("recip_ready"), st.sem("heads_ready")
        sp_passed, pool_passed = st.sem("sp_passed"), st.sem("pool_passed")

        def steps(eng, one):
            for k in range(-4, 8):
                one(0, k)
            with eng.Fori(1, BATCH // 2 - 1) as i:
                for k in range(8):
                    one(i, k)
            for k in range(10):
                one(BATCH // 2 - 1, k)

        def there(i, k):
            return not isinstance(i, int) or 0 <= 8 * i + k < NSTEP

        @block.sync
        def _(sp):
            sp.wait_ge(cleared, 4)

            def load(i, k):
                if not 0 <= k < 8:
                    return
                s, par, g = 8 * i + k, k // 4, k % 4
                if there(i, k - 8):
                    sp.wait_ge(score_mm, (s - 7) * NEX)
                cols = bass.ds((8 * i + 4 * par) * P, SEQ)
                for j in range(2):
                    sp.dma_start(QS[par][0:ROWS, 2 * g + j, :], q_dram[:, 16 * (2 * g + j):16 * (2 * g + j) + 16, cols])\
                      .then_inc(loaded[k], 16)
                if there(i, k - 2):
                    sp.wait_ge(keys_ready, s - 1)
                for j in range(2):
                    sp.dma_start(KP[k % 2][0:ROWS, j, :], k_dram[:, 16 * (2 * g + j):16 * (2 * g + j) + 16, cols])\
                      .then_inc(loaded[k], 16)
                if g == 2:
                    if there(i, k - 8):
                        sp.wait_ge(v_ready, 2 * i + par - 1)
                        pass_waits(sp, sp_passed)
                    sp.dma_start(v_in[par][:, :, :], v_dram[:, bass.ds(8 * i + 4 * par, NKB), :])\
                      .then_inc(v_loaded[par], 16)
            steps(sp, load)

        @block.scalar
        def _(act):
            act.dma_start(bo[:, :], a["L0_attn_bo"].partition_broadcast(P)).then_inc(bo_loaded, 16)

            def expo(i, k, u):
                if not there(i, k):
                    return
                s = 8 * i + k
                act.wait_ge(score_mm, s * NEX + u + 1)
                if u == 0 and there(i, k - 2):
                    act.wait_ge(values_mm, s - 1)
                w, at = EXP_UNITS[u % 3][0], EXP_AT[u % 3]
                nc.scalar.activation(probs[k % 2][:, u // 3, at:at + w], exp_ps[u % 2][:, 0:w], ACT.Exp)\
                  .then_inc(exp_done, 1)

            def copy_batch(i, k):
                if k % 4 == 1 and there(i, k - 2):
                    b = 2 * i + (k - 2) // 4
                    act.wait_ge(all_turned, b + 1)
                    nc.scalar.copy(xnT[:, bass.ds(b * SEQ, SEQ)], misc_ps[:, :]).then_inc(batch_done, 1)

            def copy_raw(i, k):
                if there(i, k - 1):
                    s = 8 * i + k - 1
                    act.wait_ge(values_mm, s + 1)
                    if there(i, k - 2):
                        act.wait_ge(raw_turned, s)
                    nc.scalar.copy(out_raw[:, :], sum_ps[:, :]).then_inc(raw_ready, 1)

            def copy_max(i, k):
                if there(i, k + 3):
                    m, par, g = 8 * i + k + 3, (k + 3) % 8 // 4, (k + 3) % 4
                    act.wait_ge(m_turned, m + 1)
                    nc.scalar.copy(QS[par][ROWS:P - 16, 2 * g:2 * g + 2, :], misc_b[ROWS:P - 16, :, :])\
                      .then_inc(m_ready, 1)

            def step(i, k):
                expo(i, k, 0)
                expo(i, k, 1)
                copy_batch(i, k)
                expo(i, k, 2)
                expo(i, k, 3)
                copy_raw(i, k)
                expo(i, k, 4)
                copy_max(i, k)
                expo(i, k, 5)
            steps(act, step)
            act.wait_ge(batch_done, BATCH)

        @block.vector
        def _(dve):
            link = chained(dve, link_sem)
            dve.wait_ge(cleared, 5)
            link(nc.vector.tensor_scalar(row_no[:, :], row_no[:, :], 8, None, ALU.bitwise_and))
            link(nc.vector.tensor_scalar(head_rows[:, 1:2], row_no[:, :], 0.125, None, ALU.mult))
            nc.vector.tensor_scalar(head_rows[:, 0:1], head_rows[:, 1:2], -1.0, 1.0, ALU.mult, ALU.add)\
              .then_inc(heads_ready, 1)
            LINKED = 2

            def maxima(i, k):
                if not there(i, k):
                    return
                m = 8 * i + k
                for u, (h, n, qb) in enumerate(MAX_UNITS):
                    dve.wait_ge(max_mm, m * NMX + u + 1)
                    N = (qb + 1) * P
                    nc.vector.tensor_reduce(mx[k % 2][:, qb, h:h + n],
                                            max_ps[(k + u) % 2][:, 0:n * N].rearrange("p (n k) -> p n k", n=n),
                                            AX.X, ALU.max).then_inc(max_done, 1)

            def split_max(i, k):
                if not there(i, k):
                    return
                m = 8 * i + k
                top, rest, parts = mx[k % 2], mrest[k % 2], mstack[k % 2]

                def linked(n, ins):
                    ins.then_inc(link_sem, 1)
                    dve.wait_ge(link_sem, LINKED + 4 * m + n)
                dve.wait_ge(max_done, (m + 1) * NMX)
                if there(i, k - 2):
                    dve.wait_ge(m_turned, m - 1)
                linked(1, nc.vector.tensor_scalar(parts[:, :, :, 0], top[:, :, :], -1.0, None, ALU.mult))
                linked(2, nc.vector.scalar_tensor_tensor(out=rest[:, :, :], in0=top[:, :, :], scalar=-1.0,
                                                         in1=parts[:, :, :, 0], op0=ALU.mult, op1=ALU.subtract))
                linked(3, nc.vector.tensor_copy(parts[:, :, :, 1], rest[:, :, :]))
                linked(4, nc.vector.tensor_tensor(rest[:, :, :], rest[:, :, :], parts[:, :, :, 1], ALU.subtract))
                nc.vector.tensor_copy(parts[:, :, :, 2], rest[:, :, :]).then_inc(mstack_ready, 1)

            def divide(i, k):
                if not there(i, k):
                    return
                s, g = 8 * i + k, k % 4
                dve.wait_ge(raw_turned, s + 1)
                raw = misc_ps[:, :].rearrange("p (b h c) -> p b h c", b=NKB, h=4)
                nc.vector.reciprocal(recip[:, :, :], raw[:, :, :, HD]).then_inc(recip_ready, 1)
                dve.wait_ge(recip_ready, s + 1)
                if g == 0 and there(i, k - 4):
                    dve.wait_ge(all_turned, 2 * i + k // 4)
                nc.vector.tensor_tensor(
                    out_tok[:, :, g * 32:g * 32 + 32].rearrange("p b (h c) -> p b h c", h=4), raw[:, :, :, 0:HD],
                    recip[:, :, :].unsqueeze(3).broadcast_to([P, NKB, 4, HD]), ALU.mult).then_inc(tok_ready, 1)

            dve.wait_ge(consts, 7)
            def step(i, k):
                maxima(i, k + 4)
                split_max(i, k + 4)
                divide(i, k - 1)
            steps(dve, step)

        @block.gpsimd
        def _(pool):
            for k in range(2):
                nc.gpsimd.memset(QS[k][ROWS:P, :, :], 0.0).then_inc(cleared, 1)
                nc.gpsimd.memset(KP[k][ROWS:P, :, :], 1.0).then_inc(cleared, 1)
            pool.wait_ge(cleared, 4)
            nc.gpsimd.iota(row_no[:, :], pattern=[[0, 1]], base=0, channel_multiplier=1).then_inc(cleared, 1)
            for k in range(2):
                nc.gpsimd.memset(v_aug[k][:, :, :, :], 0.0).then_inc(consts, 1)
                nc.gpsimd.memset(mstack[k][:, :, :, :], 0.0).then_inc(consts, 1)
            nc.gpsimd.memset(mask_q[:, :], 0.0).then_inc(consts, 1)
            nc.gpsimd.memset(mask_k[:, :], 0.0).then_inc(consts, 1)
            pool.wait_ge(consts, 6)
            nc.gpsimd.affine_select(out=mask_q[:, :], in_=mask_q[:, :], compare_op=ALU.is_ge, fill=NEG, base=0,
                                    pattern=[[-1, P]], channel_multiplier=1).then_inc(consts, 1)
            nc.gpsimd.affine_select(out=mask_k[:, :], in_=mask_k[:, :], compare_op=ALU.is_ge, fill=NEG, base=0,
                                    pattern=[[1, P]], channel_multiplier=-1).then_inc(consts, 1)
            for k in range(2):
                nc.gpsimd.memset(v_aug[k][:, :, :, HD:HD + 1], 1.0).then_inc(consts, 1)
            pool.wait_ge(heads_ready, 1)

            def keys(i, k):
                if not 0 <= k < 8:
                    return
                s, par, g = 8 * i + k, k // 4, k % 4
                pool.wait_ge(loaded[k], 64 * (i + 1))
                if there(i, k - 8):
                    pool.wait_ge(score_mm, (s - 7) * NEX)
                    pass_waits(pool, pool_passed)
                heads = KS[par][:, :, :].rearrange("p (j e) t -> p j e t", e=2)
                for e in range(2):
                    ins = nc.gpsimd.tensor_scalar(heads[:, 2 * g:2 * g + 2, e, :], KP[k % 2][:, :, :],
                                                  head_rows[:, e:e + 1], None, ALU.mult)
                ins.then_inc(keys_ready, 1)
                if g == 2:
                    pool.wait_ge(v_loaded[par], 16 * (i + 1))
                    if there(i, k - 8):
                        pool.wait_ge(values_mm, 8 * i + 4 * par - 4)
                        pass_waits(pool, pool_passed)
                    nc.gpsimd.tensor_copy(v_aug[par][:, :, :, 0:HD],
                                          v_in[par][:, :, :].rearrange("p b (h c) -> p b h c", h=HEADS))\
                      .then_inc(v_ready, 1)
            pool.wait_ge(consts, 10)
            steps(pool, keys)
            pool.wait_ge(bo_loaded, 16)
            nc.gpsimd.tensor_tensor(keep["x"][:, :, :], keep["x"][:, :, :],
                                    bo[:, :].unsqueeze(1).broadcast_to([P, RUN, D]), ALU.add).then_inc(x_biased, 1)
            pool.wait_ge(x_biased, 1)

        @block.tensor
        def _(pe):
            pe.wait_ge(consts, 10)

            def score(i, k, u):
                if not there(i, k):
                    return
                s, par, g = 8 * i + k, k % 8 // 4, k % 4
                if u == 0:
                    pe.wait_ge(m_ready, s + 1)
                if u >= 2 or there(i, k - 1):
                    pe.wait_ge(exp_done, s * NEX + u - 1)
                out, j = exp_ps[u % 2], 2 * g + u // 3
                for c, e, kb in EXP_UNITS[u % 3][1]:
                    n = SEQ - kb * P
                    nc.tensor.matmul(out[:, c:c + n], KS[par][:, 2 * j + e, kb * P:(kb + 1) * P],
                                     QS[par][:, j, kb * P:SEQ], start=True, stop=False)
                    mm = nc.tensor.matmul(out[:, c:c + P], identb[:, :], mask_k[:, :], start=False, stop=True)
                mm.then_inc(score_mm, 1)

            def maximum(i, k, u):
                if not there(i, k):
                    return
                m, par, g = 8 * i + k, k % 8 // 4, k % 4
                if u == 0:
                    pe.wait_ge(keys_ready, m + 1)
                if u >= 2 or there(i, k - 1):
                    pe.wait_ge(max_done, m * NMX + u - 1)
                h0, heads, qb = MAX_UNITS[u]
                n = (qb + 1) * P
                for e in range(heads):
                    h, out = 4 * g + h0 + e, max_ps[(k + u) % 2]
                    nc.tensor.matmul(out[:, e * n:(e + 1) * n], QS[par][0:ROWS, h // 2, qb * P:(qb + 1) * P],
                                     KS[par][0:ROWS, h, 0:n], start=True, stop=False)
                    mm = nc.tensor.matmul(out[:, (e + 1) * n - P:(e + 1) * n], identb[:, :], mask_q[:, :],
                                          start=False, stop=True)
                mm.then_inc(max_mm, 1)

            def values(i, k, kb):
                if not there(i, k):
                    return
                s, par, g = 8 * i + k, k % 8 // 4, k % 4
                if kb == 0:
                    pe.wait_ge(exp_done, (s + 1) * NEX)
                    pe.wait_ge(v_ready, 2 * i + k // 4 + 1)
                    if there(i, k - 1):
                        pe.wait_ge(raw_ready, s)
                n = SEQ - kb * P
                for h in range(4):
                    at = PROB_AT[h % 2, kb]
                    mm = nc.tensor.matmul(sum_ps[32 * h:32 * h + 32, kb * P:SEQ], v_aug[par][:, kb, 4 * g + h, :],
                                          probs[k % 2][:, h // 2, at:at + n], start=(kb == 0), stop=(kb == NKB - 1))
                if kb == NKB - 1:
                    mm.then_inc(values_mm, 1)

            def turn_batch(i, k):
                if k % 4 == 1 and there(i, k - 2):
                    pe.wait_ge(tok_ready, 8 * i + k - 1)
                    for b in range(NKB):
                        mm = nc.tensor.transpose(misc_ps[:, b * P:(b + 1) * P], out_tok[:, b, :], ident[:, :])
                    mm.then_inc(all_turned, 1)

            def turn_max(i, k):
                if there(i, k + 3):
                    pe.wait_ge(mstack_ready, 8 * i + k + 4)
                    if there(i, k - 2):
                        pe.wait_ge(tok_ready, 8 * i + k - 1)
                    if k % 4 == 1 and there(i, k - 2):
                        pe.wait_ge(batch_done, 2 * i + (k - 2) // 4 + 1)
                    if there(i, k + 2):
                        pe.wait_ge(m_ready, 8 * i + k + 3)
                    for j in range(2):
                        for b in range(NKB):
                            mm = nc.tensor.transpose(misc_b[ROWS:P - 16, j, b * P:(b + 1) * P],
                                                     mstack[(k + 3) % 2][:, b, 2 * j:2 * j + 2, :]
                                                     .rearrange("p h c -> p (h c)"), identb[:, :])
                    mm.then_inc(m_turned, 1)

            def turn_raw(i, k):
                if there(i, k - 1):
                    s = 8 * i + k - 1
                    pe.wait_ge(raw_ready, s + 1)
                    if there(i, k + 3):
                        pe.wait_ge(m_ready, s + 5)
                    elif k % 4 == 1 and there(i, k - 2):
                        pe.wait_ge(batch_done, 2 * i + (k - 2) // 4 + 1)
                    elif there(i, k - 2):
                        pe.wait_ge(tok_ready, s)
                    for b in range(NKB):
                        mm = nc.tensor.transpose(misc_ps[:, b * P:(b + 1) * P], out_raw[:, b * P:(b + 1) * P],
                                                 ident[:, :])
                    mm.then_inc(raw_turned, 1)

            def step(i, k):
                score(i, k, 0)
                maximum(i, k + 4, 0)
                maximum(i, k + 4, 1)
                score(i, k, 1)
                turn_batch(i, k)
                maximum(i, k + 4, 2)
                maximum(i, k + 4, 3)
                values(i, k - 1, 0)
                score(i, k, 2)
                maximum(i, k + 4, 4)
                maximum(i, k + 4, 5)
                values(i, k - 1, 1)
                score(i, k, 3)
                maximum(i, k + 4, 6)
                maximum(i, k + 4, 7)
                values(i, k - 1, 2)
                values(i, k - 1, 3)
                score(i, k, 4)
                maximum(i, k + 4, 8)
                maximum(i, k + 4, 9)
                turn_max(i, k)
                score(i, k, 5)
                maximum(i, k + 4, 10)
                turn_raw(i, k)
            steps(pe, step)


def mla_output(nc, keep, a, st0, name):
    x, outT = keep["x"], st0[0]
    with Stage(nc, name) as st:
        wo = st.sb("wo", [P, D])
        out_ps = [st.ps(f"out{k}", [P, CH, D]) for k in range(4)]
        loaded, projected, added = st.sem("loaded"), st.sem("projected"), st.sem("added")
        runs = outT[:, :].rearrange("d (p r) -> d p r", r=RUN)
        block = st.block()

        @block.sync
        def _(sp):
            sp.dma_start(wo[:, :], a["L0_attn_Wo"]).then_inc(loaded, 16)

        @block.tensor
        def _(pe):
            pe.wait_ge(loaded, 16)
            for c in range(NCH):
                if c >= 4:
                    pe.wait_ge(added, c - 3)
                for t in range(CH):
                    mm = nc.tensor.matmul(out_ps[c % 4][:, t, :], runs[:, :, c * CH + t], wo[:, :], start=True, stop=True)
                mm.then_inc(projected, 1)

        @block.vector
        def _(dve):
            for c in range(NCH):
                dve.wait_ge(projected, c + 1)
                xs = x[:, c * CH:(c + 1) * CH, :]
                nc.vector.tensor_tensor(xs, xs, out_ps[c % 4][:, :, :], ALU.add).then_inc(added, 1)
                for n in ((c - 1,) if 0 < c < NCH - 1 else (c - 1, c) if c else ()):
                    dve.wait_ge(added, n + 1)
                    for t in range(CH):
                        token_stats(nc, keep, n * CH + t)


def mla(nc, keep, a, name):
    with ExitStack() as ctx:
        xnT = ctx.enter_context(nc.sbuf_tensor(f"{name}_xnT", [P, TOK], F32))
        q_dram = nc.dram_tensor(f"{name}_q", [SLOTS, P, TOK], BF16, kind="Internal").ap()
        k_dram = nc.dram_tensor(f"{name}_k", [SLOTS, P, TOK], BF16, kind="Internal").ap()
        v_dram = nc.dram_tensor(f"{name}_v", [P, BATCH * NKB, D], F32, kind="Internal").ap()
        st0 = (xnT, q_dram, k_dram, v_dram)
        mla_project(nc, keep, a, st0, name)
        mla_attend(nc, keep, a, st0, name + "a")
        mla_output(nc, keep, a, st0, name + "o")


E = 64
TOKS = 8
NS = RUN // TOKS
UI, UO = 32, 64
TAB = UI * UO
HALF = P // 2
AHEAD = 14
MOE_TABLES = ("A_up", "B_up", "A_down", "B_down")


def moe_tables(nc, keep, a, tab, name):
    ident = keep["ident"]
    with Stage(nc, name) as st:
        router_up, router_down = st.sb("router_up", [E, TOKS, P]), st.sb("router_down", [E, UI, 2, UO])
        bias_rows, bias_left = st.sb("bias_rows", [UO, 2, UO]), st.sb("bias_left", [P, 2, UO])
        turn_ps = [st.ps(f"turn{k}", [P, TOKS, E]) for k in range(2)]
        loaded_r, link_sem, turned, copied = st.sem("loaded_r"), st.sem("link"), st.sem("turned"), st.sem("copied")
        zeroed, scaled, consts = st.sem("zeroed"), st.sem("scaled"), st.sem("consts")
        block = st.block()

        @block.sync
        def _(sp):
            sp.dma_start(router_up[:, :, :], a["L1_ffn_W_up"].rearrange("e (t d) -> e t d", t=TOKS)).then_inc(loaded_r, 16)
            for h in range(2):
                sp.dma_start(router_down[:, :, h, :], a["L1_ffn_W_down"].rearrange("e (h o p) -> e h o p", h=2, p=UO)[:, h])\
                  .then_inc(loaded_r, 16)
                sp.dma_start(bias_rows[:, h, :], a["L1_ffn_bias_up"].rearrange("(o p) -> o p", p=UO)).then_inc(loaded_r, 16)
            sp.dma_start(tab["bias_down"][:, :], a["L1_ffn_bias_down"].partition_broadcast(P)).then_inc(loaded_r, 16)
            sp.dma_start(tab["scale_up"][:, :], a["L1_ffn_scale_up"].partition_broadcast(P)).then_inc(loaded_r, 16)
            sp.dma_start(tab["scale_down"][:, :], a["L1_ffn_scale_down"].partition_broadcast(P)).then_inc(loaded_r, 16)

        @block.scalar
        def _(act):
            for n in range(6):
                act.wait_ge(turned, n + 1)
                if n == 0:
                    out, src = tab["router_upT"][:, :, :], turn_ps[0][:, :, :]
                elif n == 1:
                    out, src = bias_left[:, 0, :], turn_ps[1][:, 0, :]
                else:
                    out, src = tab["router_downT"][:, (n - 2) * TOKS:(n - 1) * TOKS, :], turn_ps[n % 2][:, :, :]
                nc.scalar.copy(out, src).then_inc(copied, 1)
            act.wait_ge(copied, 6)

        @block.tensor
        def _(pe):
            pe.wait_ge(loaded_r, 8 * 16)
            for t in range(TOKS):
                mm = nc.tensor.transpose(turn_ps[0][:, t, :], router_up[:, t, :], ident[0:E, 0:E])
            mm.then_inc(turned, 1)
            nc.tensor.transpose(turn_ps[1][:, 0, :], bias_rows[:, :, :].rearrange("o h p -> o (h p)"),
                                ident[0:UO, 0:UO]).then_inc(turned, 1)
            for n in range(4):
                pe.wait_ge(copied, n + 1)
                for t in range(TOKS):
                    mm = nc.tensor.transpose(turn_ps[n % 2][:, t, :], router_down[:, n * TOKS + t, :, :].rearrange("e h p -> e (h p)"),
                                             ident[0:E, 0:E])
                mm.then_inc(turned, 1)

        @block.gpsimd
        def _(pool):
            nc.gpsimd.iota(tab["expert_no"][:, :, :], pattern=[[0, 2], [1, E]], base=0, channel_multiplier=0,
                           allow_small_or_imprecise_dtypes=True).then_inc(consts, 1)
            for n in ("spread", "pick_half", "pick0", "pick1"):
                nc.gpsimd.memset(tab[n][:, :], 0.0).then_inc(zeroed, 1)
            nc.gpsimd.memset(tab["euler"][:, :], float(np.e)).then_inc(zeroed, 1)
            pool.wait_ge(zeroed, 5)
            for b in range(2):
                nc.gpsimd.affine_select(out=tab["spread"][:, :], in_=tab["spread"][:, :], compare_op=ALU.not_equal,
                                        fill=1.0, base=-HALF * b, pattern=[[-1, HALF]], channel_multiplier=1)\
                  .then_inc(consts, 1)
                pool.wait_ge(consts, 2 + b)

        @block.vector
        def _(dve):
            link = chained(dve, link_sem)
            dve.wait_ge(zeroed, 5)
            for h in range(2):
                rows = slice(h * HALF, (h + 1) * HALF)
                link(nc.vector.memset(tab["pick_half"][rows, rows], 1.0))
                link(nc.vector.memset(tab["pick0"][rows, h * HALF:h * HALF + 32], 1.0))
                link(nc.vector.memset(tab["pick1"][rows, h * HALF + 32:(h + 1) * HALF], 1.0))
            dve.wait_ge(loaded_r, 8 * 16)
            link(nc.vector.tensor_scalar(tab["bias_down"][:, :], tab["bias_down"][:, :], 0.5, None, ALU.mult))
            link(nc.vector.tensor_scalar(tab["scale_down"][:, :], tab["scale_down"][:, :], 0.5, None, ALU.mult))
            dve.wait_ge(copied, 2)
            bias, left = bias_left[:, 0, :], bias_left[:, 1, :]
            parts = tab["bias_up"]
            link(nc.vector.tensor_copy(parts[:, 0, :], bias))
            link(nc.vector.tensor_tensor(left, bias, parts[:, 0, :], ALU.subtract))
            link(nc.vector.tensor_copy(parts[:, 1, :], left))
            link(nc.vector.tensor_copy(parts[HALF:P, 0, :], parts[HALF:P, 1, :]))
            link(nc.vector.tensor_tensor(left, left, parts[:, 1, :], ALU.subtract))
            link(nc.vector.tensor_copy(parts[0:HALF, 1, :], left[0:HALF]))
            link(nc.vector.memset(parts[HALF:P, 1, :], 0.0))
            dve.wait_ge(consts, 3)
            for h in range(2):
                link(nc.vector.tensor_copy(tab["both"][:, h * HALF:(h + 1) * HALF], tab["spread"][:, :]))


def moe(nc, keep, tab, name, more):
    x, ident, identb = keep["x"], keep["ident"], keep["identb"]
    with Stage(nc, name) as st:
        xn = st.sb("xn", [P, TOKS, D])
        xnT = st.sb("xnT", [P, TOKS, P])
        xsT = st.sb("xsT", [P, 32, 2, UI])
        Bu, Au = st.sb("Bu", [P, 32, UO]), st.sb("Au", [P, 32, UO])
        Zu = st.sb("Zu", [P, 32, UO])
        hT = [st.sb(f"hT{k}", [P, 2, 32, UO]) for k in range(2)]
        hR = st.sb("hR", [P, UI, P])
        Bd = st.sb("Bd", [P, 2, 32, 2, 32])
        Ad = st.sb("Ad", [P, 2, 32, 2, 32])
        ytok = xnT[:, :, :].rearrange("p t n -> p (t n)")
        lgT, spreadp = keep["gateT"][:, 0, :], keep["gateT"][:, 1, :].rearrange("p (k c) -> p k c", k=2)
        lg, top, topi = keep["downT"][:, 2, 0:E], st.sb("top", [P, 8]), st.sb("topi", [P, 8], U32)
        chosen, gap, ratio, den = st.sb("chosen", [P, 2]), st.sb("gap", [P, 1]), st.sb("ratio", [P, 1]), st.sb("den", [P, 1])
        prob = st.sb("prob", [P, 2])
        onehot = [st.sb(f"onehot{k}", [P, 2 * E], BF16) for k in range(2)]
        ohTu = st.sb("ohTu", [P, 2, 2, 2, 32], BF16)
        ohTd = st.sb("ohTd", [P, 2, P], BF16)
        probu, probd = keep["downT"][:, 2, HALF:P], keep["gateT"][:, 2, :].rearrange("p (k c) -> p k c", k=2)
        gat_ps = [st.ps(f"gat{k}", [P, 512]) for k in range(2)]
        z_ps = [st.ps(f"z{k}", [P, 8, UO]) for k in range(2)]
        y_ps = st.ps("y", [P, 32, 32])
        misc = [st.ps(f"misc{k}", [P, 512]) for k in range(2)]
        names = ("xn_ready", "turned_x", "log_mm", "logits", "one_ready", "pow_in", "pow_done",
                 "probs_ready", "oh_turned", "spread_mm", "free0", "free1", "gat_mm",
                 "gat_read", "z_mm", "z_read", "h_mm", "h_ready", "hR_ready", "pe_passed", "dve_passed",
                 "xsT_ready", "y_mm", "y_read", "x_done", "link", "zeroed", "x_biased")
        S = {n: st.sem(n) for n in names}
        block = st.block()
        y_flat = y_ps[:, :, :].rearrange("p a b -> p (a b)")
        h_ps = [y_flat[:, b * 512:(b + 1) * 512].rearrange("p (n o) -> p n o", n=8) for b in range(2)]

        def turns(eng, one):
            one(-1, 1)
            one(0, 0)
            one(1, 1)
            with eng.Fori(0, NS // 2 - 2) as i:
                one(i * 2 + 2, 0)
                one(i * 2 + 3, 1)
            one(NS - 2, 0)
            one(NS - 1, 1)
            one(NS, 0)

        def has(s, d):
            return not isinstance(s, int) or 0 <= s + d < NS

        def before(s, j, up):
            if not isinstance(s, int) or 0 < s < NS:
                return 2 * up * s - up + j
            return j if s == 0 else 2 * up * NS - 2 * up + j

        def uses(s, j):
            if isinstance(s, int) and s == -1:
                return j - 2
            return 5 * s + 1 + j - (3 if isinstance(s, int) and s == NS else 0)

        def routing(s, down):
            if isinstance(s, int) and s == -1:
                return 0
            if isinstance(s, int) and s == NS:
                return 2 * NS - 1
            return 2 * s + (0 if down else 1)

        @block.tensor
        def _(pe):
            def gather(s, j):
                if j < 16:
                    m, w, q = j // 8, "BA"[j // 4 % 2], j % 4
                    if j % 4 == 0 and m == 0:
                        pe.wait_ge(S["free0"], uses(s - 1, 4) + 1)
                else:
                    w, m, q = "BA"[(j - 16) // 8], (j - 16) // 4 % 2, j % 4
                    if j == 16:
                        pe.wait_ge(S["free0"], uses(s, 1) + 1)
                n = before(s, j, 16)
                if j >= 2 or not isinstance(s, int) or s > 0:
                    pe.wait_ge(S["gat_read"], n - 1)
                out = gat_ps[j % 2]
                if j < 16:
                    lhs = ohTu[:, m, :, :, :].rearrange("e h k n -> e (h k n)")
                    for c, t in enumerate((w + "_up", w + "_up3")):
                        mm = nc.tensor.matmul(out[:, :], lhs, tab[t][:, q * 512:(q + 1) * 512], start=(c == 0), stop=(c == 1))
                else:
                    k, half = q // 2, q % 2
                    for c, t in enumerate((w + "_down", w + "_down3")):
                        cols = tab[t][:, :].rearrange("e (p b j) -> e p b j", b=2, j=32)
                        for h in range(2):
                            for b in range(2):
                                n0 = 64 * h + 32 * m
                                mm = nc.tensor.matmul(out[64 * h + 32 * b:64 * h + 32 * b + 32, :],
                                                      ohTd[:, k, n0:n0 + 32], cols[:, half * 16:half * 16 + 16, b, :],
                                                      start=(c == 0), stop=(c == 1))
                mm.then_inc(S["gat_mm"], 1)

            def z_free(s, j):
                if j % 8 >= 2 or not isinstance(s, int) or s > 0:
                    pe.wait_ge(S["z_read"], before(s, j, 8) - 1)

            def up_right(s, m, u):
                if u == 0:
                    pe.wait_ge(S["gat_read"], before(s, 8 * m + 4, 16))
                    pe.wait_ge(S["xsT_ready"], 8 * s + 4 * m + 4)
                z_free(s, 4 * m + u)
                pass_waits(pe, S["pe_passed"])
                for n in range(8 * u, 8 * u + 8):
                    for h in range(2):
                        rows = slice(64 * h, 64 * h + 64)
                        mm = nc.tensor.matmul(z_ps[u % 2][rows, n % 8, :], xsT[rows, n, :, :].rearrange("p k i -> p (k i)"),
                                              Bu[rows, n, :], start=True, stop=True)
                mm.then_inc(S["z_mm"], 1)

            def up_left(s, m, u):
                if u == 0:
                    pe.wait_ge(S["gat_read"], before(s, 8 * m + 8, 16))
                    pe.wait_ge(S["z_read"], before(s, 4 * m + 4, 8))
                if m == 0 and u < 2:
                    if not isinstance(s, int) or s > 1:
                        pe.wait_ge(S["y_read"], s - 1)
                if 4 * m + u >= 2 or not isinstance(s, int) or s > 0:
                    pe.wait_ge(S["h_ready"], 8 * s + 4 * m + u - 1)
                for part in range(2):
                    nc.tensor.matmul(h_ps[u % 2], tab["both"][:, :], tab["bias_up"][:, part, :].unsqueeze(1)
                                     .broadcast_to([P, 8, UO]), start=(part == 0), stop=False)
                for n in range(8 * u, 8 * u + 8):
                    for h in range(2):
                        rows = slice(64 * h, 64 * h + 64)
                        mm = nc.tensor.matmul(h_ps[u % 2][rows, n % 8, :], Zu[rows, n, :], Au[rows, n, :],
                                              start=False, stop=(n == 8 * u + 7))
                mm.then_inc(S["h_mm"], 1)

            def down_right(s, m, u, k):
                if u == 0:
                    pe.wait_ge(S["gat_read"], before(s, 20 + 4 * m, 16))
                    pe.wait_ge(S["h_ready"], 8 * s)
                z_free(s, 8 + 4 * m + u)
                pass_waits(pe, S["pe_passed"])
                for n in range(8 * u, 8 * u + 8):
                    for h in range(2):
                        rows = slice(64 * h, 64 * h + 64)
                        mm = nc.tensor.matmul(z_ps[u % 2][rows, n % 8, :], hT[k][rows, m, n, :],
                                              Bd[rows, m, n, :, :].rearrange("p k c -> p (k c)"), start=True, stop=True)
                mm.then_inc(S["z_mm"], 1)

            def down_left(s, u):
                if u == 0:
                    pe.wait_ge(S["gat_read"], before(s, 32, 16))
                    pe.wait_ge(S["z_read"], before(s, 16, 8))
                    if has(s, 0):
                        pe.wait_ge(S["h_ready"], 8 * s + 8)
                    pass_waits(pe, S["pe_passed"])
                for n in range(4 * u, 4 * u + 4):
                    for h in range(2):
                        for m in range(2):
                            rows, g = slice(64 * h, 64 * h + 64), 2 * h + m
                            for k in range(2):
                                mm = nc.tensor.matmul(y_ps[32 * g:32 * g + 32, n, :], Ad[rows, m, n, k, :],
                                                      Bd[rows, m, n, k, :], start=(k == 0), stop=(k == 1))
                if u == 7:
                    mm.then_inc(S["y_mm"], 1)

            def router(s, down, t0, t1):
                use, steps = (0, UI) if down else (3, TOKS)
                if t0 == 0:
                    if down:
                        pe.wait_ge(S["hR_ready"], s)
                    else:
                        for b in range(2):
                            pe.wait_ge(S[f"free{b}"], uses(s, 2) + 1)
                    pe.wait_ge(S["free0"], uses(s, use))
                for t in range(t0, t1):
                    half = slice(64 * (t % 2), 64 * (t % 2) + 64)
                    if down:
                        lhs, rhs = tab["router_downT"][:, t, :], hR[:, t, :]
                    else:
                        lhs, rhs = tab["router_upT"][:, t, :], xnT[:, t, :]
                    mm = nc.tensor.matmul(misc[0][half, 0:P], lhs, rhs, start=(t < 2), stop=(t >= (UI if down else TOKS) - 2))
                if t1 == steps:
                    mm.then_inc(S["log_mm"], 1)

            def logits(s, down):
                n = uses(s, 0 if down else 3)
                pe.wait_ge(S["free0"], n + 1)
                pe.wait_ge(S["free1"], n)
                nc.tensor.matmul(misc[1][:, 0:E], lgT[:, :], tab["spread"][:, :], start=True, stop=True).then_inc(S["logits"], 1)

            def choices(s, down):
                pe.wait_ge(S["one_ready"], routing(s, down) + 1)
                pe.wait_ge(S["free0"], uses(s, 1 if down else 4))
                for k in range(2):
                    mm = nc.tensor.transpose(misc[0][:, :].bitcast(BF16)[:, k * P:(k + 1) * P], onehot[k][:, :], identb[:, :])
                mm.then_inc(S["oh_turned"], 1)
                pe.wait_ge(S["probs_ready"], routing(s, down) + 1)
                pe.wait_ge(S["free1"], uses(s, 1 if down else 4))
                if down:
                    mm = nc.tensor.matmul(misc[1][:, 0:P], tab["pick_half"][:, :], spreadp[:, :, :].rearrange("p k c -> p (k c)"),
                                          start=True, stop=True)
                else:
                    for k in range(2):
                        mm = nc.tensor.matmul(misc[1][:, 0:HALF], tab[f"pick{k}"][:, :], spreadp[:, k, :],
                                              start=(k == 0), stop=(k == 1))
                mm.then_inc(S["spread_mm"], 1)

            def turn_x(s):
                pe.wait_ge(S["xn_ready"], s + 2)
                for b in range(2):
                    if not (isinstance(s, int) and s == -1):
                        pe.wait_ge(S[f"free{b}"], uses(s, 2))
                    for t in range(4):
                        mm = nc.tensor.transpose(misc[b][:, t * P:(t + 1) * P], xn[:, 4 * b + t, :], ident[:, :])
                    mm.then_inc(S["turned_x"], 1)

            def turn(s, k):
                up, down, nxt = has(s, 0), has(s, -1), has(s, 1)
                for u in range(4):
                    if up:
                        gather(s, 4 + u)
                        up_right(s, 0, u)
                    if down and u == 1:
                        logits(s, True)
                if up:
                    for u in range(4):
                        gather(s, 8 + u)
                        up_left(s, 0, u)
                for u in range(4):
                    if up:
                        gather(s, 12 + u)
                        up_right(s, 1, u)
                    if down and u == 1:
                        choices(s, True)
                for u in range(4):
                    if down:
                        gather(s, 16 + u)
                    if up:
                        up_left(s, 1, u)
                if nxt:
                    turn_x(s)
                for u in range(4):
                    if down:
                        gather(s, 20 + u)
                        down_right(s, 0, u, 1 - k)
                    if nxt and u == 1:
                        router(s, False, 0, TOKS)
                    if nxt and u == 3:
                        logits(s, False)
                if down:
                    for u in range(4):
                        gather(s, 24 + u)
                        down_right(s, 1, u, 1 - k)
                for u in range(4):
                    if down:
                        gather(s, 28 + u)
                    if nxt and u == 1:
                        choices(s, False)
                if up:
                    router(s + 1, True, 0, AHEAD)
                for u in range(8):
                    if down:
                        down_left(s, u)
                    if nxt and u % 2 == 0:
                        gather(s + 1, u // 2)
                    if up:
                        router(s + 1, True, AHEAD + (UI - AHEAD) * u // 8, AHEAD + (UI - AHEAD) * (u + 1) // 8)
            turns(pe, turn)

        @block.vector
        def _(dve):
            def norm(s, u):
                if u == 0 and not (isinstance(s, int) and s == -1):
                    dve.wait_ge(S["turned_x"], 2 * s + 2)
                    dve.wait_ge(S["xsT_ready"], 8 * s + 8)
                for t in range(2 * u, 2 * u + 2):
                    ins = normalize(nc, keep, xn[:, t, :], s * TOKS + TOKS + t)
                if u == 3:
                    ins.then_inc(S["xn_ready"], 1)

            def square(s, u):
                m, h, k = u // 4, u // 2 % 2, u % 2
                if u == 0:
                    dve.wait_ge(S["xn_ready"], s + 1)
                src, dst = 64 * h + 32 * m, 64 * h + 32 * k
                nc.vector.transpose(xsT[dst:dst + 32, :, k, :].rearrange("j n i -> j i n"),
                                    xn[src:src + 32, :, :].rearrange("n t (c j) -> n (t c) j", j=32))\
                  .then_inc(S["xsT_ready"], 1)

            def placed(s, j):
                dve.wait_ge(S["gat_mm"], before(s, j, 16) + 1)
                src = gat_ps[j % 2][:, :].rearrange("n (c j) -> n c j", j=32)
                if j < 16:
                    q, dst = j % 4, (Bu, Au)[j // 4 % 2]
                    out = dst[:, :, q * 16:q * 16 + 16].rearrange("j n c -> j c n")
                else:
                    t, m, q = (j - 16) // 8, (j - 16) // 4 % 2, j % 4
                    if j % 8 == 0 and not (isinstance(s, int) and s == 1):
                        dve.wait_ge(S["y_mm"], s - 1)
                    dst = (Bd, Ad)[t]
                    out = dst[:, m, :, q // 2, q % 2 * 16:q % 2 * 16 + 16].rearrange("j n c -> j c n")
                nc.vector.transpose(out, src).then_inc(S["gat_read"], 1)

            def weigh_up(s, m, u):
                dve.wait_ge(S["z_mm"], before(s, 4 * m + u, 8) + 1)
                if u == 0 and m == 0:
                    dve.wait_ge(S["free1"], uses(s - 1, 4) + 1)
                c = 32 * m + 8 * u
                nc.vector.tensor_tensor(Zu[:, 8 * u:8 * u + 8, :], z_ps[u % 2][:, :, :],
                                        probu[:, c:c + 8].unsqueeze(2).broadcast_to([P, 8, UO]), ALU.mult)\
                  .then_inc(S["z_read"], 1)

            def weigh_down(s, m, u):
                dve.wait_ge(S["z_mm"], before(s, 8 + 4 * m + u, 8) + 1)
                if m == 0 and u == 0:
                    dve.wait_ge(S["free1"], uses(s, 1) + 1)
                c = 32 * m + 8 * u
                nc.vector.tensor_tensor(Bd[:, m, 8 * u:8 * u + 8, :, :],
                                        z_ps[u % 2][:, :, :].rearrange("p n (k c) -> p n k c", k=2),
                                        probd[:, :, c:c + 8].rearrange("p k n -> p n k").unsqueeze(3)
                                        .broadcast_to([P, 8, 2, 32]), ALU.mult).then_inc(S["z_read"], 1)

            def route(s, down, part):
                r = routing(s, down)
                LINKS = 7

                def link(n, ins):
                    ins.then_inc(S["link"], 1)

                def linked(n):
                    dve.wait_ge(S["link"], r * LINKS + n)
                if part == 0:
                    dve.wait_ge(S["logits"], r + 1)
                    nc.vector.tensor_copy(lg[:, :], misc[1][:, 0:E]).then_inc(S["free1"], 1)
                    dve.wait_ge(S["free1"], uses(s, 0 if down else 3) + 1)
                    pass_waits(dve, S["dve_passed"])
                    link(1, nc.vector.max(out=top[:, :], in_=lg[:, :]))
                    linked(1)
                    nc.vector.tensor_tensor(gap[:, :], top[:, 1:2], top[:, 0:1], ALU.subtract).then_inc(S["pow_in"], 1)
                    link(2, nc.vector.max_index(out=topi[:, :], in_max=top[:, :], in_values=lg[:, :]))
                elif part == 1:
                    linked(2)
                    link(3, nc.vector.tensor_copy(chosen[:, :], topi[:, 0:2]))
                    dve.wait_ge(S["pow_done"], r + 1)
                    link(4, nc.vector.tensor_scalar(den[:, :], ratio[:, :], 1.0, None, ALU.add))
                elif part == 2:
                    if not (isinstance(s, int) and s == -1):
                        dve.wait_ge(S["oh_turned"], r)
                    linked(4)
                    for k in range(2):
                        ins = nc.vector.tensor_scalar(onehot[k][:, :], tab["expert_no"][:, :, :].rearrange("p a e -> p (a e)"),
                                                      chosen[:, k:k + 1], None, ALU.is_equal)
                    ins.then_inc(S["one_ready"], 1)
                    link(5, nc.vector.reciprocal(prob[:, 0:1], den[:, :]))
                else:
                    if not (isinstance(s, int) and s == -1):
                        dve.wait_ge(S["spread_mm"], r)
                    linked(5)
                    link(6, nc.vector.tensor_tensor(prob[:, 1:2], ratio[:, :], prob[:, 0:1], ALU.mult))
                    scale = tab["scale_down" if down else "scale_up"][:, 0:1]
                    link(7, nc.vector.tensor_scalar(spreadp[:, 0, :], tab["spread"][:, :], prob[:, 0:1], scale, ALU.mult, ALU.mult))
                    linked(7)
                    nc.vector.tensor_scalar(spreadp[:, 1, :], tab["spread"][:, :], prob[:, 1:2], scale, ALU.mult, ALU.mult)\
                      .then_inc(S["probs_ready"], 1)

            def turn_back(s):
                dve.wait_ge(S["y_mm"], s)
                nc.vector.transpose(ytok.rearrange("n (o p) -> n p o", p=32),
                                    y_ps[:, :, :].rearrange("o n p -> o p n")).then_inc(S["y_read"], 1)

            def add(s):
                dve.wait_ge(S["y_read"], s)
                dve.wait_ge(S["x_biased"], s)
                xs = x[:, bass.ds(s * TOKS - TOKS, TOKS), :].rearrange("p t d -> p (t d)")
                nc.vector.tensor_tensor(xs, xs, ytok, ALU.add).then_inc(S["x_done"], 1)

            def stats(c, u):
                for t in range(2 * u, 2 * u + 2):
                    token_stats(nc, keep, c * TOKS + t)

            def turn(s, k):
                up, down, nxt, ended = has(s, 0), has(s, -1), has(s, 1), has(s, -2)
                for u in range(4):
                    if up:
                        placed(s, 4 + u)
                        weigh_up(s, 0, u)
                    if ended and u == 1:
                        turn_back(s - 1)
                for u in range(4):
                    if up:
                        placed(s, 8 + u)
                        square(s, 4 + u)
                    if down:
                        route(s, True, u)
                for u in range(4):
                    if up:
                        placed(s, 12 + u)
                        weigh_up(s, 1, u)
                for u in range(4):
                    if down:
                        placed(s, 16 + u)
                    if nxt:
                        norm(s, u)
                    if ended and u == 0:
                        add(s - 1)
                for u in range(4):
                    if down:
                        if u == 0 and ended:
                            dve.wait_ge(S["x_done"], s - 1)
                        placed(s, 20 + u)
                        weigh_down(s, 0, u)
                    if ended and more:
                        stats(s - 2, u)
                for u in range(4):
                    if down:
                        placed(s, 24 + u)
                        weigh_down(s, 1, u)
                    if nxt and u > 0:
                        route(s, False, u - 1)
                for u in range(4):
                    if down:
                        placed(s, 28 + u)
                    if nxt and u == 0:
                        route(s, False, 3)
                if nxt:
                    for u in range(4):
                        square(s + 1, u)
                        placed(s + 1, u)
            nc.vector.memset(xsT[:, :, :, :], 0.0).then_inc(S["zeroed"], 1)
            dve.wait_ge(S["zeroed"], 1)
            turns(dve, turn)
            turn_back(NS)
            add(NS)
            dve.wait_ge(S["x_done"], NS)
            if more:
                for u in range(4):
                    stats(NS - 1, u)

        @block.gpsimd
        def _(pool):
            def turn(s, k):
                if has(s, 0):
                    pool.wait_ge(S["xn_ready"], s + 1)
                    xs = x[:, bass.ds(s * TOKS, TOKS), :].rearrange("p t d -> p (t d)")
                    nc.gpsimd.tensor_tensor(xs, xs, tab["bias_down"][:, :], ALU.add).then_inc(S["x_biased"], 1)
                for down in (True, False):
                    if has(s, -1 if down else 1):
                        r = routing(s, down)
                        pool.wait_ge(S["pow_in"], r + 1)
                        nc.gpsimd.tensor_tensor(ratio[:, :], tab["euler"][:, :], gap[:, :], ALU.pow).then_inc(S["pow_done"], 1)
            turns(pool, turn)

        @block.scalar
        def _(act):
            def copy_logits(s, down):
                act.wait_ge(S["log_mm"], routing(s, down) + 1)
                if not (isinstance(s, int) and s == -1):
                    act.wait_ge(S["logits"], routing(s, down))
                nc.scalar.copy(lgT[:, :], misc[0][:, 0:P]).then_inc(S["free0"], 1)

            def copy_choices(s, down):
                r = routing(s, down)
                act.wait_ge(S["oh_turned"], r + 1)
                turned = misc[0][:, :].bitcast(BF16)[:, 0:2 * P]
                if down:
                    nc.scalar.copy(ohTd[:, :, :], turned.rearrange("e (k n) -> e k n", k=2)).then_inc(S["free0"], 1)
                else:
                    if has(s, 0):
                        act.wait_ge(S["gat_mm"], before(s, 16, 16))
                    for k in range(2):
                        ins = nc.scalar.copy(ohTu[:, :, :, k, :].rearrange("e m h n -> e h m n"),
                                             turned[:, k * P:(k + 1) * P].rearrange("e (h m n) -> e h m n", h=2, m=2))
                    ins.then_inc(S["free0"], 1)
                act.wait_ge(S["spread_mm"], r + 1)
                if down:
                    nc.scalar.copy(probd[:, :, :], misc[1][:, 0:P].rearrange("p (k c) -> p k c", k=2)).then_inc(S["free1"], 1)
                else:
                    if has(s, 0):
                        act.wait_ge(S["z_read"], before(s, 8, 8))
                    nc.scalar.copy(probu[:, :], misc[1][:, 0:HALF]).then_inc(S["free1"], 1)

            def gelu(s, m, u, k):
                if m == 0 and u == 0 and (not isinstance(s, int) or s > 1):
                    act.wait_ge(S["hR_ready"], s - 1)
                act.wait_ge(S["h_mm"], 8 * s + 4 * m + u + 1)
                nc.scalar.activation(hT[k][:, m, 8 * u:8 * u + 8, :], h_ps[u % 2], ACT.Gelu).then_inc(S["h_ready"], 1)

            def copy_turned(s):
                if has(s, -2):
                    act.wait_ge(S["x_done"], s - 1)
                for b in range(2):
                    act.wait_ge(S["turned_x"], 2 * s + 3 + b)
                    nc.scalar.copy(xnT[:, 4 * b:4 * b + 4, :].rearrange("p t n -> p (t n)"), misc[b][:, :])\
                      .then_inc(S[f"free{b}"], 1)

            def for_router(s, k):
                act.wait_ge(S["h_ready"], 8 * s + 8)
                if has(s, -1):
                    act.wait_ge(S["log_mm"], routing(s, True) + 1)
                for h in range(2):
                    for o in range(2):
                        ins = nc.scalar.copy(
                            hR[64 * o:64 * o + 64, :, 64 * h:64 * h + 64],
                            hT[k][64 * h:64 * h + 64, :, :, 32 * o:32 * o + 32].rearrange("p m n o -> p o (m n)"))
                ins.then_inc(S["hR_ready"], 1)

            def turn(s, k):
                up, down, nxt = has(s, 0), has(s, -1), has(s, 1)
                if down:
                    copy_logits(s, True)
                if up:
                    for u in range(4):
                        gelu(s, 0, u, k)
                if down:
                    copy_choices(s, True)
                if up:
                    for u in range(4):
                        gelu(s, 1, u, k)
                if nxt:
                    copy_turned(s)
                    copy_logits(s, False)
                if up:
                    for_router(s, k)
                if nxt:
                    copy_choices(s, False)
            turns(act, turn)


WR = 8
WCH = RUN // WR
WKEYS = 6
WSCALE = D ** -0.5


def window(nc, keep, a, name):
    x, ident = keep["x"], keep["ident"]
    with Stage(nc, name) as st:
        wqkv, wo = st.sb("wqkv", [P, 3, D]), st.sb("wo", [P, D])
        bias, biases = st.sb("bias", [P, D]), [st.sb(f"bias{k}", [P, D]) for k in range(3)]
        inner = [st.sb(n, [P, 1]) for n in ("has_before", "has_after")]
        count = [st.sb(n, [P, 1]) for n in ("count_first", "count_last")]
        xn = st.sb("xn", [P, WR, D])
        xnT = st.sb("xnT", [P, WR, P])
        haloT = st.sb("haloT", [P, 4, P + 2])
        q = [st.sb(f"q{k}", [P, WR + 2, D]) for k in range(2)]
        kk = [st.sb(f"k{k}", [P, WR + 4, D]) for k in range(2)]
        vv = [st.sb(f"v{k}", [P, WR + 4, D]) for k in range(2)]
        k_end, v_end = st.sb("k_end", [P, 2, D]), st.sb("v_end", [P, 2, D])
        prod = [st.sb(f"prod{o}", [P, WR, D]) for o in range(WKEYS)]
        sc = st.sb("sc", [P, WKEYS, WR * HEADS])
        pair_max, win_max = st.sb("pair_max", [P, 3, WR * HEADS]), st.sb("win_max", [P, 2, WR * HEADS])
        pr = st.sb("pr", [P, 2, 4, WR * HEADS])
        half_sum = st.sb("half_sum", [P, 2, 2, WR * HEADS])
        den = st.sb("den", [P, 2, WR * HEADS])
        weighed = [st.sb(f"weighed{j}", [P, WR, D]) for j in range(3)]
        oT = st.sb("oT", [P, WR, P])
        bank = [st.ps(f"bank{j}", [P, 4, D]) for j in range(4)]
        oT_ps = [st.ps(f"oT{b}", [P, 4, P]) for b in range(2)]
        out_ps = st.ps("out", [P, WR, D])
        names = ("loaded", "zeroed", "masks", "xn_ready", "filled", "moved", "carried", "prod_ready", "reduced", "link",
                 "dif_ready", "exp_done", "masked", "weighed", "accumulated", "oT_moved", "projected", "biased", "bias_made",
                 "added")
        S = {n: st.sem(n) for n in names}
        block = st.block()

        def turns(eng, one):
            one(-1, 1)
            one(0, 0)
            one(1, 1)
            with eng.Fori(0, WCH // 2 - 2) as i:
                one(i * 2 + 2, 0)
                one(i * 2 + 3, 1)
            one(WCH - 2, 0)
            one(WCH - 1, 1)
            one(WCH, 0)

        def first(c):
            return isinstance(c, int) and c == 0

        def last(c):
            return isinstance(c, int) and c == WCH

        def rows(c):
            return (2, WR) if first(c) else (0, 2) if last(c) else (0, WR)

        def fill(c, j):
            return 3 + 8 * c + j

        def link_value(c, n):
            return 8 * c + n

        @block.sync
        def _(sp):
            sp.dma_start(wqkv[:, :, :].rearrange("p a d -> p (a d)"), a["L1_attn_w_qkv"]).then_inc(S["loaded"], 16)
            sp.dma_start(wo[:, :], a["L1_attn_w_out"]).then_inc(S["loaded"], 16)
            sp.dma_start(bias[:, :], a["L1_attn_b_out"].partition_broadcast(P)).then_inc(S["loaded"], 16)

        @block.tensor
        def _(pe):
            def take(c, j, n=None):
                n = fill(c, j) if n is None else n
                if not isinstance(n, int) or n >= 4:
                    pe.wait_ge(S["moved"], n - 3)
                return bank[(3 + j) % 4 if n is None or not isinstance(n, int) else n % 4]

            def halo():
                pe.wait_ge(S["xn_ready"], 1)
                for t in range(4):
                    mm = nc.tensor.transpose(bank[0][:, t, :], xn[:, t, :], ident[:, :])
                mm.then_inc(S["filled"], 1)
                pe.wait_ge(S["loaded"], 48)
                pe.wait_ge(S["zeroed"], 2)
                pe.wait_ge(S["moved"], 1)
                for w in (1, 2):
                    for t in range(4):
                        at = 0 if t < 2 else 2
                        mm = nc.tensor.matmul(bank[w][:, t, :], haloT[:, t, at:at + P], wqkv[:, w, :], start=True, stop=True)
                    mm.then_inc(S["filled"], 1)

            def turn_chunk(c):
                pe.wait_ge(S["xn_ready"], c + 2)
                for b in range(2):
                    into = take(c, b)
                    for t in range(4):
                        mm = nc.tensor.transpose(into[:, t, :], xn[:, 4 * b + t, :], ident[:, :])
                    mm.then_inc(S["filled"], 1)

            def project(c):
                pe.wait_ge(S["moved"], fill(c, 1) + 1)
                for w in range(3):
                    for b in range(2):
                        into = take(c, 2 + 2 * w + b)
                        for t in range(4):
                            mm = nc.tensor.matmul(into[:, t, :], xnT[:, 4 * b + t, :], wqkv[:, w, :], start=True, stop=True)
                        mm.then_inc(S["filled"], 1)

            def accumulate(c):
                t0, t1 = rows(c)
                for o in range(WKEYS):
                    pe.wait_ge(S["weighed"], WKEYS * c + o + 1)
                    if o == 0 and not first(c):
                        pe.wait_ge(S["oT_moved"], 2 * c)
                    for t in range(t0, t1):
                        mm = nc.tensor.matmul(oT_ps[t // 4][:, t % 4, :], weighed[o % 3][:, t, :], ident[:, :],
                                              start=(o == 0 and t in (t0, 4)),
                                              stop=(o == WKEYS - 1 and t in (3, t1 - 1)))
                    mm.then_inc(S["accumulated"], 1)

            def output(c):
                t0, t1 = rows(c)
                pe.wait_ge(S["oT_moved"], 2 * c + 2)
                if not first(c):
                    pe.wait_ge(S["added"], c)
                for t in range(t0, t1):
                    mm = nc.tensor.matmul(out_ps[:, t, :], oT[:, t, :], wo[:, :], start=True, stop=True)
                mm.then_inc(S["projected"], 1)

            def turn(c, k):
                if isinstance(c, int) and c == -1:
                    halo()
                if not isinstance(c, int) or c + 1 < WCH:
                    turn_chunk(c + 1)
                    project(c + 1)
                if not isinstance(c, int) or c >= 0:
                    accumulate(c)
                    output(c)
            turns(pe, turn)

        @block.scalar
        def _(act):
            def move(c, j, out, src=None, n=None):
                n = fill(c, j) if n is None else n
                act.wait_ge(S["filled"], n + 1)
                nc.scalar.copy(out, bank[(3 + j) % 4][:, :, :] if src is None else src).then_inc(S["moved"], 1)

            def halo():
                act.wait_ge(S["zeroed"], 1)
                move(0, 0, haloT[:, :, 1:P + 1], bank[0][:, :, :], 0)
                for n, (ring, end) in enumerate(((kk, k_end), (vv, v_end))):
                    act.wait_ge(S["filled"], n + 2)
                    nc.scalar.copy(ring[0][:, 2:4, :], bank[1 + n][:, 0:2, :])
                    nc.scalar.copy(end[:, :, :], bank[1 + n][:, 2:4, :]).then_inc(S["moved"], 1)

            def carry(c, k):
                if not (isinstance(c, int) and c == 0):
                    act.wait_ge(S["moved"], fill(c - 1, 7) + 1)
                    if not (isinstance(c, int) and c == 1):
                        act.wait_ge(S["prod_ready"], WKEYS * c - WKEYS)
                        act.wait_ge(S["weighed"], WKEYS * c - WKEYS)
                    nc.scalar.copy(q[k][:, 0:2, :], q[1 - k][:, WR:WR + 2, :])
                    nc.scalar.copy(kk[k][:, 0:4, :], kk[1 - k][:, WR:WR + 4, :])
                    nc.scalar.copy(vv[k][:, 0:4, :], vv[1 - k][:, WR:WR + 4, :]).then_inc(S["carried"], 1)

            def move_chunk(c, k):
                for b in range(2):
                    move(c, b, xnT[:, 4 * b:4 * b + 4, :])
                for w, (dst, at) in enumerate(((q, 2), (kk, 4), (vv, 4))):
                    for b in range(2):
                        move(c, 2 + 2 * w + b, dst[k][:, at + 4 * b:at + 4 * b + 4, :])

            def attend(c):
                t0, t1 = rows(c)
                lanes = slice(t0 * HEADS, t1 * HEADS)
                for w in range(2):
                    act.wait_ge(S["dif_ready"], 2 * c + w + 1)
                    nc.scalar.activation(pr[:, w, :, lanes], pr[:, w, :, lanes], ACT.Exp, scale=WSCALE).then_inc(S["exp_done"], 1)
                act.wait_ge(S["accumulated"], WKEYS * c + WKEYS)
                if not first(c):
                    act.wait_ge(S["projected"], c)
                for b in range(2):
                    s0, s1 = max(t0, 4 * b), min(t1, 4 * b + 4)
                    if s1 > s0:
                        nc.scalar.copy(oT[:, s0:s1, :], oT_ps[b][:, s0 - 4 * b:s1 - 4 * b, :]).then_inc(S["oT_moved"], 1)
                    else:
                        act.sem_inc(S["oT_moved"], 1)

            def turn(c, k):
                if isinstance(c, int) and c == -1:
                    halo()
                if not last(c):
                    carry(c + 1, 1 - k)
                if not isinstance(c, int) or c + 1 < WCH:
                    move_chunk(c + 1, 1 - k)
                elif c + 1 == WCH:
                    nc.scalar.copy(kk[1 - k][:, 4:6, :], k_end[:, :, :])
                    nc.scalar.copy(vv[1 - k][:, 4:6, :], v_end[:, :, :]).then_inc(S["moved"], 1)
                if not isinstance(c, int) or c >= 0:
                    attend(c)
            turns(act, turn)

        @block.gpsimd
        def _(pool):
            nc.gpsimd.memset(haloT[:, :, 0:1], 0.0).then_inc(S["zeroed"], 1)
            nc.gpsimd.memset(haloT[:, :, P + 1:P + 2], 0.0).then_inc(S["zeroed"], 1)

            def add_bias(c):
                pool.wait_ge(S["xn_ready"], c + 1 if last(c) else c + 2)
                t0, t1 = rows(c)
                parts = [(2, 4, 1), (4, WR, 0)] if first(c) else [(0, 2, 2)] if last(c) else [(t0, t1, 0)]
                for s0, s1, n in parts:
                    xs = x[:, bass.ds(c * WR - 2 + s0, s1 - s0), :]
                    ins = nc.gpsimd.tensor_tensor(xs, xs, biases[n][:, :].unsqueeze(1).broadcast_to([P, s1 - s0, D]), ALU.add)
                ins.then_inc(S["biased"], 1)

            def turn(c, k):
                if isinstance(c, int) and c == -1:
                    return
                t0, t1 = rows(c)
                pairs = (t1 - t0) // 2
                if last(c):
                    pool.wait_ge(S["moved"], fill(c, 0) + 1)
                else:
                    pool.wait_ge(S["moved"], fill(c, 5) + 1)
                if not first(c):
                    pool.wait_ge(S["carried"], c)
                for o in range(WKEYS):
                    if not first(c):
                        pool.wait_ge(S["reduced"], WKEYS * c - WKEYS + o + 1)
                    keys = kk[k][:, t0 + o:t0 + o + 2 * pairs - 1:2, :].unsqueeze(2).broadcast_to([P, pairs, 2, D])
                    nc.gpsimd.tensor_tensor(prod[o][:, t0:t1, :].rearrange("p (m i) d -> p m i d", i=2),
                                            q[k][:, t0:t1, :].rearrange("p (m i) d -> p m i d", i=2), keys, ALU.mult)\
                      .then_inc(S["prod_ready"], 1)
                if first(c):
                    pool.wait_ge(S["bias_made"], 3)
                add_bias(c)
            turns(pool, turn)

        @block.vector
        def _(dve):
            def edges():
                for n, at in enumerate((0, 7)):
                    nc.vector.tensor_reduce(inner[n][:, :], ident[:, at:P:8], AX.X, ALU.add).then_inc(S["masks"], 1)
                    dve.wait_ge(S["masks"], 3 * n + 1)
                    nc.vector.tensor_scalar(count[n][:, :], inner[n][:, :], -1.0, 2.0, ALU.mult, ALU.add).then_inc(S["masks"], 1)
                    nc.vector.tensor_scalar(inner[n][:, :], inner[n][:, :], -1.0, 1.0, ALU.mult, ALU.add).then_inc(S["masks"], 1)
                    dve.wait_ge(S["masks"], 3 * n + 3)

            def norm(c):
                if not (isinstance(c, int) and c == 0):
                    dve.wait_ge(S["filled"], fill(c - 1, 1) + 1)
                else:
                    dve.wait_ge(S["filled"], 1)
                for t in range(WR):
                    ins = normalize(nc, keep, xn[:, t, :], c * WR + t)
                ins.then_inc(S["xn_ready"], 1)

            def scores(c):
                t0, t1 = rows(c)
                for o in range(WKEYS):
                    dve.wait_ge(S["prod_ready"], WKEYS * c + o + 1)
                    nc.vector.tensor_reduce(sc[:, o, t0 * HEADS:t1 * HEADS],
                                            prod[o][:, t0:t1, :].rearrange("p t (h e) -> p (t h) e", e=HD), AX.X, ALU.add)\
                      .then_inc(S["reduced"], 1)

            def probabilities(c, between):
                t0, t1 = rows(c)
                at, n = slice(t0 * HEADS, t1 * HEADS), (t1 - t0) * HEADS

                def link(v, ins):
                    ins.then_inc(S["link"], 1)
                    dve.wait_ge(S["link"], link_value(c, v))
                dve.wait_ge(S["reduced"], WKEYS * c + WKEYS)
                link(1, nc.vector.tensor_tensor(pair_max[:, :, at], sc[:, 0:WKEYS:2, at], sc[:, 1:WKEYS:2, at], ALU.max))
                link(2, nc.vector.tensor_tensor(win_max[:, :, at], pair_max[:, 0:2, at], pair_max[:, 1:3, at], ALU.max))
                for w in range(2):
                    nc.vector.tensor_tensor(pr[:, w, :, at], sc[:, 2 * w:2 * w + 4, at],
                                            win_max[:, w, at].unsqueeze(1).broadcast_to([P, 4, n]), ALU.subtract)\
                      .then_inc(S["dif_ready"], 1)
                between()
                dve.wait_ge(S["exp_done"], 2 * c + 2)
                link(3, nc.vector.tensor_tensor(half_sum[:, :, :, at], pr[:, :, 0:2, at], pr[:, :, 2:4, at], ALU.add))
                link(4, nc.vector.tensor_tensor(den[:, :, at], half_sum[:, :, 0, at], half_sum[:, :, 1, at], ALU.add))
                link(5, nc.vector.reciprocal(den[:, :, at], den[:, :, at]))
                if first(c) or last(c):
                    w, edge = (0, slice(2 * HEADS, 4 * HEADS)) if first(c) else (1, slice(0, 2 * HEADS))
                    nc.vector.tensor_scalar(den[:, w, edge], den[:, w, edge], inner[w][:, 0:1], None, ALU.mult)\
                      .then_inc(S["masked"], 1)
                    dve.wait_ge(S["masked"], w + 1)
                for w in range(2):
                    link(6 + w, nc.vector.tensor_tensor(pr[:, w, :, at], pr[:, w, :, at],
                                                        den[:, w, at].unsqueeze(1).broadcast_to([P, 4, n]), ALU.mult))
                link(8, nc.vector.tensor_tensor(pr[:, 0, 2:4, at], pr[:, 0, 2:4, at], pr[:, 1, 0:2, at], ALU.add))

            def stats(c):
                for t in range(*rows(c)):
                    token_stats(nc, keep, c * WR - 2 + t)

            def weigh(c, k):
                t0, t1 = rows(c)
                pairs = (t1 - t0) // 2
                if not last(c):
                    dve.wait_ge(S["moved"], fill(c, 7) + 1)
                for o in range(WKEYS):
                    if o >= 3 or not first(c):
                        dve.wait_ge(S["accumulated"], WKEYS * c + o - 2)
                    w, m = (0, o) if o < 4 else (1, o - 2)
                    for i in range(2):
                        values = vv[k][:, t0 + o:t0 + o + 2 * pairs - 1:2, :].rearrange("p m (h e) -> p m h e", e=HD)
                        weights = pr[:, w, m, :].rearrange("p (t h) -> p t h", h=HEADS)[:, t0 + i:t1 + i - 1:2, :]\
                            .unsqueeze(3).broadcast_to([P, pairs, HEADS, HD])
                        ins = nc.vector.tensor_tensor(weighed[o % 3][:, t0 + i:t1 + i - 1:2, :]
                                                      .rearrange("p m (h e) -> p m h e", e=HD), values, weights, ALU.mult)
                    ins.then_inc(S["weighed"], 1)

            def add(c):
                t0, t1 = rows(c)
                dve.wait_ge(S["biased"], c + 1)
                dve.wait_ge(S["projected"], c + 1)
                xs = x[:, bass.ds(c * WR - 2 + t0, t1 - t0), :]
                nc.vector.tensor_tensor(xs, xs, out_ps[:, t0:t1, :], ALU.add).then_inc(S["added"], 1)

            edges()
            for t, r in enumerate((RUN - 2, RUN - 1, 0, 1)):
                ins = normalize(nc, keep, xn[:, t, :], r)
            ins.then_inc(S["xn_ready"], 1)
            dve.wait_ge(S["loaded"], 48)
            for n, times in enumerate((2.0, count[0][:, 0:1], count[1][:, 0:1])):
                nc.vector.tensor_scalar(biases[n][:, :], bias[:, :], times, None, ALU.mult).then_inc(S["bias_made"], 1)

            def turn(c, k):
                if not isinstance(c, int) or c + 1 < WCH:
                    norm(c + 1)
                if not isinstance(c, int) or c >= 0:
                    scores(c)

                    def between():
                        if not first(c):
                            add(c - 1)
                    probabilities(c, between)
                    if not first(c):
                        dve.wait_ge(S["added"], c)
                    weigh(c, k)
                    if not first(c):
                        stats(c - 1)
            turns(dve, turn)
            add(WCH)
            dve.wait_ge(S["added"], WCH + 1)
            stats(WCH)


def store(nc, keep, out):
    with Stage(nc, "store") as st:
        stored = st.sem("stored")
        block = st.block()

        @block.sync
        def _(sp):
            sp.dma_start(out.rearrange("b (g r) d -> (b g) r d", r=RUN), keep["x"][:, :, :]).then_inc(stored, 16)
            sp.wait_ge(stored, 16)


def macaron(nc, a, out, stages=range(6)):
    def allocate(ctx, shapes):
        return {n: ctx.enter_context(nc.sbuf_tensor(n, shape, dt)) for n, (shape, dt) in shapes.items()}

    Stage.used = []
    with ExitStack() as ctx:
        keep = allocate(ctx, {
            "x": ([P, RUN, D], F32), "ident": ([P, P], F32), "identb": ([P, P], BF16),
            "half_neg": ([P, RUN], F32), "mean": ([P, RUN], F32), "rstd": ([P, RUN], F32),
            "stats": ([P, RUN, 6], F32)})
        keep.update(allocate(ctx, {"gateT": ([P, HB, P], F32), "upT": ([P, HB, P], F32), "downT": ([P, HB, D], F32)}))
        setup(nc, keep, a)
        if 0 in stages:
            layer_norm_stats(nc, keep, "ln0", False)
            ffn(nc, keep, "ffn0")
        if 1 in stages:
            layer_norm_stats(nc, keep, "ln1", 0 in stages)
            mla(nc, keep, a, "mla")
        tab = allocate(ctx, {
            **{w: ([P, TAB], BF16) for w in MOE_TABLES}, **{w + "3": ([P, TAB], BF16) for w in MOE_TABLES},
            "router_upT": ([P, TOKS, E], F32), "router_downT": ([P, UI, E], F32), "bias_up": ([P, 2, UO], BF16),
            "both": ([P, P], BF16), "bias_down": ([P, TOKS * D], F32), "scale_up": ([P, 1], F32),
            "scale_down": ([P, 1], F32), "euler": ([P, 1], F32)})
        layer_norm_stats(nc, keep, "ln2", 1 in stages)
        ffn(nc, keep, "ffn1", a, tab)
        tab.update(pick_half=keep["upT"][:, 0, :], pick0=keep["upT"][:, 1, :], pick1=keep["upT"][:, 2, :],
                   expert_no=keep["downT"][:, 0, :].rearrange("p (a e) -> p a e", a=2), spread=keep["downT"][:, 1, 0:HALF])
        if 3 in stages or 5 in stages:
            moe_tables(nc, keep, a, tab, "tables")
        if 3 in stages:
            layer_norm_stats(nc, keep, "ln3", 2 in stages)
            moe(nc, keep, tab, "moe0", True)
        if 4 in stages:
            layer_norm_stats(nc, keep, "ln4", 3 in stages)
            window(nc, keep, a, "window")
        if 5 in stages:
            layer_norm_stats(nc, keep, "ln5", 4 in stages)
            moe(nc, keep, tab, "moe1", False)
        store(nc, keep, out)


_INS = ['L0_attn_x', 'L0_attn_Wq', 'L0_attn_bq', 'L0_attn_Wkd', 'L0_attn_bkd', 'L0_attn_Wku', 'L0_attn_bku',
        'L0_attn_Wo', 'L0_attn_bo', 'L0_ffn_w_gate', 'L0_ffn_w_up', 'L0_ffn_w_down', 'L1_attn_w_qkv',
        'L1_attn_w_out', 'L1_attn_b_out', 'L1_ffn_W_up', 'L1_ffn_A_up', 'L1_ffn_B_up', 'L1_ffn_scale_up',
        'L1_ffn_bias_up', 'L1_ffn_W_down', 'L1_ffn_A_down', 'L1_ffn_B_down', 'L1_ffn_scale_down',
        'L1_ffn_bias_down']


def kernel(**inputs):
    import concourse.bacc as bacc
    from concourse.bass_utils import run_bass_kernel_spmd

    nc = bacc.Bacc("TRN2", target_bir_lowering=False, num_devices=1)
    arrays, args = {}, {}
    for name in _INS:
        v = np.ascontiguousarray(inputs[name])
        arrays[f"in_{name}"] = v
        args[name] = nc.dram_tensor(f"in_{name}", v.shape, mybir.dt.from_np(v.dtype), kind="ExternalInput").ap()
    out = nc.dram_tensor("out_x", (BATCH, SEQ, D), F32, kind="ExternalOutput").ap()
    macaron(nc, args, out)
    r = run_bass_kernel_spmd(nc, [arrays], core_ids=[0])
    return r.results[0]["out_x"]
```
